# Optimizing a Trainium2 kernel written in Bass

```python
import numpy as np
import jax
import jax.numpy as jnp

def _softmax(x, axis=-1):
    return jax.nn.softmax(x, axis=axis)

def _gelu(x):
    return jax.nn.gelu(x, approximate=True)

def _silu(x):
    return jax.nn.silu(x)

def _sigmoid(x):
    return jax.nn.sigmoid(x)

def _layernorm(x, axis=-1, eps=1e-05):
    m = jnp.mean(x, axis=axis, keepdims=True)
    v = jnp.var(x, axis=axis, keepdims=True)
    return (x - m) / jnp.sqrt(v + eps)

def _scatter_add(tgt, idx, src, axis=0):
    return tgt.at[idx].add(src)

def _segment_sum(src, seg, n):
    return jax.ops.segment_sum(src, seg, n)
kernel_name = 'mk_gps_d1_gnn_r8_b3ac43'

def setup_inputs(seed: int=0):
    np.random.seed(seed)
    _w = jnp.asarray

    def _rec_inputs():
        import jax
        import jax.numpy as jnp
        _gk = jax.random.key(seed)
        x = -0.0003713 + 1 * jax.random.normal(jax.random.fold_in(_gk, 1), (6250, 256), jnp.float32)
        src = jax.random.randint(jax.random.fold_in(_gk, 2), (100000,), 0, 6250, jnp.int32)
        dst = jnp.minimum((6250 * jax.random.uniform(jax.random.fold_in(_gk, 3), (100000,)) ** 2.0).astype(jnp.int32), 49999)
        _o = jnp.argsort(dst, stable=True)
        src = src[_o]
        dst = dst[_o]
        edge_weight = jax.random.uniform(jax.random.fold_in(_gk, 12), (100000,), jnp.float32, 0.0, 0.999998)
        return (x, src, dst, edge_weight)
    x, src, dst, edge_weight = _rec_inputs()

    def _L0_gnn_setup():
        import jax, jax.numpy as jnp
        import numpy as np
        N_NODES = 6250
        N_EDGES = 100000
        H, D_IN, D_OUT = (4, 256, 64)
        key = jax.random.key(seed)
        ks = jax.random.split(key, 7)
        x = jax.random.normal(ks[0], (N_NODES, D_IN), dtype=jnp.float32)
        idx = jax.random.randint(ks[1], (2, N_EDGES), 0, N_NODES, dtype=jnp.int32)
        elem = jax.random.uniform(ks[2], (N_EDGES,), dtype=jnp.float32)
        Ws = jax.random.normal(ks[3], (H, D_IN, D_OUT), dtype=jnp.float32) * 0.05
        bs = jax.random.normal(ks[4], (H, D_OUT), dtype=jnp.float32) * 0.05
        aw = jax.random.normal(ks[5], (H, 2 * D_OUT + 1), dtype=jnp.float32) * 0.05
        ab = jax.random.normal(ks[6], (H,), dtype=jnp.float32) * 0.05
        return {'x': x, 'idx': idx, 'elem': elem, 'Ws': Ws, 'bs': bs, 'aw': aw, 'ab': ab}
    _L0_gnn_all = _L0_gnn_setup()
    _L0_gnn_in = {k: v for k, v in _L0_gnn_all.items() if k in ('Ws', 'bs', 'aw', 'ab')}
    del _L0_gnn_all

    def _L0_mix_setup():
        import jax, jax.numpy as jnp
        import numpy as np
        B, N, C = (8, 1024, 256)
        H, D, S = (8, 32, 32)
        HID = 4 * C

        def layernorm(x, w, b, eps=1e-05):
            mu = jnp.mean(x, axis=-1, keepdims=True)
            var = jnp.mean(jnp.square(x - mu), axis=-1, keepdims=True)
            return (x - mu) * jax.lax.rsqrt(var + eps) * w + b

        def linear_no_attn(x, Wx, bx, Wq, Wk, Wv, Wo, bo):
            x_mid = x @ Wx.T + bx
            x_mid = x_mid.reshape(x.shape[0], x.shape[1], H, D).transpose(0, 2, 1, 3)
            q = jax.nn.softmax(x_mid @ Wq.T, axis=-1)
            k = jax.nn.softmax(x_mid @ Wk.T, axis=-2)
            v = x_mid @ Wv.T
            kv = jnp.einsum('bhns,bhnd->bhsd', k, v)
            qkv = jnp.einsum('bhns,bhsd->bhnd', q, kv)
            qkv = qkv.transpose(0, 2, 1, 3).reshape(x.shape[0], x.shape[1], H * D)
            return qkv @ Wo.T + bo
        key = jax.random.key(seed)
        ks = jax.random.split(key, 16)
        s = lambda fan: 1.0 / np.sqrt(fan)
        return {'fx': jax.random.normal(ks[0], (B, N, C), jnp.float32), 'ln1_w': jnp.ones((C,), jnp.float32), 'ln1_b': jnp.zeros((C,), jnp.float32), 'Wx': jax.random.uniform(ks[1], (C, C), jnp.float32, -s(C), s(C)), 'bx': jax.random.uniform(ks[2], (C,), jnp.float32, -s(C), s(C)), 'Wq': jax.random.uniform(ks[3], (S, D), jnp.float32, -s(D), s(D)), 'Wk': jax.random.uniform(ks[4], (S, D), jnp.float32, -s(D), s(D)), 'Wv': jax.random.uniform(ks[5], (D, D), jnp.float32, -s(D), s(D)), 'Wo': jax.random.uniform(ks[6], (C, C), jnp.float32, -s(C), s(C)), 'bo': jax.random.uniform(ks[7], (C,), jnp.float32, -s(C), s(C)), 'ln2_w': jnp.ones((C,), jnp.float32), 'ln2_b': jnp.zeros((C,), jnp.float32), 'W1': jax.random.uniform(ks[8], (HID, C), jnp.float32, -s(C), s(C)), 'b1': jax.random.uniform(ks[9], (HID,), jnp.float32, -s(C), s(C)), 'W2': jax.random.uniform(ks[10], (C, HID), jnp.float32, -s(HID), s(HID)), 'b2': jax.random.uniform(ks[11], (C,), jnp.float32, -s(HID), s(HID))}
    _L0_mix_all = _L0_mix_setup()
    _L0_mix_in = {k: v for k, v in _L0_mix_all.items() if k in ('ln1_w', 'ln1_b', 'Wx', 'bx', 'Wq', 'Wk', 'Wv', 'Wo', 'bo', 'ln2_w', 'ln2_b', 'W1', 'b1', 'W2', 'b2')}
    del _L0_mix_all

    def _L0_ffn_setup():
        import jax, jax.numpy as jnp
        import numpy as np
        B, S, D, E, H, K = (4, 512, 256, 8, 512, 2)
        key = jax.random.key(seed)
        ks = jax.random.split(key, 6)
        x = jax.random.normal(ks[0], (B, S, D), jnp.float32)
        Wg = jax.random.normal(ks[1], (D, E), jnp.float32) * 0.02
        bg = jnp.zeros((E,), jnp.float32)
        W1 = jax.random.normal(ks[2], (E, D, H), jnp.float32) * 0.02
        b1 = jnp.zeros((E, H), jnp.float32)
        W2 = jax.random.normal(ks[3], (E, H, D), jnp.float32) * 0.02
        b2 = jnp.zeros((E, D), jnp.float32)
        return {'x': x, 'Wg': Wg, 'bg': bg, 'W1': W1, 'b1': b1, 'W2': W2, 'b2': b2}
    _L0_ffn_all = _L0_ffn_setup()
    _L0_ffn_in = {k: v for k, v in _L0_ffn_all.items() if k in ('Wg', 'bg', 'W1', 'b1', 'W2', 'b2')}
    del _L0_ffn_all
    return {'x': x, 'src': src, 'dst': dst, 'edge_weight': edge_weight, 'L0_gnn_Ws': _L0_gnn_in['Ws'], 'L0_gnn_bs': _L0_gnn_in['bs'], 'L0_gnn_aw': _L0_gnn_in['aw'], 'L0_gnn_ab': _L0_gnn_in['ab'], 'L0_mix_ln1_w': _L0_mix_in['ln1_w'], 'L0_mix_ln1_b': _L0_mix_in['ln1_b'], 'L0_mix_Wx': _L0_mix_in['Wx'], 'L0_mix_bx': _L0_mix_in['bx'], 'L0_mix_Wq': _L0_mix_in['Wq'], 'L0_mix_Wk': _L0_mix_in['Wk'], 'L0_mix_Wv': _L0_mix_in['Wv'], 'L0_mix_Wo': _L0_mix_in['Wo'], 'L0_mix_bo': _L0_mix_in['bo'], 'L0_mix_ln2_w': _L0_mix_in['ln2_w'], 'L0_mix_ln2_b': _L0_mix_in['ln2_b'], 'L0_mix_W1': _L0_mix_in['W1'], 'L0_mix_b1': _L0_mix_in['b1'], 'L0_mix_W2': _L0_mix_in['W2'], 'L0_mix_b2': _L0_mix_in['b2'], 'L0_ffn_Wg': _L0_ffn_in['Wg'], 'L0_ffn_bg': _L0_ffn_in['bg'], 'L0_ffn_W1': _L0_ffn_in['W1'], 'L0_ffn_b1': _L0_ffn_in['b1'], 'L0_ffn_W2': _L0_ffn_in['W2'], 'L0_ffn_b2': _L0_ffn_in['b2']}

def reference(x, src, dst, edge_weight, L0_gnn_Ws, L0_gnn_bs, L0_gnn_aw, L0_gnn_ab, L0_mix_ln1_w, L0_mix_ln1_b, L0_mix_Wx, L0_mix_bx, L0_mix_Wq, L0_mix_Wk, L0_mix_Wv, L0_mix_Wo, L0_mix_bo, L0_mix_ln2_w, L0_mix_ln2_b, L0_mix_W1, L0_mix_b1, L0_mix_W2, L0_mix_b2, L0_ffn_Wg, L0_ffn_bg, L0_ffn_W1, L0_ffn_b1, L0_ffn_W2, L0_ffn_b2):
    import jax
    import jax.numpy as jnp

    def _L0_gnn_ref(x, idx, elem, Ws, bs, aw, ab):
        import jax, jax.numpy as jnp
        import numpy as np
        N_NODES = 6250
        N_EDGES = 100000
        H, D_IN, D_OUT = (4, 256, 64)
        N = x.shape[0]
        O = Ws.shape[-1]
        feats = jnp.einsum('nd,hdo->hno', x, Ws) + bs[:, None, :]
        aw_src, aw_dst, aw_e = (aw[:, :O], aw[:, O:2 * O], aw[:, 2 * O])
        a_s = jnp.einsum('hno,ho->hn', feats, aw_src)
        a_d = jnp.einsum('hno,ho->hn', feats, aw_dst)
        src, dst = (idx[0], idx[1])
        score = a_s[:, src] + a_d[:, dst] + aw_e[:, None] * elem[None, :] + ab[:, None]
        w = jnp.exp(-jax.nn.relu(score / 20.0))
        dst_f = feats[:, dst]
        seg = lambda vals: jax.ops.segment_sum(vals, src, num_segments=N)
        pooled = jax.vmap(lambda wi, fi: seg(wi[:, None] * fi))(w, dst_f)
        row_sum = jax.vmap(lambda wi: seg(wi))(w)
        out = pooled / row_sum[:, :, None]
        return jnp.transpose(out, (1, 0, 2)).reshape(N, H * O)

    def _L0_mix_ref(fx, ln1_w, ln1_b, Wx, bx, Wq, Wk, Wv, Wo, bo, ln2_w, ln2_b, W1, b1, W2, b2):
        import jax, jax.numpy as jnp
        import numpy as np
        B, N, C = (8, 1024, 256)
        H, D, S = (8, 32, 32)
        HID = 4 * C

        def layernorm(x, w, b, eps=1e-05):
            mu = jnp.mean(x, axis=-1, keepdims=True)
            var = jnp.mean(jnp.square(x - mu), axis=-1, keepdims=True)
            return (x - mu) * jax.lax.rsqrt(var + eps) * w + b

        def linear_no_attn(x, Wx, bx, Wq, Wk, Wv, Wo, bo):
            x_mid = x @ Wx.T + bx
            x_mid = x_mid.reshape(x.shape[0], x.shape[1], H, D).transpose(0, 2, 1, 3)
            q = jax.nn.softmax(x_mid @ Wq.T, axis=-1)
            k = jax.nn.softmax(x_mid @ Wk.T, axis=-2)
            v = x_mid @ Wv.T
            kv = jnp.einsum('bhns,bhnd->bhsd', k, v)
            qkv = jnp.einsum('bhns,bhsd->bhnd', q, kv)
            qkv = qkv.transpose(0, 2, 1, 3).reshape(x.shape[0], x.shape[1], H * D)
            return qkv @ Wo.T + bo
        h = linear_no_attn(layernorm(fx, ln1_w, ln1_b), Wx, bx, Wq, Wk, Wv, Wo, bo) + fx
        y = layernorm(h, ln2_w, ln2_b)
        y = jax.nn.gelu(y @ W1.T + b1, approximate=False)
        y = y @ W2.T + b2
        return y + h

    def _L0_ffn_ref(x, Wg, bg, W1, b1, W2, b2):
        import jax, jax.numpy as jnp
        import numpy as np
        B, S, D, E, H, K = (4, 512, 256, 8, 512, 2)
        Bv, Sv, Dv = x.shape
        gate_scores = x @ Wg + bg
        _, idx = jax.lax.top_k(gate_scores, K)
        mask = jax.nn.one_hot(idx, E, dtype=x.dtype).sum(axis=-2)
        xf = x.reshape(-1, Dv)
        mf = mask.reshape(-1, E)
        h = jax.nn.gelu(jnp.einsum('td,edh->teh', xf, W1) + b1[None], approximate=False)
        y = jnp.einsum('teh,ehd->ted', h, W2) + b2[None]
        out = jnp.einsum('ted,te->td', y, mf)
        return out.reshape(Bv, Sv, Dv)
    edge_index = jnp.stack([src, dst])
    xn = _layernorm(x, axis=-1)
    x = x + _L0_gnn_ref(xn, edge_index, edge_weight, L0_gnn_Ws, L0_gnn_bs, L0_gnn_aw, L0_gnn_ab) + _L0_mix_ref(xn[None], L0_mix_ln1_w, L0_mix_ln1_b, L0_mix_Wx, L0_mix_bx, L0_mix_Wq, L0_mix_Wk, L0_mix_Wv, L0_mix_Wo, L0_mix_bo, L0_mix_ln2_w, L0_mix_ln2_b, L0_mix_W1, L0_mix_b1, L0_mix_W2, L0_mix_b2)[0]
    x = x + _L0_ffn_ref(_layernorm(x, axis=-1)[None], L0_ffn_Wg, L0_ffn_bg, L0_ffn_W1, L0_ffn_b1, L0_ffn_W2, L0_ffn_b2)[0]
    return x

_drawn_inputs = setup_inputs


def setup_inputs(seed=0):
    import zlib

    import numpy as np

    out = dict(_drawn_inputs(seed))
    spreads = {'L0_mix_ln1_w': (1.0, 0.6),
     'L0_mix_ln1_b': (0.0, 0.512),
     'L0_mix_ln2_w': (1.0, 0.6),
     'L0_mix_ln2_b': (0.0, 2.0),
     'L0_ffn_bg': (0.0, 0.8),
     'L0_ffn_b1': (0.0, 2.0),
     'L0_ffn_b2': (0.0, 2.0)}
    factors = {'edge_weight': 64.0,
     'L0_gnn_aw': 64.0,
     'L0_gnn_ab': 200.0,
     'L0_mix_Wx': 4.195,
     'L0_mix_bx': 6.795,
     'L0_mix_Wq': 8.0,
     'L0_mix_Wk': 8.0,
     'L0_mix_Wv': 3.392,
     'L0_mix_Wo': 3.547,
     'L0_mix_b1': 51.744,
     'L0_mix_b2': 35.648,
     'L0_gnn_Ws': 8.0,
     'L0_gnn_bs': 8.0,
     'L0_mix_bo': 8.0,
     'L0_mix_W1': 6.936,
     'L0_mix_W2': 5.916,
     'L0_ffn_Wg': 7.88,
     'L0_ffn_W1': 8.0,
     'L0_ffn_W2': 8.0}
    for name, (base, spread) in spreads.items():
        noise = np.random.default_rng([zlib.crc32(name.encode()), seed]).standard_normal(out[name].shape)
        drawn = base * np.exp(spread * noise) if base else spread * noise
        out[name] = jnp.asarray(drawn.astype(out[name].dtype))
    for name, factor in factors.items():
        out[name] = (out[name] * factor).astype(out[name].dtype)
    return out
```

```python
from contextlib import ExitStack

import concourse.bass as bass
from concourse import mybir

F32 = mybir.dt.float32
I32 = mybir.dt.int32
BF16 = mybir.dt.bfloat16
ALU = mybir.AluOpType
ACT = mybir.ActivationFunctionType
AX = mybir.AxisListType.X
ds = bass.ds

P = 128
N = 6250
D = 256
T = -(-N // P)
LAST = N - (T - 1) * P
J = 7
G = T // J
GN = J * P
HALF = GN // 2
KC = D // P

GH, GO = 4, 64
FW = D + GH
FX = FW + GH

MH, MD = 8, 32
HID = 1024
HC = HID // P

NE, EH, TOP = 8, 512, 2
EHC = EH // P

ECOUNT = 100000
EP = 125
EC = ECOUNT // EP
CB = 40
SC = CB // 2
NB = EC // CB
B = 8
CU = 2
UNIT = CU * P
UG = B // CU
CH = -(-(ECOUNT // UNIT + T) // (2 * UG)) * 2 * B
CI = CH // (2 * B)
CPP = CH // B
EPS = 1e-5
NEG = -1e30
assert T == G * J and NB * CB == EC and NB > G


def wait(eng, sem, count):
    eng.wait_ge(sem, count)
    if not isinstance(count, int):
        eng.nop(nofuse=True)


def norm_stats(nc, dve, act_go, act_done, count, src, st, mv, var, sd, r, nb):
    for j in range(J):
        nc.vector.bn_stats(st[:, j, :], src(j))
    dve.drain()
    for j in range(J):
        nc.vector.bn_aggr(mv[:, j, :], st[:, j, :])
    dve.drain()
    nc.vector.tensor_scalar(var[:, :], mv[:, :, 1], EPS, None, ALU.add).then_inc(act_go, 1)
    wait(dve, act_done, count)
    nc.vector.reciprocal(r[:, :], sd[:, :])
    dve.drain()
    return nc.vector.scalar_tensor_tensor(nb[:, :], mv[:, :, 0], -1.0, r[:, :], ALU.mult, ALU.mult)


def constants(nc, ctx, sb, sem):
    k = {}
    k["X"] = sb(ctx, "X", [P, T, D])
    k["scl"] = sb(ctx, "scl", [P, T, 4])
    k["a_src"] = sb(ctx, "a_src", [P, T, 3, GH], BF16)
    k["ident"] = sb(ctx, "ident", [P, P])
    k["ones"] = sb(ctx, "ones", [P, P])
    k["iota"] = sb(ctx, "iota", [P, P])
    k["awe"] = sb(ctx, "awe", [P, GH])
    k["tiles"] = sb(ctx, "tiles", [1, CH // CU + 4 * UG], I32)
    return k


def front(nc, k, d, dram, sb, ps, sem, keep):
    ctx = ExitStack()
    with ctx:
        X, scl, a_src, ident, ones, iota = (k[n] for n in ("X", "scl", "a_src", "ident", "ones", "iota"))
        order = sb(keep, "order", [EP, EC], I32)
        rec = sb(keep, "rec", [EP, EC, 4])
        tile_f = sb(keep, "tile_f", [EP, EC])
        carry = sb(keep, "carry", [EP, T])
        kmax = sb(keep, "kmax", [P, D])
        stage_i = sb(keep, "stage_i", [EP, 2, SC], I32)
        stage_r = sb(keep, "stage_r", [EP, 2, SC, 4])
        k.update(order=order, rec=rec, tile_f=tile_f, carry=carry, kmax=kmax, stage_i=stage_i, stage_r=stage_r)
        k["E"] = E = sb(keep, "E", [EP, T, CB])
        k["S"] = S = sb(keep, "S", [EP, T, CB])
        k["seg"] = seg = sb(keep, "seg", [EP, T, CB], mybir.dt.bfloat16)
        k["pos"] = sb(keep, "pos", [EP, CB])
        k["pos_i"] = sb(keep, "pos_i", [EP, 3, CB], I32)
        k["eq0"] = sb(keep, "eq0", [EP, T])
        src_i = sb(ctx, "src_i", [EP, EC], I32)
        dst_i = sb(ctx, "dst_i", [EP, EC], I32)
        tmp_i = sb(ctx, "tmp_i", [EP, EC], I32)
        elem = sb(ctx, "elem", [EP, EC])
        junk = sb(ctx, "junk", [EP, EC])
        hist = sb(ctx, "hist", [EP, T])
        before = sb(ctx, "before", [P, P])
        nch_i = sb(ctx, "nch_i", [P, T], I32)
        nch = sb(ctx, "nch", [P, T])
        cend = sb(ctx, "cend", [P, T])
        onesT = sb(ctx, "onesT", [P, T])
        cidx_i = sb(ctx, "cidx_i", [CPP, UG], I32)
        cidx = sb(ctx, "cidx", [CPP, UG])
        ccmp = sb(ctx, "ccmp", [CPP, UG, T])
        ctile = sb(ctx, "ctile", [CPP, UG])
        ctile_i = sb(ctx, "ctile_i", [CPP, UG], I32)
        iota_i = sb(ctx, "iota_i", [P, P], I32)
        blank = sb(ctx, "blank", [P, CH, 4])
        padneg = sb(ctx, "padneg", [P, T])
        wx = sb(ctx, "wx", [P, KC, D])
        wst = sb(ctx, "wst", [P, KC, D])
        wfe = sb(ctx, "wfe", [P, KC, FX])
        wqk = sb(ctx, "wqk", [P, KC, 2 * D])
        bdqk = sb(ctx, "bdqk", [P, 2, P])
        bdaw = sb(ctx, "bdaw", [P, KC, 2 * GH])
        bcol = sb(ctx, "bcol", [P, 2, KC])
        bbc = sb(ctx, "bbc", [P, 2, KC, P])
        fbias = sb(ctx, "fbias", [P, FX])
        abias = sb(ctx, "abias", [P, GH])
        qkbias = sb(ctx, "qkbias", [P, 2 * D])
        ln1 = sb(ctx, "ln1", [P, 2, KC])
        st = sb(ctx, "st", [P, J, 6])
        mv = sb(ctx, "mv", [P, J, 2])
        var = sb(ctx, "var", [P, J])
        sd = sb(ctx, "sd", [P, J])
        r = sb(ctx, "r", [P, 2, J])
        nb = sb(ctx, "nb", [P, 2, J])
        tmpj = sb(ctx, "tmpj", [P, J])
        xn = sb(ctx, "xn", [P, J, D])
        z = sb(ctx, "z", [P, J, D])
        xnT = sb(ctx, "xnT", [P, J, D])
        lT = sb(ctx, "lT", [P, J, D])
        fe = sb(ctx, "fe", [P, J, FX])
        qk = sb(ctx, "qk", [P, J, 2 * D])
        gmax = sb(ctx, "gmax", [P, D])
        part = sb(ctx, "part", [P, J, GH], BF16)
        rest = sb(ctx, "rest", [P, J, GH])
        qs = sb(ctx, "qs", [P, 2, J * MH])
        pt = [ps(ctx, f"f_pt{i}", [P, 512]) for i in range(2)]
        pf = [ps(ctx, f"f_pf{i}", [P, 512]) for i in range(2)]
        pq = [ps(ctx, f"f_pq{i}", [P, 512]) for i in range(2)]
        pc = ps(ctx, "f_pc", [P, 512])
        pb = ps(ctx, "f_pb", [P, 512])

        x_in, edges_in, weights_in = sem("x_in"), sem("edges_in"), sem("weights_in")
        consts_made, blocks_made, x_cleared = sem("consts_made"), sem("blocks_made"), sem("x_cleared")
        hist_done, counts_done, bases_done = sem("hist_done"), sem("counts_done"), sem("bases_done")
        sorted_ = k["sorted"] = sem("sorted_")
        scattered = k["scattered"] = [sem("scattered0"), sem("scattered1")]
        staged = k["staged"] = sem("staged")
        blank_made, blank_out = sem("blank_made"), sem("blank_out")
        ctile_made, ctile_out, tiles_in = sem("ctile_made"), sem("ctile_out"), sem("tiles_in")
        bias_made, folded, fold_kept = sem("bias_made"), sem("folded"), sem("fold_kept")
        var_go, sd_done, stats_go, xn_done, z_done = (sem(s) for s in ("var_go", "sd_done", "stats_go", "xn_done", "z_done"))
        turned, turned_kept, fe_prod, fe_kept = (sem(s) for s in ("turned", "turned_kept", "fe_prod", "fe_kept"))
        qk_prod, qk_kept, qsub, qexp, rows_ready = (sem(s) for s in ("qk_prod", "qk_kept", "qsub", "qexp", "rows_ready"))
        rows_out, rows_free = sem("rows_out"), sem("rows_free")
        k["rows_out"] = rows_out

        block = ctx.enter_context(nc.Block())

        @block.sync
        def _(sp):
            for tile, name in ((src_i, "src"), (dst_i, "dst"), (elem, "edge_weight")):
                sp.dma_start(tile[:, :], d[name].rearrange("(p c) -> p c", p=EP)).then_inc(edges_in, 16)
            sp.wait_ge(x_cleared, 1)
            sp.dma_start(X[:, 0:T - 1, :], d["x"][0:(T - 1) * P, :].rearrange("(t p) c -> p t c", p=P)).then_inc(x_in, 16)
            sp.dma_start(X[0:LAST, T - 1, :], d["x"][(T - 1) * P:N, :]).then_inc(x_in, 16)
            sp.wait_ge(ctile_made, 1)
            sp.dma_start(dram["ctile"].rearrange("(p b) -> p b", b=UG), ctile_i[:, :]).then_inc(ctile_out, 16)
            sp.wait_ge(ctile_out, 16)
            sp.dma_start(k["tiles"][0:1, UG:UG + CH // CU], dram["ctile"].unsqueeze(0)).then_inc(tiles_in, 16)
            sp.sem_inc(rows_free, 1)
            with sp.Fori(0, G) as g:
                wait(sp, rows_ready, g + 1)
                sp.dma_start(dram["feat"][ds(g * GN, GN), :].rearrange("(j p) f -> p j f", p=P),
                             fe[:, :, 0:FW]).then_inc(rows_out, 16)
                sp.dma_start(dram["qk"][ds(g * GN, GN), :].rearrange("(j p) f -> p j f", p=P),
                             qk[:, :, :]).then_inc(rows_out, 16)
                wait(sp, rows_out, g * 32 + 32)
                sp.sem_inc(rows_free, 1)
            sp.wait_ge(tiles_in, 16)
            sp.wait_ge(blank_out, 16)

        @block.gpsimd
        def _(pool):
            nc.gpsimd.iota(iota_i[:, :], pattern=[[1, P]], base=0, channel_multiplier=0).then_inc(consts_made, 1)
            nc.gpsimd.iota(cidx_i[:, :], pattern=[[1, UG]], base=0, channel_multiplier=UG).then_inc(consts_made, 1)
            nc.gpsimd.memset(before[:, :], 1.0).then_inc(consts_made, 1)
            nc.gpsimd.memset(ones[:, :], 1.0).then_inc(consts_made, 1)
            nc.gpsimd.memset(ident[:, :], 0.0).then_inc(consts_made, 1)
            nc.gpsimd.memset(padneg[:, :], 0.0).then_inc(consts_made, 1)
            nc.gpsimd.memset(onesT[:, :], 1.0).then_inc(consts_made, 1)
            pool.wait_ge(consts_made, 7)
            nc.gpsimd.affine_select(out=before[:, :], in_=before[:, :], compare_op=ALU.is_gt, fill=0.0,
                                    base=0, pattern=[[1, P]], channel_multiplier=-1).then_inc(consts_made, 1)
            nc.gpsimd.affine_select(out=ident[:, :], in_=ident[:, :], compare_op=ALU.not_equal, fill=1.0,
                                    base=0, pattern=[[-1, P]], channel_multiplier=1).then_inc(consts_made, 1)
            nc.gpsimd.affine_select(out=padneg[:, T - 1:T], in_=padneg[:, T - 1:T], compare_op=ALU.is_gt, fill=NEG,
                                    base=LAST, pattern=[[0, 1]], channel_multiplier=-1).then_inc(consts_made, 1)
            nc.gpsimd.memset(blank[:, :, :], 0.0).then_inc(blank_made, 1)
            pool.wait_ge(blank_made, 1)
            nc.gpsimd.memset(blank[:, :, 1], -1.0).then_inc(blank_made, 1)
            nc.gpsimd.memset(rec[:, :, 3], 0.0).then_inc(consts_made, 1)
            pool.wait_ge(blank_made, 2)
            pool.dma_start(dram["rec"].rearrange("(p c) f -> p c f", p=P), blank[:, :, :]).then_inc(blank_out, 16)
            pool.wait_ge(consts_made, 11)
            pool.wait_ge(blank_out, 16)
            scatter(nc, pool, k, dram, 0, True)
            with pool.Fori(1, G) as b:
                scatter(nc, pool, k, dram, b, False)

        @block.scalar
        def _(act):
            act.wait_ge(blocks_made, 2)
            loads = [(wx, "Wx"), (wst, "WsT")]
            for tile, name in loads:
                act.dma_start(tile[:, :, :], d[name].rearrange("(k p) n -> p k n", p=P)).then_inc(weights_in, 16)
            act.dma_start(wfe[:, :, 0:D], d["Ws"].rearrange("(k p) n -> p k n", p=P)).then_inc(weights_in, 16)
            for i, name in enumerate(("WqT", "WkT")):
                for h in range(P // MD):
                    act.dma_start(bdqk[h * MD:(h + 1) * MD, i, h * MD:(h + 1) * MD], d[name]).then_inc(weights_in, 16)
            for h in range(GH):
                p0 = h % 2 * GO
                for i, c0 in ((0, GO), (1, 0)):
                    act.dma_start(bdaw[p0:p0 + GO, h // 2, i * GH + h:i * GH + h + 1],
                                  d["aw"][h, c0:c0 + GO].unsqueeze(1)).then_inc(weights_in, 16)
            act.dma_start(bcol[:, 0, :], d["bx_c"]).then_inc(weights_in, 16)
            act.dma_start(bcol[:, 1, :], d["bs_c"]).then_inc(weights_in, 16)
            act.dma_start(fbias[:, 0:D], d["bs"].partition_broadcast(P)).then_inc(weights_in, 16)
            act.dma_start(abias[:, :], d["ab"].partition_broadcast(P)).then_inc(weights_in, 16)
            act.dma_start(k["awe"][:, :], d["awe"].partition_broadcast(P)).then_inc(weights_in, 16)
            act.dma_start(ln1[:, 0, :], d["ln1_wc"]).then_inc(weights_in, 16)
            act.dma_start(ln1[:, 1, :], d["ln1_bc"]).then_inc(weights_in, 16)
            assert NW == 3 + 2 * (P // MD) + 2 * GH + 7
            act.wait_ge(fold_kept, FOLDS)
            act.wait_ge(x_in, 32)
            with act.Fori(0, G) as g:
                for i in range(2):
                    wait(act, var_go, 2 * g + i + 1)
                    nc.scalar.activation(sd[:, :], var[:, :], ACT.Sqrt).then_inc(sd_done, 1)
                    wait(act, stats_go, 2 * g + i + 1)
                    for j in range(J):
                        if i == 0:
                            nc.scalar.activation(xn[:, j, :], X[:, ds(g * J + j, 1), :].rearrange("p a c -> p (a c)"),
                                                 ACT.Identity, bias=nb[:, 0, j:j + 1],
                                                 scale=r[:, 0, j:j + 1]).then_inc(xn_done, 1)
                        else:
                            nc.scalar.activation(z[:, j, :], xn[:, j, :], ACT.Identity, bias=nb[:, 1, j:j + 1],
                                                 scale=r[:, 1, j:j + 1]).then_inc(z_done, 1)
                for j in range(J):
                    wait(act, turned, g * J + j + 1)
                    nc.scalar.copy(xnT[:, j, :], pt[j % 2][:, 0:D])
                    for c in range(KC):
                        last = nc.scalar.activation(lT[:, j, c * P:(c + 1) * P], pt[j % 2][:, D + c * P:D + (c + 1) * P],
                                                    ACT.Identity, bias=ln1[:, 1, c:c + 1], scale=ln1[:, 0, c:c + 1])
                    last.then_inc(turned_kept, 1)
                wait(act, qsub, g + 1)
                nc.scalar.activation(qk[:, :, 0:D], qk[:, :, 0:D], ACT.Exp).then_inc(qexp, 1)

        @block.tensor
        def _(pe):
            pe.wait_ge(consts_made, 10)
            pe.wait_ge(hist_done, 1)
            nc.tensor.matmul(pc[:, 0:T], before[0:EP, :], hist[:, :], start=True, stop=True)
            nc.tensor.matmul(pc[:, 64:64 + T], ones[0:EP, :], hist[:, :], start=True, stop=True).then_inc(counts_done, 1)
            pe.wait_ge(weights_in, NW * 16)
            for c2 in range(KC):
                for i in range(2):
                    for c in range(KC):
                        last = nc.tensor.matmul(pq[c2][:, i * D + c * P:i * D + (c + 1) * P],
                                                wx[:, c, c2 * P:(c2 + 1) * P], bdqk[:, i, :], start=True, stop=True)
            last.then_inc(folded, 1)
            for c2 in range(KC):
                for c in range(KC):
                    last = nc.tensor.matmul(pb[:, c2 * 16:c2 * 16 + 2 * GH], wst[:, c, c2 * P:(c2 + 1) * P],
                                            bdaw[:, c, :], start=(c == 0), stop=(c == KC - 1))
            pe.wait_ge(bias_made, 1)
            for c in range(KC):
                nc.tensor.matmul(pb[:, 64:64 + 2 * GH], bbc[:, 1, c, :], bdaw[:, c, :], start=(c == 0), stop=(c == KC - 1))
            for i in range(2):
                for c in range(KC):
                    last = nc.tensor.matmul(pf[0][:, i * D + c * P:i * D + (c + 1) * P], bbc[:, 0, c, :],
                                            bdqk[:, i, :], start=True, stop=True)
            last.then_inc(folded, 1)
            pe.wait_ge(fold_kept, FOLDS)
            pe.sem_inc(turned_kept, 1)
            pe.sem_inc(fe_kept, 1)
            pe.sem_inc(qk_kept, 1)
            with pe.Fori(0, G) as g:
                for j in range(J):
                    if j == 0:
                        wait(pe, z_done, g * J + J)
                    wait(pe, turned_kept, g * J + max(j - 1, 0) + 1)
                    for c in range(KC):
                        nc.tensor.transpose(pt[j % 2][:, c * P:(c + 1) * P], xn[:, j, c * P:(c + 1) * P], ident[:, :])
                    for c in range(KC):
                        last = nc.tensor.transpose(pt[j % 2][:, D + c * P:D + (c + 1) * P], z[:, j, c * P:(c + 1) * P],
                                                   ident[:, :])
                    last.then_inc(turned, 1)
                for j in range(J):
                    wait(pe, turned_kept, g * J + j + 2)
                    wait(pe, fe_kept, g * J + max(j - 1, 0) + 1)
                    for c in range(KC):
                        last = nc.tensor.matmul(pf[j % 2][:, 0:FX], xnT[:, j, c * P:(c + 1) * P], wfe[:, c, :],
                                                start=(c == 0), stop=(c == KC - 1))
                    last.then_inc(fe_prod, 1)
                    wait(pe, qk_kept, g * J + max(j - 1, 0) + 1)
                    for c in range(KC):
                        last = nc.tensor.matmul(pq[j % 2][:, :], lT[:, j, c * P:(c + 1) * P], wqk[:, c, :],
                                                start=(c == 0), stop=(c == KC - 1))
                    last.then_inc(qk_prod, 1)

        @block.vector
        def _(dve):
            nc.vector.memset(bdqk[:, :, :], 0.0).then_inc(blocks_made, 1)
            nc.vector.memset(bdaw[:, :, :], 0.0).then_inc(blocks_made, 1)
            nc.vector.memset(X[:, T - 1, :], 0.0).then_inc(x_cleared, 1)
            nc.vector.memset(kmax[:, :], NEG)
            nc.vector.memset(seg[:, :, :], 1.0)
            nc.vector.memset(k["tiles"][0:1, 0:UG], 0)
            nc.vector.memset(k["tiles"][0:1, UG + CH // CU:], 0)
            dve.drain()
            nc.vector.memset(seg[:, :, 0], 0.0)
            dve.wait_ge(edges_in, 48)
            nc.vector.tensor_scalar(tmp_i[:, :], src_i[:, :], 7, None, ALU.logical_shift_right)
            dve.wait_ge(consts_made, 10)
            nc.vector.tensor_copy(iota[:, :], iota_i[:, :])
            nc.vector.tensor_copy(cidx[:, :], cidx_i[:, :])
            dve.drain()
            nc.vector.tensor_copy(tile_f[:, :], tmp_i[:, :])
            dve.drain()
            for t in range(T):
                nc.vector.tensor_scalar(junk[:, :], tile_f[:, :], float(t), 0.0, ALU.is_equal, ALU.add,
                                        accum_out=hist[:, t:t + 1])
                dve.drain()
            nc.vector.tensor_scalar(tmp_i[:, :], src_i[:, :], P - 1, None, ALU.bitwise_and).then_inc(hist_done, 1)
            dve.wait_ge(counts_done, 1)
            nc.vector.tensor_scalar(nch_i[:, :], pc[:, 64:64 + T], float(UNIT - 1), None, ALU.add)
            dve.drain()
            nc.vector.tensor_scalar(nch_i[:, :], nch_i[:, :], UNIT.bit_length() - 1, None, ALU.logical_shift_right)
            dve.drain()
            nc.vector.tensor_copy(nch[:, :], nch_i[:, :])
            nc.vector.tensor_copy(rec[:, :, 1], tmp_i[:, :])
            nc.vector.tensor_copy(rec[:, :, 0], dst_i[:, :])
            nc.vector.tensor_copy(rec[:, :, 2], elem[:, :])
            dve.drain()
            nc.vector.tensor_tensor_scan(cend[:, :], onesT[:, :], nch[:, :], 0.0, ALU.mult, ALU.add)
            dve.drain()
            nc.vector.tensor_tensor(nch[:, :], cend[:, :], nch[:, :], ALU.subtract)
            nc.vector.tensor_tensor(ccmp[:, :, :], cend[0:CPP, :].unsqueeze(1).broadcast_to([CPP, UG, T]),
                                    cidx[:, :].unsqueeze(2).broadcast_to([CPP, UG, T]), ALU.is_le)
            dve.drain()
            nc.vector.tensor_scalar(nch[:, :], nch[:, :], float(UNIT), -1.0, ALU.mult, ALU.add)
            nc.vector.tensor_reduce(ctile[:, :], ccmp[:, :, :], AX, ALU.add)
            dve.drain()
            nc.vector.tensor_tensor(carry[:, :], pc[0:EP, 0:T], nch[0:EP, :], ALU.add)
            nc.vector.tensor_scalar(ctile_i[:, :], ctile[:, :], float(T - 1), None, ALU.min).then_inc(ctile_made, 1)
            dve.wait_ge(weights_in, NW * 16)
            for i in range(2):
                for c in range(KC):
                    last = nc.vector.tensor_scalar(bbc[:, i, c, :], ones[:, :], bcol[:, i, c:c + 1], None, ALU.mult)
            last.then_inc(bias_made, 1)
            dve.wait_ge(folded, 2)
            for c2 in range(KC):
                nc.vector.tensor_copy(wqk[:, c2, :], pq[c2][:, :])
                nc.vector.tensor_copy(wfe[:, c2, D:FX], pb[:, c2 * 16:c2 * 16 + 2 * GH])
            nc.vector.tensor_copy(fbias[:, D:FW], pb[:, 64:64 + GH])
            nc.vector.tensor_tensor(fbias[:, FW:FX], pb[:, 64 + GH:64 + 2 * GH], abias[:, :], ALU.add)
            nc.vector.tensor_copy(qkbias[:, :], pf[0][:, :]).then_inc(fold_kept, FOLDS)
            dve.wait_ge(x_in, 32)
            with dve.Fori(0, G) as g:
                place_edges(nc, dve, k, iota, g)
                norm_stats(nc, dve, var_go, sd_done, 2 * g + 1,
                           lambda j: X[:, ds(g * J + j, 1), :].rearrange("p a c -> p (a c)"),
                           st, mv, var, sd, r[:, 0, :], nb[:, 0, :]).then_inc(stats_go, 1)
                wait(dve, xn_done, g * J + J)
                norm_stats(nc, dve, var_go, sd_done, 2 * g + 2, lambda j: xn[:, j, :],
                           st, mv, var, sd, r[:, 1, :], nb[:, 1, :]).then_inc(stats_go, 1)
                nc.vector.tensor_tensor(tmpj[:, :], nb[:, 0, :], r[:, 1, :], ALU.mult)
                nc.vector.tensor_copy(scl[:, ds(g * J, J), 0], r[:, 0, :])
                nc.vector.tensor_copy(scl[:, ds(g * J, J), 1], nb[:, 0, :])
                nc.vector.tensor_tensor(scl[:, ds(g * J, J), 2], r[:, 0, :], r[:, 1, :], ALU.mult)
                dve.drain()
                nc.vector.tensor_tensor(scl[:, ds(g * J, J), 3], tmpj[:, :], nb[:, 1, :], ALU.add)
                wait(dve, rows_free, g + 1)
                for j in range(J):
                    wait(dve, fe_prod, g * J + j + 1)
                    nc.vector.tensor_tensor(fe[:, j, :], pf[j % 2][:, 0:FX], fbias[:, :], ALU.add).then_inc(fe_kept, 1)
                    wait(dve, qk_prod, g * J + j + 1)
                    nc.vector.scalar_tensor_tensor(out=qk[:, j, :], in0=pq[j % 2][:, :],
                                                   scalar=padneg[:, ds(g * J + j, 1)], in1=qkbias[:, :],
                                                   op0=ALU.add, op1=ALU.add).then_inc(qk_kept, 1)
                dve.drain()
                nc.vector.tensor_copy(part[:, :, :], fe[:, :, FW:FX])
                nc.vector.tensor_copy(rest[:, :, :], fe[:, :, FW:FX])
                dve.drain()
                for n in range(3):
                    nc.vector.tensor_copy(a_src[:, ds(g * J, J), n, :], part[:, :, :])
                    if n < 2:
                        nc.vector.tensor_tensor(rest[:, :, :], rest[:, :, :], part[:, :, :], ALU.subtract)
                        dve.drain()
                        nc.vector.tensor_copy(part[:, :, :], rest[:, :, :])
                        dve.drain()
                q4 = qk[:, :, 0:D].rearrange("p j (h s) -> p j h s", s=MD)
                nc.vector.tensor_reduce(qs[:, 0, :].rearrange("p (j h) -> p j h", h=MH), q4, AX, ALU.max)
                nc.vector.tensor_reduce(gmax[:, :], qk[:, :, D:2 * D].rearrange("p j c -> p c j"), AX, ALU.max)
                dve.drain()
                top = qs[:, 0, :].rearrange("p (j h) -> p j h", h=MH).unsqueeze(3).broadcast_to([P, J, MH, MD])
                nc.vector.tensor_tensor(q4, q4, top, ALU.subtract).then_inc(qsub, 1)
                nc.vector.tensor_tensor(kmax[:, :], kmax[:, :], gmax[:, :], ALU.max)
                wait(dve, qexp, g + 1)
                nc.vector.tensor_reduce(qs[:, 0, :].rearrange("p (j h) -> p j h", h=MH), q4, AX, ALU.add)
                dve.drain()
                nc.vector.reciprocal(qs[:, 1, :], qs[:, 0, :])
                dve.drain()
                inv = qs[:, 1, :].rearrange("p (j h) -> p j h", h=MH).unsqueeze(3).broadcast_to([P, J, MH, MD])
                nc.vector.tensor_tensor(q4, q4, inv, ALU.mult).then_inc(rows_ready, 1)


NW = 3 + 2 * (P // MD) + 2 * GH + 7
FOLDS = 1


def place_edges(nc, dve, k, iota, b):
    E, S, seg, carry, tile_f, pos, pos_i, eq0 = (k[n] for n in ("E", "S", "seg", "carry", "tile_f", "pos", "pos_i", "eq0"))
    cols = tile_f[:, ds(b * CB, CB)]
    dve.drain()
    nc.vector.tensor_tensor(E[:, :, :], cols.unsqueeze(1).broadcast_to([EP, T, CB]),
                            iota[0:EP, 0:T].unsqueeze(2).broadcast_to([EP, T, CB]), ALU.is_equal)
    dve.drain()
    nc.vector.tensor_copy(eq0[:, :], E[:, :, 0])
    dve.drain()
    nc.vector.tensor_tensor(E[:, :, 0], eq0[:, :], carry[:, :], ALU.add)
    dve.drain()
    nc.vector.tensor_tensor_scan(S[:, :, :].rearrange("p t c -> p (t c)"), seg[:, :, :].rearrange("p t c -> p (t c)"),
                                 E[:, :, :].rearrange("p t c -> p (t c)"), 0.0, ALU.mult, ALU.add)
    dve.drain()
    nc.vector.tensor_copy(carry[:, :], S[:, :, CB - 1])
    nc.vector.tensor_copy(E[:, :, 0], eq0[:, :])
    dve.drain()
    nc.vector.tensor_tensor(S[:, :, :], S[:, :, :], E[:, :, :], ALU.mult)
    dve.drain()
    nc.vector.tensor_reduce(pos[:, :], S[:, :, :].rearrange("p t c -> p c t"), AX, ALU.add)
    dve.drain()
    nc.vector.tensor_copy(pos_i[:, 0, :], pos[:, :])
    dve.drain()
    nc.vector.tensor_scalar(pos_i[:, 1, :], pos_i[:, 0, :], P - 1, None, ALU.bitwise_and)
    nc.vector.tensor_scalar(pos_i[:, 2, :], pos_i[:, 0, :], 7, None, ALU.logical_shift_right)
    dve.drain()
    nc.vector.scalar_tensor_tensor(out=k["order"][:, ds(b * CB, CB)], in0=pos_i[:, 1, :], scalar=float(CH),
                                   in1=pos_i[:, 2, :], op0=ALU.mult, op1=ALU.add).then_inc(k["sorted"], 1)


def scatter(nc, pool, k, dram, b, first):
    wait(pool, k["sorted"], b + 1)
    for slot in range(2):
        c0 = b * CB + slot * SC
        if not first:
            wait(pool, k["scattered"][slot], b * (16 * SC))
        nc.gpsimd.tensor_copy(k["stage_i"][:, slot, :], k["order"][:, ds(c0, SC)]).then_inc(k["staged"], 1)
        nc.gpsimd.tensor_copy(k["stage_r"][:, slot, :, :], k["rec"][:, ds(c0, SC), :]).then_inc(k["staged"], 1)
        wait(pool, k["staged"], b * 4 + slot * 2 + 2)
        for c in range(SC):
            nc.gpsimd.indirect_dma_start(dram["rec"], bass.IndirectOffsetOnAxis(k["stage_i"][:, slot, c:c + 1], 0),
                                         k["stage_r"][:, slot, c, :], None).then_inc(k["scattered"][slot], 16)


def mixer(nc, k, d, dram, sb, ps, sem):
    ctx = ExitStack()
    with ctx:
        X, scl, ident, ones, iota, kmax = (k[n] for n in ("X", "scl", "ident", "ones", "iota", "kmax"))
        w1 = sb(ctx, "w1", [P, KC, HID])
        w2 = sb(ctx, "w2", [P, HC, D])
        wxt = sb(ctx, "wxt", [P, KC, D])
        wot = sb(ctx, "wot", [P, KC, D])
        bdv = sb(ctx, "bdv", [P, P])
        headmask = sb(ctx, "headmask", [P, P])
        cols = sb(ctx, "cols", [P, 3, KC])
        b1c = sb(ctx, "b1c", [P, HC])
        rows = sb(ctx, "m_rows", [P, 4, D])
        M = sb(ctx, "M", [P, KC, D])
        chain = sb(ctx, "chain", [P, 3, KC, D])
        small = sb(ctx, "small", [P, 8])
        st = sb(ctx, "m_st", [P, J, 6])
        mv = sb(ctx, "m_mv", [P, J, 2])
        var = sb(ctx, "m_var", [P, J])
        sd = sb(ctx, "m_sd", [P, J])
        r = sb(ctx, "m_r", [P, J])
        nb = sb(ctx, "m_nb", [P, J])
        scs = sb(ctx, "scs", [P, J, 4])
        qin = sb(ctx, "qin", [P, J, D])
        qT = sb(ctx, "qT", [P, 2, D])
        xnb = sb(ctx, "xnb", [P, J, D])
        h = sb(ctx, "h", [P, J, D])
        z2 = sb(ctx, "z2", [P, J, D])
        yT = sb(ctx, "yT", [P, KC, GN])
        gT = sb(ctx, "gT", [P, HC, GN])
        zx = gT[:, :, :].rearrange("p a n -> p (a n)")[:, 0:J * 258].rearrange("p (j f) -> p j f", f=258)
        kin, kx = z2, h
        pk = [ps(ctx, f"m_pk{i}", [P, 512]) for i in range(2)]
        pt = [ps(ctx, f"m_pt{i}", [P, 512]) for i in range(2)]
        p1 = [ps(ctx, f"m_p1{i}", [P, 512]) for i in range(2)]
        p2 = [ps(ctx, f"m_p2{i}", [P, 512]) for i in range(2)]

        names = ("bd_made w_in kmax_turned kmax_col kdiag kmax_row k_in ksub kexp scs_made zx_made ktz_prod "
                 "cleared kl kl_turned klt kxt kxt_kept kvt kvt_kept m_prod m_kept q_in q_used q_turned qT_kept "
                 "att att_kept xn_made m_var_go m_sd_done m_stats z2_made z_turned yT_kept h1_prod g_made h2_prod "
                 "h2_kept k_used ones_made h_free")
        s = {n: sem(n) for n in names.split()}
        block = ctx.enter_context(nc.Block())

        zeros = yT[:, 0, :]

        def attend(pe, g, j):
            wait(pe, s["qT_kept"], g * J + j + 2)
            wait(pe, s["att_kept"], g * J + max(j - 1, 0) + 1)
            for c in range(KC):
                last = nc.tensor.matmul(pk[j % 2][:, 0:D], qT[:, j % 2, c * P:(c + 1) * P], M[:, c, :],
                                        start=(c == 0), stop=(c == KC - 1))
            last.then_inc(s["att"], 1)

        @block.sync
        def _(sp):
            sp.wait_ge(s["bd_made"], 1)
            n = 0
            for tile, name in ((w1, "W1T"), (w2, "W2T"), (wxt, "WxT"), (wot, "WoT")):
                sp.dma_start(tile[:, :, :], d[name].rearrange("(k p) n -> p k n", p=P)).then_inc(s["w_in"], 16)
            for i in range(P // MD):
                sp.dma_start(bdv[i * MD:(i + 1) * MD, i * MD:(i + 1) * MD], d["WvT"]).then_inc(s["w_in"], 16)
            for i, name in enumerate(("ln2_wc", "ln2_bc", "bx_c")):
                sp.dma_start(cols[:, i, :], d[name]).then_inc(s["w_in"], 16)
            sp.dma_start(b1c[:, :], d["b1_c"]).then_inc(s["w_in"], 16)
            for i, name in enumerate(("ln1_w", "ln1_b", "bo", "b2")):
                sp.dma_start(rows[:, i, :], d[name].partition_broadcast(P)).then_inc(s["w_in"], 16)
            sp.sem_inc(s["k_used"], 1)
            sp.sem_inc(s["q_turned"], 1)
            with sp.Fori(0, G) as g:
                wait(sp, s["k_used"], g + 1)
                sp.dma_start(kin[:, :, :], dram["qk"][ds(g * GN, GN), D:2 * D].rearrange("(j p) f -> p j f", p=P))\
                    .then_inc(s["k_in"], 16)
            with sp.Fori(0, G) as g:
                wait(sp, s["q_turned"], g * J + 1)
                sp.dma_start(qin[:, :, :], dram["qk"][ds(g * GN, GN), 0:D].rearrange("(j p) f -> p j f", p=P))\
                    .then_inc(s["q_in"], 16)

        @block.gpsimd
        def _(pool):
            with pool.Fori(G, NB) as b:
                scatter(nc, pool, k, dram, b, False)
            for slot in range(2):
                pool.wait_ge(k["scattered"][slot], NB * 16 * SC)

        @block.scalar
        def _(act):
            with act.Fori(0, G) as g:
                wait(act, s["ksub"], g + 1)
                nc.scalar.activation(kx[:, :, :], kx[:, :, :], ACT.Exp).then_inc(s["kexp"], 1)
                wait(act, s["scs_made"], g + 1)
                for j in range(J):
                    last = nc.scalar.activation(zx[:, j, 0:D], X[:, ds(g * J + j, 1), :].rearrange("p a c -> p (a c)"),
                                                ACT.Identity, bias=scs[:, j, 3:4], scale=scs[:, j, 2:3])
                last.then_inc(s["zx_made"], 1)
            with act.Fori(0, G) as g:
                wait(act, s["scs_made"], G + g + 1)
                for j in range(J):
                    last = nc.scalar.activation(xnb[:, j, :], X[:, ds(g * J + j, 1), :].rearrange("p a c -> p (a c)"),
                                                ACT.Identity, bias=scs[:, j, 1:2], scale=scs[:, j, 0:1])
                last.then_inc(s["xn_made"], 1)
                for j in range(J):
                    wait(act, s["q_turned"], g * J + j + 2)
                    if j < 2:
                        wait(act, s["att"], g * J + (0 if j == 0 else j - 1) + 1)
                    else:
                        wait(act, s["att"], g * J + j)
                    nc.scalar.copy(qT[:, j % 2, :], pt[j % 2][:, 0:D]).then_inc(s["qT_kept"], 1)
                wait(act, s["m_var_go"], g + 1)
                nc.scalar.activation(sd[:, :], var[:, :], ACT.Sqrt).then_inc(s["m_sd_done"], 1)
                wait(act, s["m_stats"], g + 1)
                for j in range(J):
                    nc.scalar.activation(z2[:, j, :], h[:, j, :], ACT.Identity, bias=nb[:, j:j + 1],
                                         scale=r[:, j:j + 1]).then_inc(s["z2_made"], 1)
                for j in range(J):
                    wait(act, s["z_turned"], g * J + j + 1)
                    for c in range(KC):
                        last = nc.scalar.activation(yT[:, c, j * P:(j + 1) * P], pt[j % 2][:, c * P:(c + 1) * P],
                                                    ACT.Identity, bias=cols[:, 1, c:c + 1], scale=cols[:, 0, c:c + 1])
                    last.then_inc(s["yT_kept"], 1)
                for n in range(2 * HC):
                    hc, half = n // 2, n % 2
                    wait(act, s["h1_prod"], g * 2 * HC + n + 1)
                    nc.scalar.activation(gT[:, hc, half * HALF:(half + 1) * HALF], p1[half][:, 0:HALF], ACT.Gelu,
                                         bias=b1c[:, hc:hc + 1]).then_inc(s["g_made"], 1)

        @block.tensor
        def _(pe):
            for c in range(KC):
                last = nc.tensor.transpose(pt[0][:, c * P:(c + 1) * P], kmax[:, c * P:(c + 1) * P], ident[:, :])
            last.then_inc(s["kmax_turned"], 1)
            pe.wait_ge(s["kdiag"], 1)
            nc.tensor.matmul(pt[1][:, 0:D], ones[:, :], chain[:, 0, 0, :], start=True, stop=True).then_inc(s["kmax_row"], 1)
            pe.wait_ge(s["bd_made"], 1)
            for c in range(KC):
                nc.tensor.matmul(pk[c][:, 0:D + 2], zeros[:, 0:P], zeros[:, 0:D + 2], start=True, stop=False, skip_group_check=True)
            with pe.Fori(0, G) as g:
                wait(pe, s["kexp"], g + 1)
                wait(pe, s["zx_made"], g + 1)
                for j in range(J):
                    for c in range(KC):
                        last = nc.tensor.matmul(pk[c][:, 0:D + 2], kx[:, j, c * P:(c + 1) * P], zx[:, j, :],
                                                start=False, stop=False, skip_group_check=True)
                last.then_inc(s["ktz_prod"], 1)
            for c in range(KC):
                last = nc.tensor.matmul(pk[c][:, 0:D + 2], zeros[:, 0:P], zeros[:, 0:D + 2], start=False, stop=True,
                                        skip_group_check=True)
            last.then_inc(s["ktz_prod"], 1)
            pe.wait_ge(s["kl"], 1)
            for kk in range(KC):
                for c in range(KC):
                    last = nc.tensor.transpose(pt[0][:, kk * D + c * P:kk * D + (c + 1) * P],
                                               chain[:, 0, c, kk * P:(kk + 1) * P], ident[:, :])
            last.then_inc(s["kl_turned"], 1)
            pe.wait_ge(s["w_in"], 16 * 16)
            pe.wait_ge(s["klt"], 1)
            for c in range(KC):
                for kk in range(KC):
                    last = nc.tensor.matmul(pt[1][:, c * P:(c + 1) * P], wxt[:, kk, c * P:(c + 1) * P],
                                            chain[:, 1, kk, c * P:(c + 1) * P], start=(kk == 0), stop=(kk == KC - 1))
            last.then_inc(s["kxt"], 1)
            pe.wait_ge(s["kxt_kept"], 1)
            last = nc.tensor.matmul(pt[0][:, 0:D], bdv[:, :], chain[:, 2, 0, :], start=True, stop=True)
            last.then_inc(s["kvt"], 1)
            pe.wait_ge(s["kvt_kept"], 1)
            for c in range(KC):
                last = nc.tensor.matmul(pt[1][:, c * D:(c + 1) * D], chain[:, 0, 0, c * P:(c + 1) * P], wot[:, c, :],
                                        start=True, stop=True)
            last.then_inc(s["m_prod"], 1)
            pe.wait_ge(s["m_kept"], 1)
            pe.sem_inc(s["att"], 1)
            pe.sem_inc(s["att_kept"], 1)
            pe.sem_inc(s["g_made"], 2)
            pe.sem_inc(s["h2_kept"], 1)
            with pe.Fori(0, G) as g:
                wait(pe, s["q_in"], g * 16 + 16)
                for j in range(J):
                    wait(pe, s["qT_kept"], g * J + max(j - 1, 0) + 1)
                    for c in range(KC):
                        last = nc.tensor.transpose(pt[j % 2][:, c * P:(c + 1) * P], qin[:, j, c * P:(c + 1) * P], ident[:, :])
                    last.then_inc(s["q_turned"], 1)
                    if j:
                        attend(pe, g, j - 1)
                attend(pe, g, J - 1)
                wait(pe, s["z2_made"], g * J + J)
                for j in range(J):
                    wait(pe, s["yT_kept"], g * J + max(j - 1, 0) + 1)
                    for c in range(KC):
                        last = nc.tensor.transpose(pt[j % 2][:, c * P:(c + 1) * P], z2[:, j, c * P:(c + 1) * P], ident[:, :])
                    last.then_inc(s["z_turned"], 1)
                wait(pe, s["yT_kept"], g * J + J + 1)
                for n in range(2 * HC):
                    hc, half = n // 2, n % 2
                    wait(pe, s["g_made"], g * 2 * HC + n + 1)
                    for c in range(KC):
                        last = nc.tensor.matmul(p1[half][:, 0:HALF], w1[:, c, hc * P:(hc + 1) * P],
                                                yT[:, c, half * HALF:(half + 1) * HALF],
                                                start=(c == 0), stop=(c == KC - 1))
                    last.then_inc(s["h1_prod"], 1)
                wait(pe, s["g_made"], g * 2 * HC + 2 * HC + 2)
                for j in range(J):
                    wait(pe, s["h2_kept"], g * J + max(j - 1, 0) + 1)
                    for hc in range(HC):
                        last = nc.tensor.matmul(p2[j % 2][:, 0:D], gT[:, hc, j * P:(j + 1) * P], w2[:, hc, :],
                                                start=(hc == 0), stop=(hc == HC - 1))
                    last.then_inc(s["h2_prod"], 1)

        @block.vector
        def _(dve):
            nc.vector.memset(bdv[:, :], 0.0)
            nc.vector.memset(headmask[:, :], 0.0)
            nc.vector.memset(zx[:, :, D:D + 2], 1.0)
            nc.vector.memset(zeros[:, 0:D + 2], 0.0)
            dve.drain()
            for i in range(P // MD):
                last = nc.vector.memset(headmask[i * MD:(i + 1) * MD, i * MD:(i + 1) * MD], 1.0)
            last.then_inc(s["bd_made"], 1)
            dve.sem_inc(s["qT_kept"], 1)
            dve.sem_inc(s["yT_kept"], 1)
            dve.wait_ge(s["kmax_turned"], 1)
            nc.vector.tensor_reduce(small[:, 0:KC], pt[0][:, 0:D].rearrange("p (k q) -> p k q", k=KC), AX, ALU.max)
            dve.drain()
            for c in range(KC):
                last = nc.vector.tensor_scalar(chain[:, 0, 0, c * P:(c + 1) * P], ident[:, :], small[:, c:c + 1], None, ALU.mult)
            last.then_inc(s["kdiag"], 1)
            dve.wait_ge(s["kmax_row"], 1)
            nc.vector.tensor_copy(chain[:, 1, 0, :], pt[1][:, 0:D])
            dve.drain()
            krow = chain[:, 1, 0, :].unsqueeze(1).broadcast_to([P, J, D])
            dve.sem_inc(s["ktz_prod"], 1)
            with dve.Fori(0, G) as g:
                wait(dve, s["ktz_prod"], g + 1)
                nc.vector.tensor_copy(scs[:, :, :], scl[:, ds(g * J, J), :]).then_inc(s["scs_made"], 1)
                wait(dve, s["k_in"], g * 16 + 16)
                nc.vector.tensor_tensor(kx[:, :, :], kin[:, :, :], krow, ALU.subtract).then_inc(s["ksub"], 1)
                wait(dve, s["ksub"], g + 1)
                dve.sem_inc(s["k_used"], 1)
                place_edges(nc, dve, k, iota, g + G)
            dve.wait_ge(s["ktz_prod"], G + 2)
            dve.wait_ge(s["w_in"], 16 * 16)
            for c in range(KC):
                nc.vector.reciprocal(small[:, 2 + c:3 + c], pk[c][:, D:D + 1])
            dve.drain()
            for c in range(KC):
                nc.vector.scalar_tensor_tensor(out=chain[:, 0, c, :], in0=pk[c][:, 0:D], scalar=small[:, 2 + c:3 + c],
                                               in1=rows[:, 0, :], op0=ALU.mult, op1=ALU.mult)
            dve.drain()
            nc.vector.tensor_tensor(chain[:, 0, :, :], chain[:, 0, :, :],
                                    rows[:, 1, :].unsqueeze(1).broadcast_to([P, KC, D]), ALU.add).then_inc(s["kl"], 1)
            dve.wait_ge(s["kl_turned"], 1)
            nc.vector.tensor_copy(chain[:, 1, :, :], pt[0][:, :].rearrange("p (k c) -> p k c", k=KC)).then_inc(s["klt"], 1)
            dve.wait_ge(s["kxt"], 1)
            for c in range(KC):
                last = nc.vector.scalar_tensor_tensor(out=chain[:, 2, 0, c * P:(c + 1) * P], in0=pt[1][:, c * P:(c + 1) * P],
                                                      scalar=cols[:, 2, c:c + 1], in1=headmask[:, :],
                                                      op0=ALU.add, op1=ALU.mult)
            last.then_inc(s["kxt_kept"], 1)
            dve.wait_ge(s["kvt"], 1)
            nc.vector.tensor_copy(chain[:, 0, 0, :], pt[0][:, 0:D]).then_inc(s["kvt_kept"], 1)
            dve.wait_ge(s["m_prod"], 1)
            nc.vector.tensor_copy(M[:, :, :], pt[1][:, :].rearrange("p (k c) -> p k c", k=KC)).then_inc(s["m_kept"], 1)

            def body(g, sort):
                wait(dve, s["h_free"], g + 1)
                nc.vector.tensor_copy(scs[:, :, :], scl[:, ds(g * J, J), :]).then_inc(s["scs_made"], 1)
                wait(dve, s["xn_made"], g + 1)
                nc.vector.tensor_tensor(xnb[:, :, :], xnb[:, :, :], rows[:, 2, :].unsqueeze(1).broadcast_to([P, J, D]), ALU.add)
                dve.drain()
                for j in range(J):
                    wait(dve, s["att"], g * J + j + 2)
                    nc.vector.tensor_tensor(h[:, j, :], pk[j % 2][:, 0:D], xnb[:, j, :], ALU.add).then_inc(s["att_kept"], 1)
                dve.drain()
                norm_stats(nc, dve, s["m_var_go"], s["m_sd_done"], g + 1, lambda j: h[:, j, :],
                           st, mv, var, sd, r, nb).then_inc(s["m_stats"], 1)
                if sort:
                    place_edges(nc, dve, k, iota, g + 2 * G)
                xg = X[:, ds(g * J, J), :]
                nc.vector.tensor_tensor(xg, xg, h[:, :, :], ALU.add)
                dve.drain()
                nc.vector.tensor_tensor(xg, xg, rows[:, 3, :].unsqueeze(1).broadcast_to([P, J, D]), ALU.add)
                dve.drain()
                for j in range(J):
                    xt = X[:, ds(g * J + j, 1), :].rearrange("p a c -> p (a c)")
                    wait(dve, s["h2_prod"], g * J + j + 1)
                    nc.vector.tensor_tensor(xt, xt, p2[j % 2][:, 0:D], ALU.add).then_inc(s["h2_kept"], 1)
                dve.drain()
                dve.sem_inc(s["h_free"], 1)

            dve.sem_inc(s["h_free"], 1)
            with dve.Fori(0, NB - 2 * G) as g:
                body(g, True)
            for g in range(NB - 2 * G, G):
                body(g, False)


def graph(nc, k, d, dram, sb, ps, sem):
    ctx = ExitStack()
    with ctx:
        X, a_src, ident, iota, awe = (k[n] for n in ("X", "a_src", "ident", "iota", "awe"))
        erec = sb(ctx, "erec", [P, CH + 2 * B, 4])
        acc = sb(ctx, "acc", [P, T, FW])
        hot = sb(ctx, "hot", [P, 2, B, P])
        hotT = sb(ctx, "hotT", [P, 2, B, P], BF16)
        rows = sb(ctx, "g_rows", [P, 2, B, FW])
        wrows = sb(ctx, "wrows", [P, 2, B, FW])
        ew = sb(ctx, "ew", [P, 2, B, GH])
        pre = sb(ctx, "pre", [P, 2, B, GH])
        sc = sb(ctx, "sc", [P, 2, B, GH])
        gi = sb(ctx, "gi", [P, 2, B], I32)
        pad_i = sb(ctx, "pad_i", [P, 1])
        warm = sb(ctx, "warm", [P, 2])
        inv = sb(ctx, "g_inv", [P, J, GH])
        pT = [ps(ctx, f"g_pT{i}", [P, 512]) for i in range(2)]
        pA = [ps(ctx, f"g_pA{i}", [P, 512]) for i in range(2)]
        pO = [ps(ctx, f"g_pO{i}", [P, 512]) for i in range(UG)]
        gathered = [sem("gathered0"), sem("gathered1")]
        s = {n: sem(n) for n in ("rec_in idx_made hot_made hot_turned hotT_kept a_prod pre_made sc_made w_made "
                                 "scaled out_prod acc_done pad_made").split()}
        block = ctx.enter_context(nc.Block())

        @block.sync
        def _(sp):
            sp.dma_start(erec[:, 0:CH, :], dram["rec"].rearrange("(p c) f -> p c f", p=P)).then_inc(s["rec_in"], 16)
            sp.wait_ge(s["rec_in"], 16)

        @block.gpsimd
        def _(pool):
            nc.gpsimd.memset(pad_i[:, :], 0.0).then_inc(s["pad_made"], 1)
            pool.wait_ge(s["pad_made"], 1)
            nc.gpsimd.affine_select(out=pad_i[:, :], in_=pad_i[:, :], compare_op=ALU.is_gt, fill=1.0,
                                    base=LAST, pattern=[[0, 1]], channel_multiplier=-1).then_inc(s["pad_made"], 1)
            pool.wait_ge(s["rec_in"], 16)
            pool.sem_inc(s["scaled"], 2)
            with pool.Fori(0, CI) as i:
                for u in range(2):
                    q = i * 2 + u
                    wait(pool, s["scaled"], q + 1)
                    nc.gpsimd.tensor_copy(gi[:, u, :], erec[:, ds(q * B, B), 0]).then_inc(s["idx_made"], 1)
                    wait(pool, s["idx_made"], q + 1)
                    for b in range(B):
                        nc.gpsimd.indirect_dma_start(rows[:, u, b, :], None, dram["feat"],
                                                     bass.IndirectOffsetOnAxis(gi[:, u, b:b + 1], 0))\
                            .then_inc(gathered[u], 16)

        @block.scalar
        def _(act):
            def keep_turned(q, u):
                wait(act, s["hot_turned"], q + 1)
                for n in range(2):
                    last = nc.scalar.copy(hotT[:, u, 4 * n:4 * n + 4, :].rearrange("p b e -> p (b e)"), pT[n][:, :])
                last.then_inc(s["hotT_kept"], 1)

            keep_turned(0, 0)
            with act.Fori(0, CI) as i:
                nc.scalar.activation(warm[:, 1:2], warm[:, 0:1], ACT.Exp)
                for u in range(2):
                    q = i * 2 + u
                    wait(act, s["sc_made"], q + 1)
                    nc.scalar.activation(wrows[:, u, :, D:FW], sc[:, u, :, :], ACT.Exp).then_inc(s["w_made"], 1)
                    keep_turned(q + 1, 1 - u)

        @block.tensor
        def _(pe):
            def turn(q, u):
                wait(pe, s["hot_made"], q + 1)
                wait(pe, s["hotT_kept"], q + 1)
                for b in range(B):
                    last = nc.tensor.transpose(pT[b // 4][:, b % 4 * P:(b % 4 + 1) * P], hot[:, u, b, :], ident[:, :])
                last.then_inc(s["hot_turned"], 1)

            def source_scores(q, u, tiles):
                wait(pe, s["hotT_kept"], q + 2)
                wait(pe, s["pre_made"], q + 1)
                for b in range(B):
                    last = nc.tensor.matmul(pA[u][:, b * 3 * GH:(b + 1) * 3 * GH], hotT[:, u, b, :],
                                            a_src[:, ds(tiles[b // CU], 1), :, :].rearrange("p a n h -> p (a n h)"),
                                            start=True, stop=True)
                last.then_inc(s["a_prod"], 1)

            def load_tiles(c0, n):
                _, regs = nc.values_load_multi_w_load_instructions(
                    k["tiles"][0:1, ds(c0, n)], engines=[pe.engine], min_val=0, max_val=T - 1,
                    skip_runtime_bounds_check_because="the tile numbers are clipped where the table is made")
                return regs

            pe.sem_inc(s["hotT_kept"], 1)
            pe.sem_inc(s["pre_made"], 2)
            turn(0, 0)
            source_scores(0, 0, load_tiles(UG, UG))
            for n in range(UG):
                nc.tensor.matmul(pO[n][:, 0:FW], hot[:, 1, n, :], wrows[:, 1, n, :], start=True, stop=True)\
                    .then_inc(s["out_prod"], 1)
            with pe.Fori(0, CI) as i:
                tiles = load_tiles(i * 2 * UG + 2 * UG, 2 * UG)
                for u in range(2):
                    q = i * 2 + u
                    turn(q + 1, 1 - u)
                    wait(pe, s["scaled"], q + 3)
                    for n in range(UG):
                        if n == 1:
                            source_scores(q + 1, 1 - u, tiles[u * UG:(u + 1) * UG])
                        wait(pe, s["acc_done"], q * UG + n + 1)
                        for c in range(CU):
                            b = n * CU + c
                            last = nc.tensor.matmul(pO[n][:, 0:FW], hot[:, u, b, :], wrows[:, u, b, :],
                                                    start=(c == 0), stop=(c == CU - 1))
                        last.then_inc(s["out_prod"], 1)

        @block.vector
        def _(dve):
            def make_hot(q, u):
                nc.vector.tensor_tensor(hot[:, u, :, :], iota[:, :].unsqueeze(1).broadcast_to([P, B, P]),
                                        erec[:, ds(q * B, B), 1].unsqueeze(2).broadcast_to([P, B, P]),
                                        ALU.is_equal).then_inc(s["hot_made"], 1)

            def weight_part(q, u):
                nc.vector.tensor_tensor(ew[:, u, :, :], erec[:, ds(q * B, B), 2].unsqueeze(2).broadcast_to([P, B, GH]),
                                        awe[:, :].unsqueeze(1).broadcast_to([P, B, GH]), ALU.mult)

            def known_part(q, u):
                wait(dve, s["a_prod"], q + 1)
                nc.vector.tensor_reduce(pre[:, u, :, :],
                                        pA[u][:, 0:B * 3 * GH].rearrange("p (b n h) -> p b h n", n=3, h=GH), AX, ALU.add)
                dve.drain()
                nc.vector.tensor_tensor(pre[:, u, :, :], pre[:, u, :, :], ew[:, u, :, :], ALU.add)\
                    .then_inc(s["pre_made"], 1)

            def add_sums(q, tiles):
                for n in range(UG):
                    at = acc[:, ds(tiles[n], 1), :].rearrange("p a f -> p (a f)")
                    wait(dve, s["out_prod"], (q + 1) * UG + n + 1)
                    if n:
                        wait(dve, s["acc_done"], (q + 1) * UG + n)
                    nc.vector.tensor_tensor(at, at, pO[n][:, 0:FW], ALU.add).then_inc(s["acc_done"], 1)

            nc.vector.memset(hot[:, 1, :, :], 0.0)
            nc.vector.memset(wrows[:, 1, :, :], 0.0)
            nc.vector.memset(acc[:, :, :], 0.0)
            nc.vector.memset(erec[:, CH:, :], 0.0)
            nc.vector.memset(warm[:, :], 0.0)
            dve.drain()
            dve.wait_ge(s["pad_made"], 2)
            nc.vector.tensor_copy(acc[:, T - 1, D:FW], pad_i[:, 0:1].broadcast_to([P, GH]))
            dve.wait_ge(s["rec_in"], 16)
            make_hot(0, 0)
            weight_part(0, 0)
            dve.drain()
            known_part(0, 0)

            def load_tiles(c0, n):
                _, regs = nc.values_load_multi_w_load_instructions(
                    k["tiles"][0:1, ds(c0, n)], engines=[dve.engine], min_val=0, max_val=T - 1,
                    skip_runtime_bounds_check_because="the tile numbers are clipped where the table is made")
                return regs

            with dve.Fori(0, CI) as i:
                tiles = load_tiles(i * 2 * UG, 2 * UG)
                for u in range(2):
                    q = i * 2 + u
                    dve.drain()
                    wait(dve, gathered[u], i * (16 * B) + 16 * B)
                    nc.vector.tensor_tensor(sc[:, u, :, :], pre[:, u, :, :], rows[:, u, :, D:FW], ALU.add)
                    dve.drain()
                    nc.vector.tensor_scalar(sc[:, u, :, :], sc[:, u, :, :], 0.0, -1.0 / 20.0, ALU.max, ALU.mult)\
                        .then_inc(s["sc_made"], 1)
                    wait(dve, s["out_prod"], q * UG + UG)
                    make_hot(q + 1, 1 - u)
                    weight_part(q + 1, 1 - u)
                    wait(dve, s["w_made"], q + 1)
                    nc.vector.tensor_tensor(wrows[:, u, :, 0:D].rearrange("p b (h o) -> p b h o", o=GO),
                                            rows[:, u, :, 0:D].rearrange("p b (h o) -> p b h o", o=GO),
                                            wrows[:, u, :, D:FW].unsqueeze(3).broadcast_to([P, B, GH, GO]),
                                            ALU.mult).then_inc(s["scaled"], 1)
                    add_sums(q - 1, tiles[u * UG:(u + 1) * UG])
                    known_part(q + 1, 1 - u)
            dve.drain()
            add_sums(2 * CI - 1, load_tiles(CH // CU, UG))
            dve.drain()
            for g in range(G):
                t0 = g * J
                nc.vector.reciprocal(inv[:, :, :], acc[:, t0:t0 + J, D:FW])
                dve.drain()
                a4 = acc[:, t0:t0 + J, 0:D].rearrange("p j (h o) -> p j h o", o=GO)
                nc.vector.tensor_tensor(a4, a4, inv[:, :, :].unsqueeze(3).broadcast_to([P, J, GH, GO]), ALU.mult)
                dve.drain()
                nc.vector.tensor_tensor(X[:, t0:t0 + J, :], X[:, t0:t0 + J, :], acc[:, t0:t0 + J, 0:D], ALU.add)


def experts(nc, k, d, dram, sb, ps, sem):
    ctx = ExitStack()
    with ctx:
        X, ident = k["X"], k["ident"]
        w1 = sb(ctx, "e_w1", [P, NE, KC, EH])
        w2 = sb(ctx, "e_w2", [P, NE, EHC, D])
        wg = sb(ctx, "wg", [P, KC, NE])
        bg = sb(ctx, "bg", [P, NE])
        b1 = sb(ctx, "e_b1", [P, NE, EHC])
        b2 = sb(ctx, "e_b2", [NE, D])
        st = sb(ctx, "e_st", [P, J, 6])
        mv = sb(ctx, "e_mv", [P, J, 2])
        var = sb(ctx, "e_var", [P, J])
        sd = sb(ctx, "e_sd", [P, J])
        r = sb(ctx, "e_r", [P, J])
        nb = sb(ctx, "e_nb", [P, J])
        z = sb(ctx, "e_z", [P, J, D])
        zT = sb(ctx, "e_zT", [P, KC, GN])
        gT = sb(ctx, "e_gT", [P, EHC, GN])
        gate = sb(ctx, "gate", [P, J, NE])
        rank_i = sb(ctx, "rank_i", [P, NE], I32)
        rank = sb(ctx, "rank", [P, NE])
        m1 = sb(ctx, "m1", [P, J])
        eq = sb(ctx, "eq", [P, J, NE])
        hot1 = sb(ctx, "hot1", [P, J, NE])
        mask = sb(ctx, "mask", [P, J, NE])
        maskT = sb(ctx, "maskT", [NE, GN])
        Y = sb(ctx, "Y", [P, J, D])
        pt = [ps(ctx, f"e_pt{i}", [P, 512]) for i in range(2)]
        pg = ps(ctx, "e_pg", [P, 512])
        pb = ps(ctx, "e_pb", [P, 512])
        p1 = [ps(ctx, f"e_p1{i}", [P, 512]) for i in range(2)]
        p2 = [ps(ctx, f"e_p2{i}", [P, 512]) for i in range(2)]
        s = {n: sem("e_" + n) for n in ("w_in rank_made var_go sd_done stats z_made z_turned zT_kept gate_prod "
                                        "mask_made mask_turned maskT_kept b_prod y_started h_prod g_made y_prod "
                                        "y_kept out_made out_done out_free").split()}
        block = ctx.enter_context(nc.Block())

        @block.sync
        def _(sp):
            sp.dma_start(wg[:, :, :], d["Wg"].rearrange("(k p) n -> p k n", p=P)).then_inc(s["w_in"], 16)
            sp.dma_start(bg[:, :], d["bg"].partition_broadcast(P)).then_inc(s["w_in"], 16)
            sp.dma_start(b1[:, :, :], d["eb1_c"]).then_inc(s["w_in"], 16)
            sp.dma_start(b2[:, :], d["eb2"]).then_inc(s["w_in"], 16)
            for e in range(NE):
                sp.dma_start(w1[:, e, :, :], d["eW1"][e].rearrange("(k p) n -> p k n", p=P)).then_inc(s["w_in"], 16)
                sp.dma_start(w2[:, e, :, :], d["eW2"][e].rearrange("(k p) n -> p k n", p=P)).then_inc(s["w_in"], 16)
            with sp.Fori(0, G - 1) as g:
                wait(sp, s["out_made"], g + 1)
                sp.dma_start(dram["out"][ds(g * GN, GN), :].rearrange("(j p) c -> p j c", p=P), Y[:, :, :])\
                    .then_inc(s["out_done"], 16)
                wait(sp, s["out_done"], g * 16 + 16)
                sp.sem_inc(s["out_free"], 1)
            sp.wait_ge(s["out_made"], G)
            n0 = (G - 1) * GN
            sp.dma_start(dram["out"][n0:n0 + (J - 1) * P, :].rearrange("(j p) c -> p j c", p=P),
                         Y[:, 0:J - 1, :]).then_inc(s["out_done"], 16)
            sp.dma_start(dram["out"][n0 + (J - 1) * P:N, :], Y[0:LAST, J - 1, :]).then_inc(s["out_done"], 16)
            sp.wait_ge(s["out_done"], 16 * (G + 1))

        @block.gpsimd
        def _(pool):
            nc.gpsimd.iota(rank_i[:, :], pattern=[[-1, NE]], base=NE, channel_multiplier=0).then_inc(s["rank_made"], 1)

        @block.scalar
        def _(act):
            act.wait_ge(s["w_in"], 16 * NWALL)
            with act.Fori(0, G) as g:
                wait(act, s["var_go"], g + 1)
                nc.scalar.activation(sd[:, :], var[:, :], ACT.Sqrt).then_inc(s["sd_done"], 1)
                wait(act, s["stats"], g + 1)
                for j in range(J):
                    nc.scalar.activation(z[:, j, :], X[:, ds(g * J + j, 1), :].rearrange("p a c -> p (a c)"),
                                         ACT.Identity, bias=nb[:, j:j + 1], scale=r[:, j:j + 1]).then_inc(s["z_made"], 1)
                for j in range(J):
                    wait(act, s["z_turned"], g * J + j + 1)
                    nc.scalar.copy(zT[:, :, j * P:(j + 1) * P], pt[j % 2][:, 0:D].rearrange("p (k c) -> p k c", k=KC))\
                        .then_inc(s["zT_kept"], 1)
                for e in range(NE):
                    for n in range(2 * EHC):
                        hc, half = n // 2, n % 2
                        wait(act, s["h_prod"], g * (2 * EHC * NE) + e * 2 * EHC + n + 1)
                        if n == 0:
                            wait(act, s["y_prod"], g * (J * NE) + e * J + 1)
                        nc.scalar.activation(gT[:, hc, half * HALF:(half + 1) * HALF], p1[half][:, 0:HALF], ACT.Gelu,
                                             bias=b1[:, e, hc:hc + 1]).then_inc(s["g_made"], 1)

        @block.tensor
        def _(pe):
            pe.wait_ge(s["w_in"], 16 * NWALL)
            pe.sem_inc(s["zT_kept"], 1)
            pe.sem_inc(s["g_made"], 2)
            pe.sem_inc(s["y_kept"], 1)
            pe.sem_inc(s["y_started"], 1)
            pe.sem_inc(s["y_prod"], 1)
            with pe.Fori(0, G) as g:
                wait(pe, s["z_made"], g * J + J)
                for j in range(J):
                    wait(pe, s["zT_kept"], g * J + max(j - 1, 0) + 1)
                    for c in range(KC):
                        last = nc.tensor.transpose(pt[j % 2][:, c * P:(c + 1) * P], z[:, j, c * P:(c + 1) * P], ident[:, :])
                    last.then_inc(s["z_turned"], 1)
                wait(pe, s["zT_kept"], g * J + J + 1)
                for j in range(J):
                    for c in range(KC):
                        last = nc.tensor.matmul(pg[:, j * NE:(j + 1) * NE], zT[:, c, j * P:(j + 1) * P], wg[:, c, :],
                                                start=(c == 0), stop=(c == KC - 1))
                last.then_inc(s["gate_prod"], 1)
                for e in range(NE):
                    if e == 1:
                        wait(pe, s["mask_made"], g + 1)
                        for j in range(J):
                            last = nc.tensor.transpose(pt[j // 4][0:NE, j % 4 * P:(j % 4 + 1) * P], mask[:, j, :], ident[:, :])
                        last.then_inc(s["mask_turned"], 1)
                    for n in range(2 * EHC):
                        hc, half = n // 2, n % 2
                        wait(pe, s["g_made"], g * (2 * EHC * NE) + e * 2 * EHC + n + 1)
                        for c in range(KC):
                            last = nc.tensor.matmul(p1[half][:, 0:HALF], w1[:, e, c, hc * P:(hc + 1) * P],
                                                    zT[:, c, half * HALF:(half + 1) * HALF],
                                                    start=(c == 0), stop=(c == KC - 1))
                        last.then_inc(s["h_prod"], 1)
                    wait(pe, s["g_made"], g * (2 * EHC * NE) + (e + 1) * 2 * EHC + 2)
                    for j in range(J):
                        wait(pe, s["y_kept"], g * (J * NE) + e * J + max(j - 1, 0) + 1)
                        for hc in range(EHC):
                            last = nc.tensor.matmul(p2[j % 2][:, 0:D], gT[:, hc, j * P:(j + 1) * P], w2[:, e, hc, :],
                                                    start=(hc == 0), stop=(hc == EHC - 1))
                        last.then_inc(s["y_prod"], 1)
                wait(pe, s["maskT_kept"], g + 1)
                for j in range(J):
                    wait(pe, s["y_started"], g * J + j + 1)
                    nc.tensor.matmul(pb[:, 0:D], maskT[:, j * P:(j + 1) * P], b2[:, :], start=True, stop=True)\
                        .then_inc(s["b_prod"], 1)

        @block.vector
        def _(dve):
            dve.wait_ge(s["w_in"], 16 * NWALL)
            dve.wait_ge(s["rank_made"], 1)
            nc.vector.tensor_copy(rank[:, :], rank_i[:, :])
            dve.drain()
            rank3 = rank[:, :].unsqueeze(1).broadcast_to([P, J, NE])

            def pick_top(values, hot):
                nc.vector.tensor_reduce(m1[:, :], values, AX, ALU.max)
                dve.drain()
                nc.vector.tensor_tensor(eq[:, :, :], values, m1[:, :].unsqueeze(2).broadcast_to([P, J, NE]), ALU.is_equal)
                dve.drain()
                nc.vector.tensor_tensor(eq[:, :, :], eq[:, :, :], rank3, ALU.mult)
                dve.drain()
                nc.vector.tensor_reduce(m1[:, :], eq[:, :, :], AX, ALU.max)
                dve.drain()
                nc.vector.tensor_tensor(hot, m1[:, :].unsqueeze(2).broadcast_to([P, J, NE]), rank3, ALU.is_equal)
                dve.drain()

            dve.sem_inc(s["out_free"], 1)
            with dve.Fori(0, G) as g:
                norm_stats(nc, dve, s["var_go"], s["sd_done"], g + 1,
                           lambda j: X[:, ds(g * J + j, 1), :].rearrange("p a c -> p (a c)"),
                           st, mv, var, sd, r, nb).then_inc(s["stats"], 1)
                wait(dve, s["gate_prod"], g + 1)
                nc.vector.tensor_tensor(gate[:, :, :], pg[:, 0:J * NE].rearrange("p (j e) -> p j e", e=NE),
                                        bg[:, :].unsqueeze(1).broadcast_to([P, J, NE]), ALU.add)
                dve.drain()
                pick_top(gate[:, :, :], hot1[:, :, :])
                nc.vector.scalar_tensor_tensor(out=gate[:, :, :], in0=hot1[:, :, :], scalar=-3e38, in1=gate[:, :, :],
                                               op0=ALU.mult, op1=ALU.add)
                dve.drain()
                pick_top(gate[:, :, :], mask[:, :, :])
                nc.vector.tensor_tensor(mask[:, :, :], mask[:, :, :], hot1[:, :, :], ALU.add).then_inc(s["mask_made"], 1)
                wait(dve, s["out_free"], g + 1)
                dve.drain()
                for e in range(NE):
                    for j in range(J):
                        wait(dve, s["y_prod"], g * (J * NE) + e * J + j + 2)
                        if e == 0:
                            nc.vector.tensor_scalar(Y[:, j, :], p2[j % 2][:, 0:D], mask[:, j, e:e + 1], None, ALU.mult)\
                                .then_inc(s["y_kept"], 1)
                        else:
                            nc.vector.scalar_tensor_tensor(out=Y[:, j, :], in0=p2[j % 2][:, 0:D], scalar=mask[:, j, e:e + 1],
                                                           in1=Y[:, j, :], op0=ALU.mult, op1=ALU.add)\
                                .then_inc(s["y_kept"], 1)
                    dve.drain()
                    if e == 1:
                        wait(dve, s["mask_turned"], g + 1)
                        nc.vector.tensor_copy(maskT[:, 0:4 * P], pt[0][0:NE, 0:4 * P])
                        nc.vector.tensor_copy(maskT[:, 4 * P:GN], pt[1][0:NE, 0:3 * P]).then_inc(s["maskT_kept"], 1)
                nc.vector.tensor_tensor(Y[:, :, :], Y[:, :, :], X[:, ds(g * J, J), :], ALU.add)
                dve.drain()
                for j in range(J):
                    wait(dve, s["b_prod"], g * J + j + 1)
                    nc.vector.tensor_tensor(Y[:, j, :], Y[:, j, :], pb[:, 0:D], ALU.add).then_inc(s["y_started"], 1)
                wait(dve, s["y_started"], g * J + J + 1)
                dve.sem_inc(s["out_made"], 1)


NWALL = 4 + 2 * NE


def build(nc, d, out):
    dram = {
        "feat": nc.dram_tensor("feat", (T * P, FW), F32, kind="Internal").ap(),
        "qk": nc.dram_tensor("qk_rows", (T * P, 2 * D), F32, kind="Internal").ap(),
        "rec": nc.dram_tensor("edge_records", (P * CH, 4), F32, kind="Internal").ap(),
        "ctile": nc.dram_tensor("unit_tiles", (CH // CU,), I32, kind="Internal").ap(),
        "out": out,
    }
    with ExitStack() as ctx:
        def sb(stack, name, shape, dt=F32):
            return stack.enter_context(nc.sbuf_tensor(name, shape, dt))

        def ps(stack, name, shape):
            return stack.enter_context(nc.psum_tensor(name, shape, F32))

        def sem(name):
            return ctx.enter_context(nc.semaphore(name))

        k = constants(nc, ctx, sb, sem)
        with ExitStack() as keep:
            front(nc, k, d, dram, sb, ps, sem, keep)
            mixer(nc, k, d, dram, sb, ps, sem)
        graph(nc, k, d, dram, sb, ps, sem)
        experts(nc, k, d, dram, sb, ps, sem)


def kernel(x, src, dst, edge_weight, L0_gnn_Ws, L0_gnn_bs, L0_gnn_aw, L0_gnn_ab, L0_mix_ln1_w, L0_mix_ln1_b,
           L0_mix_Wx, L0_mix_bx, L0_mix_Wq, L0_mix_Wk, L0_mix_Wv, L0_mix_Wo, L0_mix_bo, L0_mix_ln2_w, L0_mix_ln2_b,
           L0_mix_W1, L0_mix_b1, L0_mix_W2, L0_mix_b2, L0_ffn_Wg, L0_ffn_bg, L0_ffn_W1, L0_ffn_b1, L0_ffn_W2,
           L0_ffn_b2):
    import numpy as np
    import concourse.bacc as bacc
    from concourse.bass_utils import run_bass_kernel_spmd as run

    def a(v):
        return np.ascontiguousarray(np.asarray(v))

    def flip(v):
        return np.ascontiguousarray(np.asarray(v).T)

    def column(v):
        v = np.asarray(v)
        return a(np.moveaxis(v.reshape(v.shape[:-1] + (-1, P)), -1, 0))

    gws, gaw = np.asarray(L0_gnn_Ws), np.asarray(L0_gnn_aw)
    arrays = {
        "x": a(x), "src": a(src), "dst": a(dst), "edge_weight": a(edge_weight),
        "Ws": a(gws.transpose(1, 0, 2).reshape(D, GH * GO)), "WsT": a(gws.transpose(0, 2, 1).reshape(GH * GO, D)),
        "bs": a(np.asarray(L0_gnn_bs).reshape(GH * GO)),
        "bs_c": column(np.asarray(L0_gnn_bs).reshape(GH * GO)), "bx_c": column(L0_mix_bx),
        "ln1_wc": column(L0_mix_ln1_w), "ln1_bc": column(L0_mix_ln1_b), "ln2_wc": column(L0_mix_ln2_w),
        "ln2_bc": column(L0_mix_ln2_b), "b1_c": column(L0_mix_b1), "eb1_c": column(L0_ffn_b1),
        "aw": a(gaw), "awe": a(gaw[:, 2 * GO]), "ab": a(L0_gnn_ab),
        "ln1_w": a(L0_mix_ln1_w), "ln1_b": a(L0_mix_ln1_b), "Wx": a(L0_mix_Wx), "WxT": flip(L0_mix_Wx),
        "WqT": flip(L0_mix_Wq), "WkT": flip(L0_mix_Wk), "WvT": flip(L0_mix_Wv),
        "WoT": flip(L0_mix_Wo), "bo": a(L0_mix_bo), 
        "W1T": flip(L0_mix_W1), "W2T": flip(L0_mix_W2), "b2": a(L0_mix_b2),
        "Wg": a(L0_ffn_Wg), "bg": a(L0_ffn_bg), "eW1": a(L0_ffn_W1), "eW2": a(L0_ffn_W2),
        "eb2": a(L0_ffn_b2),
    }
    nc = bacc.Bacc("TRN2", target_bir_lowering=False, num_devices=1)
    d = {n: nc.dram_tensor(f"in_{n}", v.shape, mybir.dt.from_np(v.dtype), kind="ExternalInput").ap()
         for n, v in arrays.items()}
    out = nc.dram_tensor("out_rows", (N, D), F32, kind="ExternalOutput").ap()
    build(nc, d, out)
    r = run(nc, [{f"in_{n}": v for n, v in arrays.items()}], core_ids=[0])
    return r.results[0]["out_rows"]
```

```python
from contextlib import ExitStack

import concourse.bass as bass
from concourse import mybir

F32 = mybir.dt.float32
I32 = mybir.dt.int32
BF16 = mybir.dt.bfloat16
ALU = mybir.AluOpType
ACT = mybir.ActivationFunctionType
AX = mybir.AxisListType.X
ds = bass.ds

P = 128
N = 6250
D = 256
T = -(-N // P)
LAST = N - (T - 1) * P
J = 7
G = T // J
GN = J * P
HALF = GN // 2
KC = D // P

GH, GO = 4, 64
FW = D + GH
FX = FW + GH

MH, MD = 8, 32
HID = 1024
HC = HID // P

NE, EH, TOP = 8, 512, 2
EHC = EH // P
CAP = (T + 1) * P
IDLE = NE * CAP
NOWHERE = IDLE + P
CT = (TOP * N + NE * (P - 1)) // P
TU = 8
ZS = 4
TURNS = (CT - 1) // TU
TABLE = CT + ZS - 1
assert TURNS * TU == CT - 1 and TU % ZS == 0 and G % 2 == 1

ECOUNT = 100000
EP = 125
EC = ECOUNT // EP
CB = 40
SC = CB // 2
NB = EC // CB
B = 8
CU = 2
UNIT = CU * P
UG = B // CU
CH = -(-(ECOUNT // UNIT + T) // (2 * UG)) * 2 * B
CI = CH // (2 * B)
CPP = CH // B
EPS = 1e-5
NEG = -1e30
assert T == G * J and NB * CB == EC and NB > G


def wait(eng, sem, count):
    eng.wait_ge(sem, count)
    if not isinstance(count, int):
        eng.nop(nofuse=True)


def norm_stats(nc, dve, act_go, act_done, count, src, st, mv, var, sd, r, nb):
    for j in range(J):
        nc.vector.bn_stats(st[:, j, :], src(j))
    dve.drain()
    for j in range(J):
        nc.vector.bn_aggr(mv[:, j, :], st[:, j, :])
    dve.drain()
    nc.vector.tensor_scalar(var[:, :], mv[:, :, 1], EPS, None, ALU.add).then_inc(act_go, 1)
    wait(dve, act_done, count)
    nc.vector.reciprocal(r[:, :], sd[:, :])
    dve.drain()
    return nc.vector.scalar_tensor_tensor(nb[:, :], mv[:, :, 0], -1.0, r[:, :], ALU.mult, ALU.mult)


def constants(nc, ctx, sb, sem):
    k = {}
    k["X"] = sb(ctx, "X", [P, T, D])
    k["scl"] = sb(ctx, "scl", [P, T, 4])
    k["a_src"] = sb(ctx, "a_src", [P, T, 3, GH], BF16)
    k["ident"] = sb(ctx, "ident", [P, P])
    k["ones"] = sb(ctx, "ones", [P, P])
    k["iota"] = sb(ctx, "iota", [P, P])
    k["awe"] = sb(ctx, "awe", [P, GH])
    k["tiles"] = sb(ctx, "tiles", [1, CH // CU + 4 * UG], I32)
    return k


def front(nc, k, d, dram, sb, ps, sem, keep):
    ctx = ExitStack()
    with ctx:
        X, scl, a_src, ident, ones, iota = (k[n] for n in ("X", "scl", "a_src", "ident", "ones", "iota"))
        order = sb(keep, "order", [EP, EC], I32)
        rec = sb(keep, "rec", [EP, EC, 4])
        tile_f = sb(keep, "tile_f", [EP, EC])
        carry = sb(keep, "carry", [EP, T])
        kmax = sb(keep, "kmax", [P, D])
        stage_i = sb(keep, "stage_i", [EP, 2, SC], I32)
        stage_r = sb(keep, "stage_r", [EP, 2, SC, 4])
        k.update(order=order, rec=rec, tile_f=tile_f, carry=carry, kmax=kmax, stage_i=stage_i, stage_r=stage_r)
        k["E"] = E = sb(keep, "E", [EP, T, CB])
        k["S"] = S = sb(keep, "S", [EP, T, CB])
        k["seg"] = seg = sb(keep, "seg", [EP, T, CB], mybir.dt.bfloat16)
        k["pos"] = sb(keep, "pos", [EP, CB])
        k["pos_i"] = sb(keep, "pos_i", [EP, 3, CB], I32)
        k["eq0"] = sb(keep, "eq0", [EP, T])
        src_i = sb(ctx, "src_i", [EP, EC], I32)
        dst_i = sb(ctx, "dst_i", [EP, EC], I32)
        tmp_i = sb(ctx, "tmp_i", [EP, EC], I32)
        elem = sb(ctx, "elem", [EP, EC])
        junk = sb(ctx, "junk", [EP, EC])
        hist = sb(ctx, "hist", [EP, T])
        before = sb(ctx, "before", [P, P])
        nch_i = sb(ctx, "nch_i", [P, T], I32)
        nch = sb(ctx, "nch", [P, T])
        cend = sb(ctx, "cend", [P, T])
        onesT = sb(ctx, "onesT", [P, T])
        cidx_i = sb(ctx, "cidx_i", [CPP, UG], I32)
        cidx = sb(ctx, "cidx", [CPP, UG])
        ccmp = sb(ctx, "ccmp", [CPP, UG, T])
        ctile = sb(ctx, "ctile", [CPP, UG])
        ctile_i = sb(ctx, "ctile_i", [CPP, UG], I32)
        iota_i = sb(ctx, "iota_i", [P, P], I32)
        blank = sb(ctx, "blank", [P, CH, 4])
        padneg = sb(ctx, "padneg", [P, T])
        wx = sb(ctx, "wx", [P, KC, D])
        wst = sb(ctx, "wst", [P, KC, D])
        wfe = sb(ctx, "wfe", [P, KC, FX])
        wqk = sb(ctx, "wqk", [P, KC, 2 * D])
        bdqk = sb(ctx, "bdqk", [P, 2, P])
        bdaw = sb(ctx, "bdaw", [P, KC, 2 * GH])
        bcol = sb(ctx, "bcol", [P, 2, KC])
        bbc = sb(ctx, "bbc", [P, 2, KC, P])
        fbias = sb(ctx, "fbias", [P, FX])
        abias = sb(ctx, "abias", [P, GH])
        qkbias = sb(ctx, "qkbias", [P, 2 * D])
        ln1 = sb(ctx, "ln1", [P, 2, KC])
        st = sb(ctx, "st", [P, J, 6])
        mv = sb(ctx, "mv", [P, J, 2])
        var = sb(ctx, "var", [P, J])
        sd = sb(ctx, "sd", [P, J])
        r = sb(ctx, "r", [P, 2, J])
        nb = sb(ctx, "nb", [P, 2, J])
        tmpj = sb(ctx, "tmpj", [P, J])
        xn = sb(ctx, "xn", [P, J, D])
        z = sb(ctx, "z", [P, J, D])
        xnT = sb(ctx, "xnT", [P, J, D])
        lT = sb(ctx, "lT", [P, J, D])
        fe = sb(ctx, "fe", [P, J, FX])
        qk = sb(ctx, "qk", [P, J, 2 * D])
        gmax = sb(ctx, "gmax", [P, D])
        part = sb(ctx, "part", [P, J, GH], BF16)
        rest = sb(ctx, "rest", [P, J, GH])
        qs = sb(ctx, "qs", [P, 2, J * MH])
        pt = [ps(ctx, f"f_pt{i}", [P, 512]) for i in range(2)]
        pf = [ps(ctx, f"f_pf{i}", [P, 512]) for i in range(2)]
        pq = [ps(ctx, f"f_pq{i}", [P, 512]) for i in range(2)]
        pc = ps(ctx, "f_pc", [P, 512])
        pb = ps(ctx, "f_pb", [P, 512])

        x_in, edges_in, weights_in = sem("x_in"), sem("edges_in"), sem("weights_in")
        consts_made, blocks_made, x_cleared = sem("consts_made"), sem("blocks_made"), sem("x_cleared")
        hist_done, counts_done, bases_done = sem("hist_done"), sem("counts_done"), sem("bases_done")
        sorted_ = k["sorted"] = sem("sorted_")
        scattered = k["scattered"] = [sem("scattered0"), sem("scattered1")]
        staged = k["staged"] = sem("staged")
        blank_made, blank_out = sem("blank_made"), sem("blank_out")
        ctile_made, ctile_out, tiles_in = sem("ctile_made"), sem("ctile_out"), sem("tiles_in")
        bias_made, folded, fold_kept = sem("bias_made"), sem("folded"), sem("fold_kept")
        var_go, sd_done, stats_go, xn_done, z_done = (sem(s) for s in ("var_go", "sd_done", "stats_go", "xn_done", "z_done"))
        turned, turned_kept, fe_prod, fe_kept = (sem(s) for s in ("turned", "turned_kept", "fe_prod", "fe_kept"))
        qk_prod, qk_kept, qsub, qexp, rows_ready = (sem(s) for s in ("qk_prod", "qk_kept", "qsub", "qexp", "rows_ready"))
        rows_out, rows_free = sem("rows_out"), sem("rows_free")
        k["rows_out"] = rows_out

        block = ctx.enter_context(nc.Block())

        @block.sync
        def _(sp):
            for tile, name in ((src_i, "src"), (dst_i, "dst"), (elem, "edge_weight")):
                sp.dma_start(tile[:, :], d[name].rearrange("(p c) -> p c", p=EP)).then_inc(edges_in, 16)
            sp.wait_ge(x_cleared, 1)
            sp.dma_start(X[:, 0:T - 1, :], d["x"][0:(T - 1) * P, :].rearrange("(t p) c -> p t c", p=P)).then_inc(x_in, 16)
            sp.dma_start(X[0:LAST, T - 1, :], d["x"][(T - 1) * P:N, :]).then_inc(x_in, 16)
            sp.wait_ge(ctile_made, 1)
            sp.dma_start(dram["ctile"].rearrange("(p b) -> p b", b=UG), ctile_i[:, :]).then_inc(ctile_out, 16)
            sp.wait_ge(ctile_out, 16)
            sp.dma_start(k["tiles"][0:1, UG:UG + CH // CU], dram["ctile"].unsqueeze(0)).then_inc(tiles_in, 16)
            sp.sem_inc(rows_free, 1)
            with sp.Fori(0, G) as g:
                wait(sp, rows_ready, g + 1)
                sp.dma_start(dram["feat"][ds(g * GN, GN), :].rearrange("(j p) f -> p j f", p=P),
                             fe[:, :, 0:FW]).then_inc(rows_out, 16)
                sp.dma_start(dram["qk"][ds(g * GN, GN), :].rearrange("(j p) f -> p j f", p=P),
                             qk[:, :, :]).then_inc(rows_out, 16)
                wait(sp, rows_out, g * 32 + 32)
                sp.sem_inc(rows_free, 1)
            sp.wait_ge(tiles_in, 16)
            sp.wait_ge(blank_out, 16)

        @block.gpsimd
        def _(pool):
            nc.gpsimd.iota(iota_i[:, :], pattern=[[1, P]], base=0, channel_multiplier=0).then_inc(consts_made, 1)
            nc.gpsimd.iota(cidx_i[:, :], pattern=[[1, UG]], base=0, channel_multiplier=UG).then_inc(consts_made, 1)
            nc.gpsimd.memset(before[:, :], 1.0).then_inc(consts_made, 1)
            nc.gpsimd.memset(ones[:, :], 1.0).then_inc(consts_made, 1)
            nc.gpsimd.memset(ident[:, :], 0.0).then_inc(consts_made, 1)
            nc.gpsimd.memset(padneg[:, :], 0.0).then_inc(consts_made, 1)
            nc.gpsimd.memset(onesT[:, :], 1.0).then_inc(consts_made, 1)
            pool.wait_ge(consts_made, 7)
            nc.gpsimd.affine_select(out=before[:, :], in_=before[:, :], compare_op=ALU.is_gt, fill=0.0,
                                    base=0, pattern=[[1, P]], channel_multiplier=-1).then_inc(consts_made, 1)
            nc.gpsimd.affine_select(out=ident[:, :], in_=ident[:, :], compare_op=ALU.not_equal, fill=1.0,
                                    base=0, pattern=[[-1, P]], channel_multiplier=1).then_inc(consts_made, 1)
            nc.gpsimd.affine_select(out=padneg[:, T - 1:T], in_=padneg[:, T - 1:T], compare_op=ALU.is_gt, fill=NEG,
                                    base=LAST, pattern=[[0, 1]], channel_multiplier=-1).then_inc(consts_made, 1)
            nc.gpsimd.memset(blank[:, :, :], 0.0).then_inc(blank_made, 1)
            pool.wait_ge(blank_made, 1)
            nc.gpsimd.memset(blank[:, :, 1], -1.0).then_inc(blank_made, 1)
            nc.gpsimd.memset(rec[:, :, 3], 0.0).then_inc(consts_made, 1)
            pool.wait_ge(blank_made, 2)
            pool.dma_start(dram["rec"].rearrange("(p c) f -> p c f", p=P), blank[:, :, :]).then_inc(blank_out, 16)
            pool.wait_ge(consts_made, 11)
            pool.wait_ge(blank_out, 16)
            scatter(nc, pool, k, dram, 0, True)
            with pool.Fori(1, G) as b:
                scatter(nc, pool, k, dram, b, False)

        @block.scalar
        def _(act):
            act.wait_ge(blocks_made, 2)
            loads = [(wx, "Wx"), (wst, "WsT")]
            for tile, name in loads:
                act.dma_start(tile[:, :, :], d[name].rearrange("(k p) n -> p k n", p=P)).then_inc(weights_in, 16)
            act.dma_start(wfe[:, :, 0:D], d["Ws"].rearrange("(k p) n -> p k n", p=P)).then_inc(weights_in, 16)
            for i, name in enumerate(("WqT", "WkT")):
                for h in range(P // MD):
                    act.dma_start(bdqk[h * MD:(h + 1) * MD, i, h * MD:(h + 1) * MD], d[name]).then_inc(weights_in, 16)
            for h in range(GH):
                p0 = h % 2 * GO
                for i, c0 in ((0, GO), (1, 0)):
                    act.dma_start(bdaw[p0:p0 + GO, h // 2, i * GH + h:i * GH + h + 1],
                                  d["aw"][h, c0:c0 + GO].unsqueeze(1)).then_inc(weights_in, 16)
            act.dma_start(bcol[:, 0, :], d["bx_c"]).then_inc(weights_in, 16)
            act.dma_start(bcol[:, 1, :], d["bs_c"]).then_inc(weights_in, 16)
            act.dma_start(fbias[:, 0:D], d["bs"].partition_broadcast(P)).then_inc(weights_in, 16)
            act.dma_start(abias[:, :], d["ab"].partition_broadcast(P)).then_inc(weights_in, 16)
            act.dma_start(k["awe"][:, :], d["awe"].partition_broadcast(P)).then_inc(weights_in, 16)
            act.dma_start(ln1[:, 0, :], d["ln1_wc"]).then_inc(weights_in, 16)
            act.dma_start(ln1[:, 1, :], d["ln1_bc"]).then_inc(weights_in, 16)
            assert NW == 3 + 2 * (P // MD) + 2 * GH + 7
            act.wait_ge(fold_kept, FOLDS)
            act.wait_ge(x_in, 32)
            with act.Fori(0, G) as g:
                for i in range(2):
                    wait(act, var_go, 2 * g + i + 1)
                    nc.scalar.activation(sd[:, :], var[:, :], ACT.Sqrt).then_inc(sd_done, 1)
                    wait(act, stats_go, 2 * g + i + 1)
                    for j in range(J):
                        if i == 0:
                            nc.scalar.activation(xn[:, j, :], X[:, ds(g * J + j, 1), :].rearrange("p a c -> p (a c)"),
                                                 ACT.Identity, bias=nb[:, 0, j:j + 1],
                                                 scale=r[:, 0, j:j + 1]).then_inc(xn_done, 1)
                        else:
                            nc.scalar.activation(z[:, j, :], xn[:, j, :], ACT.Identity, bias=nb[:, 1, j:j + 1],
                                                 scale=r[:, 1, j:j + 1]).then_inc(z_done, 1)
                for j in range(J):
                    wait(act, turned, g * J + j + 1)
                    nc.scalar.copy(xnT[:, j, :], pt[j % 2][:, 0:D])
                    for c in range(KC):
                        last = nc.scalar.activation(lT[:, j, c * P:(c + 1) * P], pt[j % 2][:, D + c * P:D + (c + 1) * P],
                                                    ACT.Identity, bias=ln1[:, 1, c:c + 1], scale=ln1[:, 0, c:c + 1])
                    last.then_inc(turned_kept, 1)
                wait(act, qsub, g + 1)
                nc.scalar.activation(qk[:, :, 0:D], qk[:, :, 0:D], ACT.Exp).then_inc(qexp, 1)

        @block.tensor
        def _(pe):
            pe.wait_ge(consts_made, 10)
            pe.wait_ge(hist_done, 1)
            nc.tensor.matmul(pc[:, 0:T], before[0:EP, :], hist[:, :], start=True, stop=True)
            nc.tensor.matmul(pc[:, 64:64 + T], ones[0:EP, :], hist[:, :], start=True, stop=True).then_inc(counts_done, 1)
            pe.wait_ge(weights_in, NW * 16)
            for c2 in range(KC):
                for i in range(2):
                    for c in range(KC):
                        last = nc.tensor.matmul(pq[c2][:, i * D + c * P:i * D + (c + 1) * P],
                                                wx[:, c, c2 * P:(c2 + 1) * P], bdqk[:, i, :], start=True, stop=True)
            last.then_inc(folded, 1)
            for c2 in range(KC):
                for c in range(KC):
                    last = nc.tensor.matmul(pb[:, c2 * 16:c2 * 16 + 2 * GH], wst[:, c, c2 * P:(c2 + 1) * P],
                                            bdaw[:, c, :], start=(c == 0), stop=(c == KC - 1))
            pe.wait_ge(bias_made, 1)
            for c in range(KC):
                nc.tensor.matmul(pb[:, 64:64 + 2 * GH], bbc[:, 1, c, :], bdaw[:, c, :], start=(c == 0), stop=(c == KC - 1))
            for i in range(2):
                for c in range(KC):
                    last = nc.tensor.matmul(pf[0][:, i * D + c * P:i * D + (c + 1) * P], bbc[:, 0, c, :],
                                            bdqk[:, i, :], start=True, stop=True)
            last.then_inc(folded, 1)
            pe.wait_ge(fold_kept, FOLDS)
            pe.sem_inc(turned_kept, 1)
            pe.sem_inc(fe_kept, 1)
            pe.sem_inc(qk_kept, 1)
            with pe.Fori(0, G) as g:
                for j in range(J):
                    if j == 0:
                        wait(pe, z_done, g * J + J)
                    wait(pe, turned_kept, g * J + max(j - 1, 0) + 1)
                    for c in range(KC):
                        nc.tensor.transpose(pt[j % 2][:, c * P:(c + 1) * P], xn[:, j, c * P:(c + 1) * P], ident[:, :])
                    for c in range(KC):
                        last = nc.tensor.transpose(pt[j % 2][:, D + c * P:D + (c + 1) * P], z[:, j, c * P:(c + 1) * P],
                                                   ident[:, :])
                    last.then_inc(turned, 1)
                for j in range(J):
                    wait(pe, turned_kept, g * J + j + 2)
                    wait(pe, fe_kept, g * J + max(j - 1, 0) + 1)
                    for c in range(KC):
                        last = nc.tensor.matmul(pf[j % 2][:, 0:FX], xnT[:, j, c * P:(c + 1) * P], wfe[:, c, :],
                                                start=(c == 0), stop=(c == KC - 1))
                    last.then_inc(fe_prod, 1)
                    wait(pe, qk_kept, g * J + max(j - 1, 0) + 1)
                    for c in range(KC):
                        last = nc.tensor.matmul(pq[j % 2][:, :], lT[:, j, c * P:(c + 1) * P], wqk[:, c, :],
                                                start=(c == 0), stop=(c == KC - 1))
                    last.then_inc(qk_prod, 1)

        @block.vector
        def _(dve):
            nc.vector.memset(bdqk[:, :, :], 0.0).then_inc(blocks_made, 1)
            nc.vector.memset(bdaw[:, :, :], 0.0).then_inc(blocks_made, 1)
            nc.vector.memset(X[:, T - 1, :], 0.0).then_inc(x_cleared, 1)
            nc.vector.memset(kmax[:, :], NEG)
            nc.vector.memset(seg[:, :, :], 1.0)
            nc.vector.memset(k["tiles"][0:1, 0:UG], 0)
            nc.vector.memset(k["tiles"][0:1, UG + CH // CU:], 0)
            dve.drain()
            nc.vector.memset(seg[:, :, 0], 0.0)
            dve.wait_ge(edges_in, 48)
            nc.vector.tensor_scalar(tmp_i[:, :], src_i[:, :], 7, None, ALU.logical_shift_right)
            dve.wait_ge(consts_made, 10)
            nc.vector.tensor_copy(iota[:, :], iota_i[:, :])
            nc.vector.tensor_copy(cidx[:, :], cidx_i[:, :])
            dve.drain()
            nc.vector.tensor_copy(tile_f[:, :], tmp_i[:, :])
            dve.drain()
            for t in range(T):
                nc.vector.tensor_scalar(junk[:, :], tile_f[:, :], float(t), 0.0, ALU.is_equal, ALU.add,
                                        accum_out=hist[:, t:t + 1])
                dve.drain()
            nc.vector.tensor_scalar(tmp_i[:, :], src_i[:, :], P - 1, None, ALU.bitwise_and).then_inc(hist_done, 1)
            dve.wait_ge(counts_done, 1)
            nc.vector.tensor_scalar(nch_i[:, :], pc[:, 64:64 + T], float(UNIT - 1), None, ALU.add)
            dve.drain()
            nc.vector.tensor_scalar(nch_i[:, :], nch_i[:, :], UNIT.bit_length() - 1, None, ALU.logical_shift_right)
            dve.drain()
            nc.vector.tensor_copy(nch[:, :], nch_i[:, :])
            nc.vector.tensor_copy(rec[:, :, 1], tmp_i[:, :])
            nc.vector.tensor_copy(rec[:, :, 0], dst_i[:, :])
            nc.vector.tensor_copy(rec[:, :, 2], elem[:, :])
            dve.drain()
            nc.vector.tensor_tensor_scan(cend[:, :], onesT[:, :], nch[:, :], 0.0, ALU.mult, ALU.add)
            dve.drain()
            nc.vector.tensor_tensor(nch[:, :], cend[:, :], nch[:, :], ALU.subtract)
            nc.vector.tensor_tensor(ccmp[:, :, :], cend[0:CPP, :].unsqueeze(1).broadcast_to([CPP, UG, T]),
                                    cidx[:, :].unsqueeze(2).broadcast_to([CPP, UG, T]), ALU.is_le)
            dve.drain()
            nc.vector.tensor_scalar(nch[:, :], nch[:, :], float(UNIT), -1.0, ALU.mult, ALU.add)
            nc.vector.tensor_reduce(ctile[:, :], ccmp[:, :, :], AX, ALU.add)
            dve.drain()
            nc.vector.tensor_tensor(carry[:, :], pc[0:EP, 0:T], nch[0:EP, :], ALU.add)
            nc.vector.tensor_scalar(ctile_i[:, :], ctile[:, :], float(T - 1), None, ALU.min).then_inc(ctile_made, 1)
            dve.wait_ge(weights_in, NW * 16)
            for i in range(2):
                for c in range(KC):
                    last = nc.vector.tensor_scalar(bbc[:, i, c, :], ones[:, :], bcol[:, i, c:c + 1], None, ALU.mult)
            last.then_inc(bias_made, 1)
            dve.wait_ge(folded, 2)
            for c2 in range(KC):
                nc.vector.tensor_copy(wqk[:, c2, :], pq[c2][:, :])
                nc.vector.tensor_copy(wfe[:, c2, D:FX], pb[:, c2 * 16:c2 * 16 + 2 * GH])
            nc.vector.tensor_copy(fbias[:, D:FW], pb[:, 64:64 + GH])
            nc.vector.tensor_tensor(fbias[:, FW:FX], pb[:, 64 + GH:64 + 2 * GH], abias[:, :], ALU.add)
            nc.vector.tensor_copy(qkbias[:, :], pf[0][:, :]).then_inc(fold_kept, FOLDS)
            dve.wait_ge(x_in, 32)
            with dve.Fori(0, G) as g:
                place_edges(nc, dve, k, iota, g)
                norm_stats(nc, dve, var_go, sd_done, 2 * g + 1,
                           lambda j: X[:, ds(g * J + j, 1), :].rearrange("p a c -> p (a c)"),
                           st, mv, var, sd, r[:, 0, :], nb[:, 0, :]).then_inc(stats_go, 1)
                wait(dve, xn_done, g * J + J)
                norm_stats(nc, dve, var_go, sd_done, 2 * g + 2, lambda j: xn[:, j, :],
                           st, mv, var, sd, r[:, 1, :], nb[:, 1, :]).then_inc(stats_go, 1)
                nc.vector.tensor_tensor(tmpj[:, :], nb[:, 0, :], r[:, 1, :], ALU.mult)
                nc.vector.tensor_copy(scl[:, ds(g * J, J), 0], r[:, 0, :])
                nc.vector.tensor_copy(scl[:, ds(g * J, J), 1], nb[:, 0, :])
                nc.vector.tensor_tensor(scl[:, ds(g * J, J), 2], r[:, 0, :], r[:, 1, :], ALU.mult)
                dve.drain()
                nc.vector.tensor_tensor(scl[:, ds(g * J, J), 3], tmpj[:, :], nb[:, 1, :], ALU.add)
                wait(dve, rows_free, g + 1)
                for j in range(J):
                    wait(dve, fe_prod, g * J + j + 1)
                    nc.vector.tensor_tensor(fe[:, j, :], pf[j % 2][:, 0:FX], fbias[:, :], ALU.add).then_inc(fe_kept, 1)
                    wait(dve, qk_prod, g * J + j + 1)
                    nc.vector.scalar_tensor_tensor(out=qk[:, j, :], in0=pq[j % 2][:, :],
                                                   scalar=padneg[:, ds(g * J + j, 1)], in1=qkbias[:, :],
                                                   op0=ALU.add, op1=ALU.add).then_inc(qk_kept, 1)
                dve.drain()
                nc.vector.tensor_copy(part[:, :, :], fe[:, :, FW:FX])
                nc.vector.tensor_copy(rest[:, :, :], fe[:, :, FW:FX])
                dve.drain()
                for n in range(3):
                    nc.vector.tensor_copy(a_src[:, ds(g * J, J), n, :], part[:, :, :])
                    if n < 2:
                        nc.vector.tensor_tensor(rest[:, :, :], rest[:, :, :], part[:, :, :], ALU.subtract)
                        dve.drain()
                        nc.vector.tensor_copy(part[:, :, :], rest[:, :, :])
                        dve.drain()
                q4 = qk[:, :, 0:D].rearrange("p j (h s) -> p j h s", s=MD)
                nc.vector.tensor_reduce(qs[:, 0, :].rearrange("p (j h) -> p j h", h=MH), q4, AX, ALU.max)
                nc.vector.tensor_reduce(gmax[:, :], qk[:, :, D:2 * D].rearrange("p j c -> p c j"), AX, ALU.max)
                dve.drain()
                top = qs[:, 0, :].rearrange("p (j h) -> p j h", h=MH).unsqueeze(3).broadcast_to([P, J, MH, MD])
                nc.vector.tensor_tensor(q4, q4, top, ALU.subtract).then_inc(qsub, 1)
                nc.vector.tensor_tensor(kmax[:, :], kmax[:, :], gmax[:, :], ALU.max)
                wait(dve, qexp, g + 1)
                nc.vector.tensor_reduce(qs[:, 0, :].rearrange("p (j h) -> p j h", h=MH), q4, AX, ALU.add)
                dve.drain()
                nc.vector.reciprocal(qs[:, 1, :], qs[:, 0, :])
                dve.drain()
                inv = qs[:, 1, :].rearrange("p (j h) -> p j h", h=MH).unsqueeze(3).broadcast_to([P, J, MH, MD])
                nc.vector.tensor_tensor(q4, q4, inv, ALU.mult).then_inc(rows_ready, 1)


NW = 3 + 2 * (P // MD) + 2 * GH + 7
FOLDS = 1


def place_edges(nc, dve, k, iota, b):
    E, S, seg, carry, tile_f, pos, pos_i, eq0 = (k[n] for n in ("E", "S", "seg", "carry", "tile_f", "pos", "pos_i", "eq0"))
    cols = tile_f[:, ds(b * CB, CB)]
    dve.drain()
    nc.vector.tensor_tensor(E[:, :, :], cols.unsqueeze(1).broadcast_to([EP, T, CB]),
                            iota[0:EP, 0:T].unsqueeze(2).broadcast_to([EP, T, CB]), ALU.is_equal)
    dve.drain()
    nc.vector.tensor_copy(eq0[:, :], E[:, :, 0])
    dve.drain()
    nc.vector.tensor_tensor(E[:, :, 0], eq0[:, :], carry[:, :], ALU.add)
    dve.drain()
    nc.vector.tensor_tensor_scan(S[:, :, :].rearrange("p t c -> p (t c)"), seg[:, :, :].rearrange("p t c -> p (t c)"),
                                 E[:, :, :].rearrange("p t c -> p (t c)"), 0.0, ALU.mult, ALU.add)
    dve.drain()
    nc.vector.tensor_copy(carry[:, :], S[:, :, CB - 1])
    nc.vector.tensor_copy(E[:, :, 0], eq0[:, :])
    dve.drain()
    nc.vector.tensor_tensor(S[:, :, :], S[:, :, :], E[:, :, :], ALU.mult)
    dve.drain()
    nc.vector.tensor_reduce(pos[:, :], S[:, :, :].rearrange("p t c -> p c t"), AX, ALU.add)
    dve.drain()
    nc.vector.tensor_copy(pos_i[:, 0, :], pos[:, :])
    dve.drain()
    nc.vector.tensor_scalar(pos_i[:, 1, :], pos_i[:, 0, :], P - 1, None, ALU.bitwise_and)
    nc.vector.tensor_scalar(pos_i[:, 2, :], pos_i[:, 0, :], 7, None, ALU.logical_shift_right)
    dve.drain()
    nc.vector.scalar_tensor_tensor(out=k["order"][:, ds(b * CB, CB)], in0=pos_i[:, 1, :], scalar=float(CH),
                                   in1=pos_i[:, 2, :], op0=ALU.mult, op1=ALU.add).then_inc(k["sorted"], 1)


def scatter(nc, pool, k, dram, b, first):
    wait(pool, k["sorted"], b + 1)
    for slot in range(2):
        c0 = b * CB + slot * SC
        if not first:
            wait(pool, k["scattered"][slot], b * (16 * SC))
        nc.gpsimd.tensor_copy(k["stage_i"][:, slot, :], k["order"][:, ds(c0, SC)]).then_inc(k["staged"], 1)
        nc.gpsimd.tensor_copy(k["stage_r"][:, slot, :, :], k["rec"][:, ds(c0, SC), :]).then_inc(k["staged"], 1)
        wait(pool, k["staged"], b * 4 + slot * 2 + 2)
        for c in range(SC):
            nc.gpsimd.indirect_dma_start(dram["rec"], bass.IndirectOffsetOnAxis(k["stage_i"][:, slot, c:c + 1], 0),
                                         k["stage_r"][:, slot, c, :], None).then_inc(k["scattered"][slot], 16)


def mixer(nc, k, d, dram, sb, ps, sem):
    ctx = ExitStack()
    with ctx:
        X, scl, ident, ones, iota, kmax = (k[n] for n in ("X", "scl", "ident", "ones", "iota", "kmax"))
        w1 = sb(ctx, "w1", [P, KC, HID])
        w2 = sb(ctx, "w2", [P, HC, D])
        wxt = sb(ctx, "wxt", [P, KC, D])
        wot = sb(ctx, "wot", [P, KC, D])
        bdv = sb(ctx, "bdv", [P, P])
        headmask = sb(ctx, "headmask", [P, P])
        cols = sb(ctx, "cols", [P, 3, KC])
        b1c = sb(ctx, "b1c", [P, HC])
        rows = sb(ctx, "m_rows", [P, 4, D])
        M = sb(ctx, "M", [P, KC, D])
        chain = sb(ctx, "chain", [P, 3, KC, D])
        small = sb(ctx, "small", [P, 8])
        st = sb(ctx, "m_st", [P, J, 6])
        mv = sb(ctx, "m_mv", [P, J, 2])
        var = sb(ctx, "m_var", [P, J])
        sd = sb(ctx, "m_sd", [P, J])
        r = sb(ctx, "m_r", [P, J])
        nb = sb(ctx, "m_nb", [P, J])
        scs = sb(ctx, "scs", [P, J, 4])
        qin = sb(ctx, "qin", [P, J, D])
        qT = sb(ctx, "qT", [P, 2, D])
        xnb = sb(ctx, "xnb", [P, J, D])
        h = sb(ctx, "h", [P, J, D])
        z2 = sb(ctx, "z2", [P, J, D])
        yT = sb(ctx, "yT", [P, KC, GN])
        gT = sb(ctx, "gT", [P, HC, GN])
        zx = gT[:, :, :].rearrange("p a n -> p (a n)")[:, 0:J * 258].rearrange("p (j f) -> p j f", f=258)
        kin, kx = z2, h
        pk = [ps(ctx, f"m_pk{i}", [P, 512]) for i in range(2)]
        pt = [ps(ctx, f"m_pt{i}", [P, 512]) for i in range(2)]
        p1 = [ps(ctx, f"m_p1{i}", [P, 512]) for i in range(2)]
        p2 = [ps(ctx, f"m_p2{i}", [P, 512]) for i in range(2)]

        names = ("bd_made w_in kmax_turned kmax_col kdiag kmax_row k_in ksub kexp scs_made zx_made ktz_prod "
                 "cleared kl kl_turned klt kxt kxt_kept kvt kvt_kept m_prod m_kept q_in q_used q_turned qT_kept "
                 "att att_kept xn_made m_var_go m_sd_done m_stats z2_made z_turned yT_kept h1_prod g_made h2_prod "
                 "h2_kept k_used ones_made h_free")
        s = {n: sem(n) for n in names.split()}
        block = ctx.enter_context(nc.Block())

        zeros = yT[:, 0, :]

        def attend(pe, g, j):
            wait(pe, s["qT_kept"], g * J + j + 2)
            wait(pe, s["att_kept"], g * J + max(j - 1, 0) + 1)
            for c in range(KC):
                last = nc.tensor.matmul(pk[j % 2][:, 0:D], qT[:, j % 2, c * P:(c + 1) * P], M[:, c, :],
                                        start=(c == 0), stop=(c == KC - 1))
            last.then_inc(s["att"], 1)

        @block.sync
        def _(sp):
            sp.wait_ge(s["bd_made"], 1)
            n = 0
            for tile, name in ((w1, "W1T"), (w2, "W2T"), (wxt, "WxT"), (wot, "WoT")):
                sp.dma_start(tile[:, :, :], d[name].rearrange("(k p) n -> p k n", p=P)).then_inc(s["w_in"], 16)
            for i in range(P // MD):
                sp.dma_start(bdv[i * MD:(i + 1) * MD, i * MD:(i + 1) * MD], d["WvT"]).then_inc(s["w_in"], 16)
            for i, name in enumerate(("ln2_wc", "ln2_bc", "bx_c")):
                sp.dma_start(cols[:, i, :], d[name]).then_inc(s["w_in"], 16)
            sp.dma_start(b1c[:, :], d["b1_c"]).then_inc(s["w_in"], 16)
            for i, name in enumerate(("ln1_w", "ln1_b", "bo", "b2")):
                sp.dma_start(rows[:, i, :], d[name].partition_broadcast(P)).then_inc(s["w_in"], 16)
            sp.sem_inc(s["k_used"], 1)
            sp.sem_inc(s["q_turned"], 1)
            with sp.Fori(0, G) as g:
                wait(sp, s["k_used"], g + 1)
                sp.dma_start(kin[:, :, :], dram["qk"][ds(g * GN, GN), D:2 * D].rearrange("(j p) f -> p j f", p=P))\
                    .then_inc(s["k_in"], 16)
            with sp.Fori(0, G) as g:
                wait(sp, s["q_turned"], g * J + 1)
                sp.dma_start(qin[:, :, :], dram["qk"][ds(g * GN, GN), 0:D].rearrange("(j p) f -> p j f", p=P))\
                    .then_inc(s["q_in"], 16)

        @block.gpsimd
        def _(pool):
            with pool.Fori(G, NB) as b:
                scatter(nc, pool, k, dram, b, False)
            for slot in range(2):
                pool.wait_ge(k["scattered"][slot], NB * 16 * SC)

        @block.scalar
        def _(act):
            with act.Fori(0, G) as g:
                wait(act, s["ksub"], g + 1)
                nc.scalar.activation(kx[:, :, :], kx[:, :, :], ACT.Exp).then_inc(s["kexp"], 1)
                wait(act, s["scs_made"], g + 1)
                for j in range(J):
                    last = nc.scalar.activation(zx[:, j, 0:D], X[:, ds(g * J + j, 1), :].rearrange("p a c -> p (a c)"),
                                                ACT.Identity, bias=scs[:, j, 3:4], scale=scs[:, j, 2:3])
                last.then_inc(s["zx_made"], 1)
            with act.Fori(0, G) as g:
                wait(act, s["scs_made"], G + g + 1)
                for j in range(J):
                    last = nc.scalar.activation(xnb[:, j, :], X[:, ds(g * J + j, 1), :].rearrange("p a c -> p (a c)"),
                                                ACT.Identity, bias=scs[:, j, 1:2], scale=scs[:, j, 0:1])
                last.then_inc(s["xn_made"], 1)
                for j in range(J):
                    wait(act, s["q_turned"], g * J + j + 2)
                    if j < 2:
                        wait(act, s["att"], g * J + (0 if j == 0 else j - 1) + 1)
                    else:
                        wait(act, s["att"], g * J + j)
                    nc.scalar.copy(qT[:, j % 2, :], pt[j % 2][:, 0:D]).then_inc(s["qT_kept"], 1)
                wait(act, s["m_var_go"], g + 1)
                nc.scalar.activation(sd[:, :], var[:, :], ACT.Sqrt).then_inc(s["m_sd_done"], 1)
                wait(act, s["m_stats"], g + 1)
                for j in range(J):
                    nc.scalar.activation(z2[:, j, :], h[:, j, :], ACT.Identity, bias=nb[:, j:j + 1],
                                         scale=r[:, j:j + 1]).then_inc(s["z2_made"], 1)
                for j in range(J):
                    wait(act, s["z_turned"], g * J + j + 1)
                    for c in range(KC):
                        last = nc.scalar.activation(yT[:, c, j * P:(j + 1) * P], pt[j % 2][:, c * P:(c + 1) * P],
                                                    ACT.Identity, bias=cols[:, 1, c:c + 1], scale=cols[:, 0, c:c + 1])
                    last.then_inc(s["yT_kept"], 1)
                for n in range(2 * HC):
                    hc, half = n // 2, n % 2
                    wait(act, s["h1_prod"], g * 2 * HC + n + 1)
                    nc.scalar.activation(gT[:, hc, half * HALF:(half + 1) * HALF], p1[half][:, 0:HALF], ACT.Gelu,
                                         bias=b1c[:, hc:hc + 1]).then_inc(s["g_made"], 1)

        @block.tensor
        def _(pe):
            for c in range(KC):
                last = nc.tensor.transpose(pt[0][:, c * P:(c + 1) * P], kmax[:, c * P:(c + 1) * P], ident[:, :])
            last.then_inc(s["kmax_turned"], 1)
            pe.wait_ge(s["kdiag"], 1)
            nc.tensor.matmul(pt[1][:, 0:D], ones[:, :], chain[:, 0, 0, :], start=True, stop=True).then_inc(s["kmax_row"], 1)
            pe.wait_ge(s["bd_made"], 1)
            for c in range(KC):
                nc.tensor.matmul(pk[c][:, 0:D + 2], zeros[:, 0:P], zeros[:, 0:D + 2], start=True, stop=False, skip_group_check=True)
            with pe.Fori(0, G) as g:
                wait(pe, s["kexp"], g + 1)
                wait(pe, s["zx_made"], g + 1)
                for j in range(J):
                    for c in range(KC):
                        last = nc.tensor.matmul(pk[c][:, 0:D + 2], kx[:, j, c * P:(c + 1) * P], zx[:, j, :],
                                                start=False, stop=False, skip_group_check=True)
                last.then_inc(s["ktz_prod"], 1)
            for c in range(KC):
                last = nc.tensor.matmul(pk[c][:, 0:D + 2], zeros[:, 0:P], zeros[:, 0:D + 2], start=False, stop=True,
                                        skip_group_check=True)
            last.then_inc(s["ktz_prod"], 1)
            pe.wait_ge(s["kl"], 1)
            for kk in range(KC):
                for c in range(KC):
                    last = nc.tensor.transpose(pt[0][:, kk * D + c * P:kk * D + (c + 1) * P],
                                               chain[:, 0, c, kk * P:(kk + 1) * P], ident[:, :])
            last.then_inc(s["kl_turned"], 1)
            pe.wait_ge(s["w_in"], 16 * 16)
            pe.wait_ge(s["klt"], 1)
            for c in range(KC):
                for kk in range(KC):
                    last = nc.tensor.matmul(pt[1][:, c * P:(c + 1) * P], wxt[:, kk, c * P:(c + 1) * P],
                                            chain[:, 1, kk, c * P:(c + 1) * P], start=(kk == 0), stop=(kk == KC - 1))
            last.then_inc(s["kxt"], 1)
            pe.wait_ge(s["kxt_kept"], 1)
            last = nc.tensor.matmul(pt[0][:, 0:D], bdv[:, :], chain[:, 2, 0, :], start=True, stop=True)
            last.then_inc(s["kvt"], 1)
            pe.wait_ge(s["kvt_kept"], 1)
            for c in range(KC):
                last = nc.tensor.matmul(pt[1][:, c * D:(c + 1) * D], chain[:, 0, 0, c * P:(c + 1) * P], wot[:, c, :],
                                        start=True, stop=True)
            last.then_inc(s["m_prod"], 1)
            pe.wait_ge(s["m_kept"], 1)
            pe.sem_inc(s["att"], 1)
            pe.sem_inc(s["att_kept"], 1)
            pe.sem_inc(s["g_made"], 2)
            pe.sem_inc(s["h2_kept"], 1)
            with pe.Fori(0, G) as g:
                wait(pe, s["q_in"], g * 16 + 16)
                for j in range(J):
                    wait(pe, s["qT_kept"], g * J + max(j - 1, 0) + 1)
                    for c in range(KC):
                        last = nc.tensor.transpose(pt[j % 2][:, c * P:(c + 1) * P], qin[:, j, c * P:(c + 1) * P], ident[:, :])
                    last.then_inc(s["q_turned"], 1)
                    if j:
                        attend(pe, g, j - 1)
                attend(pe, g, J - 1)
                wait(pe, s["z2_made"], g * J + J)
                for j in range(J):
                    wait(pe, s["yT_kept"], g * J + max(j - 1, 0) + 1)
                    for c in range(KC):
                        last = nc.tensor.transpose(pt[j % 2][:, c * P:(c + 1) * P], z2[:, j, c * P:(c + 1) * P], ident[:, :])
                    last.then_inc(s["z_turned"], 1)
                wait(pe, s["yT_kept"], g * J + J + 1)
                for n in range(2 * HC):
                    hc, half = n // 2, n % 2
                    wait(pe, s["g_made"], g * 2 * HC + n + 1)
                    for c in range(KC):
                        last = nc.tensor.matmul(p1[half][:, 0:HALF], w1[:, c, hc * P:(hc + 1) * P],
                                                yT[:, c, half * HALF:(half + 1) * HALF],
                                                start=(c == 0), stop=(c == KC - 1))
                    last.then_inc(s["h1_prod"], 1)
                wait(pe, s["g_made"], g * 2 * HC + 2 * HC + 2)
                for j in range(J):
                    wait(pe, s["h2_kept"], g * J + max(j - 1, 0) + 1)
                    for hc in range(HC):
                        last = nc.tensor.matmul(p2[j % 2][:, 0:D], gT[:, hc, j * P:(j + 1) * P], w2[:, hc, :],
                                                start=(hc == 0), stop=(hc == HC - 1))
                    last.then_inc(s["h2_prod"], 1)

        @block.vector
        def _(dve):
            nc.vector.memset(bdv[:, :], 0.0)
            nc.vector.memset(headmask[:, :], 0.0)
            nc.vector.memset(zx[:, :, D:D + 2], 1.0)
            nc.vector.memset(zeros[:, 0:D + 2], 0.0)
            dve.drain()
            for i in range(P // MD):
                last = nc.vector.memset(headmask[i * MD:(i + 1) * MD, i * MD:(i + 1) * MD], 1.0)
            last.then_inc(s["bd_made"], 1)
            dve.sem_inc(s["qT_kept"], 1)
            dve.sem_inc(s["yT_kept"], 1)
            dve.wait_ge(s["kmax_turned"], 1)
            nc.vector.tensor_reduce(small[:, 0:KC], pt[0][:, 0:D].rearrange("p (k q) -> p k q", k=KC), AX, ALU.max)
            dve.drain()
            for c in range(KC):
                last = nc.vector.tensor_scalar(chain[:, 0, 0, c * P:(c + 1) * P], ident[:, :], small[:, c:c + 1], None, ALU.mult)
            last.then_inc(s["kdiag"], 1)
            dve.wait_ge(s["kmax_row"], 1)
            nc.vector.tensor_copy(chain[:, 1, 0, :], pt[1][:, 0:D])
            dve.drain()
            krow = chain[:, 1, 0, :].unsqueeze(1).broadcast_to([P, J, D])
            dve.sem_inc(s["ktz_prod"], 1)
            with dve.Fori(0, G) as g:
                wait(dve, s["ktz_prod"], g + 1)
                nc.vector.tensor_copy(scs[:, :, :], scl[:, ds(g * J, J), :]).then_inc(s["scs_made"], 1)
                wait(dve, s["k_in"], g * 16 + 16)
                nc.vector.tensor_tensor(kx[:, :, :], kin[:, :, :], krow, ALU.subtract).then_inc(s["ksub"], 1)
                wait(dve, s["ksub"], g + 1)
                dve.sem_inc(s["k_used"], 1)
                place_edges(nc, dve, k, iota, g + G)
            dve.wait_ge(s["ktz_prod"], G + 2)
            dve.wait_ge(s["w_in"], 16 * 16)
            for c in range(KC):
                nc.vector.reciprocal(small[:, 2 + c:3 + c], pk[c][:, D:D + 1])
            dve.drain()
            for c in range(KC):
                nc.vector.scalar_tensor_tensor(out=chain[:, 0, c, :], in0=pk[c][:, 0:D], scalar=small[:, 2 + c:3 + c],
                                               in1=rows[:, 0, :], op0=ALU.mult, op1=ALU.mult)
            dve.drain()
            nc.vector.tensor_tensor(chain[:, 0, :, :], chain[:, 0, :, :],
                                    rows[:, 1, :].unsqueeze(1).broadcast_to([P, KC, D]), ALU.add).then_inc(s["kl"], 1)
            dve.wait_ge(s["kl_turned"], 1)
            nc.vector.tensor_copy(chain[:, 1, :, :], pt[0][:, :].rearrange("p (k c) -> p k c", k=KC)).then_inc(s["klt"], 1)
            dve.wait_ge(s["kxt"], 1)
            for c in range(KC):
                last = nc.vector.scalar_tensor_tensor(out=chain[:, 2, 0, c * P:(c + 1) * P], in0=pt[1][:, c * P:(c + 1) * P],
                                                      scalar=cols[:, 2, c:c + 1], in1=headmask[:, :],
                                                      op0=ALU.add, op1=ALU.mult)
            last.then_inc(s["kxt_kept"], 1)
            dve.wait_ge(s["kvt"], 1)
            nc.vector.tensor_copy(chain[:, 0, 0, :], pt[0][:, 0:D]).then_inc(s["kvt_kept"], 1)
            dve.wait_ge(s["m_prod"], 1)
            nc.vector.tensor_copy(M[:, :, :], pt[1][:, :].rearrange("p (k c) -> p k c", k=KC)).then_inc(s["m_kept"], 1)

            def body(g, sort):
                wait(dve, s["h_free"], g + 1)
                nc.vector.tensor_copy(scs[:, :, :], scl[:, ds(g * J, J), :]).then_inc(s["scs_made"], 1)
                wait(dve, s["xn_made"], g + 1)
                nc.vector.tensor_tensor(xnb[:, :, :], xnb[:, :, :], rows[:, 2, :].unsqueeze(1).broadcast_to([P, J, D]), ALU.add)
                dve.drain()
                for j in range(J):
                    wait(dve, s["att"], g * J + j + 2)
                    nc.vector.tensor_tensor(h[:, j, :], pk[j % 2][:, 0:D], xnb[:, j, :], ALU.add).then_inc(s["att_kept"], 1)
                dve.drain()
                norm_stats(nc, dve, s["m_var_go"], s["m_sd_done"], g + 1, lambda j: h[:, j, :],
                           st, mv, var, sd, r, nb).then_inc(s["m_stats"], 1)
                if sort:
                    place_edges(nc, dve, k, iota, g + 2 * G)
                xg = X[:, ds(g * J, J), :]
                nc.vector.tensor_tensor(xg, xg, h[:, :, :], ALU.add)
                dve.drain()
                nc.vector.tensor_tensor(xg, xg, rows[:, 3, :].unsqueeze(1).broadcast_to([P, J, D]), ALU.add)
                dve.drain()
                for j in range(J):
                    xt = X[:, ds(g * J + j, 1), :].rearrange("p a c -> p (a c)")
                    wait(dve, s["h2_prod"], g * J + j + 1)
                    nc.vector.tensor_tensor(xt, xt, p2[j % 2][:, 0:D], ALU.add).then_inc(s["h2_kept"], 1)
                dve.drain()
                dve.sem_inc(s["h_free"], 1)

            dve.sem_inc(s["h_free"], 1)
            with dve.Fori(0, NB - 2 * G) as g:
                body(g, True)
            for g in range(NB - 2 * G, G):
                body(g, False)


def graph(nc, k, d, dram, sb, ps, sem):
    ctx = ExitStack()
    with ctx:
        X, a_src, ident, iota, awe = (k[n] for n in ("X", "a_src", "ident", "iota", "awe"))
        erec = sb(ctx, "erec", [P, CH + 2 * B, 4])
        acc = sb(ctx, "acc", [P, T, FW])
        hot = sb(ctx, "hot", [P, 2, B, P])
        hotT = sb(ctx, "hotT", [P, 2, B, P], BF16)
        rows = sb(ctx, "g_rows", [P, 2, B, FW])
        wrows = sb(ctx, "wrows", [P, 2, B, FW])
        ew = sb(ctx, "ew", [P, 2, B, GH])
        pre = sb(ctx, "pre", [P, 2, B, GH])
        sc = sb(ctx, "sc", [P, 2, B, GH])
        gi = sb(ctx, "gi", [P, 2, B], I32)
        pad_i = sb(ctx, "pad_i", [P, 1])
        warm = sb(ctx, "warm", [P, 2])
        inv = sb(ctx, "g_inv", [P, J, GH])
        pT = [ps(ctx, f"g_pT{i}", [P, 512]) for i in range(2)]
        pA = [ps(ctx, f"g_pA{i}", [P, 512]) for i in range(2)]
        pO = [ps(ctx, f"g_pO{i}", [P, 512]) for i in range(UG)]
        gathered = [sem("gathered0"), sem("gathered1")]
        s = {n: sem(n) for n in ("rec_in idx_made hot_made hot_turned hotT_kept a_prod pre_made sc_made w_made "
                                 "scaled out_prod acc_done pad_made").split()}
        block = ctx.enter_context(nc.Block())

        @block.sync
        def _(sp):
            sp.dma_start(erec[:, 0:CH, :], dram["rec"].rearrange("(p c) f -> p c f", p=P)).then_inc(s["rec_in"], 16)
            sp.wait_ge(s["rec_in"], 16)

        @block.gpsimd
        def _(pool):
            nc.gpsimd.memset(pad_i[:, :], 0.0).then_inc(s["pad_made"], 1)
            pool.wait_ge(s["pad_made"], 1)
            nc.gpsimd.affine_select(out=pad_i[:, :], in_=pad_i[:, :], compare_op=ALU.is_gt, fill=1.0,
                                    base=LAST, pattern=[[0, 1]], channel_multiplier=-1).then_inc(s["pad_made"], 1)
            pool.wait_ge(s["rec_in"], 16)
            pool.sem_inc(s["scaled"], 2)
            with pool.Fori(0, CI) as i:
                for u in range(2):
                    q = i * 2 + u
                    wait(pool, s["scaled"], q + 1)
                    nc.gpsimd.tensor_copy(gi[:, u, :], erec[:, ds(q * B, B), 0]).then_inc(s["idx_made"], 1)
                    wait(pool, s["idx_made"], q + 1)
                    for b in range(B):
                        nc.gpsimd.indirect_dma_start(rows[:, u, b, :], None, dram["feat"],
                                                     bass.IndirectOffsetOnAxis(gi[:, u, b:b + 1], 0))\
                            .then_inc(gathered[u], 16)

        @block.scalar
        def _(act):
            def keep_turned(q, u):
                wait(act, s["hot_turned"], q + 1)
                for n in range(2):
                    last = nc.scalar.copy(hotT[:, u, 4 * n:4 * n + 4, :].rearrange("p b e -> p (b e)"), pT[n][:, :])
                last.then_inc(s["hotT_kept"], 1)

            keep_turned(0, 0)
            with act.Fori(0, CI) as i:
                nc.scalar.activation(warm[:, 1:2], warm[:, 0:1], ACT.Exp)
                for u in range(2):
                    q = i * 2 + u
                    wait(act, s["sc_made"], q + 1)
                    nc.scalar.activation(wrows[:, u, :, D:FW], sc[:, u, :, :], ACT.Exp).then_inc(s["w_made"], 1)
                    keep_turned(q + 1, 1 - u)

        @block.tensor
        def _(pe):
            def turn(q, u):
                wait(pe, s["hot_made"], q + 1)
                wait(pe, s["hotT_kept"], q + 1)
                for b in range(B):
                    last = nc.tensor.transpose(pT[b // 4][:, b % 4 * P:(b % 4 + 1) * P], hot[:, u, b, :], ident[:, :])
                last.then_inc(s["hot_turned"], 1)

            def source_scores(q, u, tiles):
                wait(pe, s["hotT_kept"], q + 2)
                wait(pe, s["pre_made"], q + 1)
                for b in range(B):
                    last = nc.tensor.matmul(pA[u][:, b * 3 * GH:(b + 1) * 3 * GH], hotT[:, u, b, :],
                                            a_src[:, ds(tiles[b // CU], 1), :, :].rearrange("p a n h -> p (a n h)"),
                                            start=True, stop=True)
                last.then_inc(s["a_prod"], 1)

            def load_tiles(c0, n):
                _, regs = nc.values_load_multi_w_load_instructions(
                    k["tiles"][0:1, ds(c0, n)], engines=[pe.engine], min_val=0, max_val=T - 1,
                    skip_runtime_bounds_check_because="the tile numbers are clipped where the table is made")
                return regs

            pe.sem_inc(s["hotT_kept"], 1)
            pe.sem_inc(s["pre_made"], 2)
            turn(0, 0)
            source_scores(0, 0, load_tiles(UG, UG))
            for n in range(UG):
                nc.tensor.matmul(pO[n][:, 0:FW], hot[:, 1, n, :], wrows[:, 1, n, :], start=True, stop=True)\
                    .then_inc(s["out_prod"], 1)
            with pe.Fori(0, CI) as i:
                tiles = load_tiles(i * 2 * UG + 2 * UG, 2 * UG)
                for u in range(2):
                    q = i * 2 + u
                    turn(q + 1, 1 - u)
                    wait(pe, s["scaled"], q + 3)
                    for n in range(UG):
                        if n == 1:
                            source_scores(q + 1, 1 - u, tiles[u * UG:(u + 1) * UG])
                        wait(pe, s["acc_done"], q * UG + n + 1)
                        for c in range(CU):
                            b = n * CU + c
                            last = nc.tensor.matmul(pO[n][:, 0:FW], hot[:, u, b, :], wrows[:, u, b, :],
                                                    start=(c == 0), stop=(c == CU - 1))
                        last.then_inc(s["out_prod"], 1)

        @block.vector
        def _(dve):
            def make_hot(q, u):
                nc.vector.tensor_tensor(hot[:, u, :, :], iota[:, :].unsqueeze(1).broadcast_to([P, B, P]),
                                        erec[:, ds(q * B, B), 1].unsqueeze(2).broadcast_to([P, B, P]),
                                        ALU.is_equal).then_inc(s["hot_made"], 1)

            def weight_part(q, u):
                nc.vector.tensor_tensor(ew[:, u, :, :], erec[:, ds(q * B, B), 2].unsqueeze(2).broadcast_to([P, B, GH]),
                                        awe[:, :].unsqueeze(1).broadcast_to([P, B, GH]), ALU.mult)

            def known_part(q, u):
                wait(dve, s["a_prod"], q + 1)
                nc.vector.tensor_reduce(pre[:, u, :, :],
                                        pA[u][:, 0:B * 3 * GH].rearrange("p (b n h) -> p b h n", n=3, h=GH), AX, ALU.add)
                dve.drain()
                nc.vector.tensor_tensor(pre[:, u, :, :], pre[:, u, :, :], ew[:, u, :, :], ALU.add)\
                    .then_inc(s["pre_made"], 1)

            def add_sums(q, tiles):
                for n in range(UG):
                    at = acc[:, ds(tiles[n], 1), :].rearrange("p a f -> p (a f)")
                    wait(dve, s["out_prod"], (q + 1) * UG + n + 1)
                    if n:
                        wait(dve, s["acc_done"], (q + 1) * UG + n)
                    nc.vector.tensor_tensor(at, at, pO[n][:, 0:FW], ALU.add).then_inc(s["acc_done"], 1)

            nc.vector.memset(hot[:, 1, :, :], 0.0)
            nc.vector.memset(wrows[:, 1, :, :], 0.0)
            nc.vector.memset(acc[:, :, :], 0.0)
            nc.vector.memset(erec[:, CH:, :], 0.0)
            nc.vector.memset(warm[:, :], 0.0)
            dve.drain()
            dve.wait_ge(s["pad_made"], 2)
            nc.vector.tensor_copy(acc[:, T - 1, D:FW], pad_i[:, 0:1].broadcast_to([P, GH]))
            dve.wait_ge(s["rec_in"], 16)
            make_hot(0, 0)
            weight_part(0, 0)
            dve.drain()
            known_part(0, 0)

            def load_tiles(c0, n):
                _, regs = nc.values_load_multi_w_load_instructions(
                    k["tiles"][0:1, ds(c0, n)], engines=[dve.engine], min_val=0, max_val=T - 1,
                    skip_runtime_bounds_check_because="the tile numbers are clipped where the table is made")
                return regs

            with dve.Fori(0, CI) as i:
                tiles = load_tiles(i * 2 * UG, 2 * UG)
                for u in range(2):
                    q = i * 2 + u
                    dve.drain()
                    wait(dve, gathered[u], i * (16 * B) + 16 * B)
                    nc.vector.tensor_tensor(sc[:, u, :, :], pre[:, u, :, :], rows[:, u, :, D:FW], ALU.add)
                    dve.drain()
                    nc.vector.tensor_scalar(sc[:, u, :, :], sc[:, u, :, :], 0.0, -1.0 / 20.0, ALU.max, ALU.mult)\
                        .then_inc(s["sc_made"], 1)
                    wait(dve, s["out_prod"], q * UG + UG)
                    make_hot(q + 1, 1 - u)
                    weight_part(q + 1, 1 - u)
                    wait(dve, s["w_made"], q + 1)
                    nc.vector.tensor_tensor(wrows[:, u, :, 0:D].rearrange("p b (h o) -> p b h o", o=GO),
                                            rows[:, u, :, 0:D].rearrange("p b (h o) -> p b h o", o=GO),
                                            wrows[:, u, :, D:FW].unsqueeze(3).broadcast_to([P, B, GH, GO]),
                                            ALU.mult).then_inc(s["scaled"], 1)
                    add_sums(q - 1, tiles[u * UG:(u + 1) * UG])
                    known_part(q + 1, 1 - u)
            dve.drain()
            add_sums(2 * CI - 1, load_tiles(CH // CU, UG))
            dve.drain()
            for g in range(G):
                t0 = g * J
                nc.vector.reciprocal(inv[:, :, :], acc[:, t0:t0 + J, D:FW])
                dve.drain()
                a4 = acc[:, t0:t0 + J, 0:D].rearrange("p j (h o) -> p j h o", o=GO)
                nc.vector.tensor_tensor(a4, a4, inv[:, :, :].unsqueeze(3).broadcast_to([P, J, GH, GO]), ALU.mult)
                dve.drain()
                nc.vector.tensor_tensor(X[:, t0:t0 + J, :], X[:, t0:t0 + J, :], acc[:, t0:t0 + J, 0:D], ALU.add)


def experts(nc, k, d, dram, sb, ps, sem):
    ctx = ExitStack()
    with ctx:
        hots = sb(ctx, "hots", [P, TOP, T, NE])
        pos = sb(ctx, "pos_z", [P, TOP, T])
        y_at = sb(ctx, "y_at", [P, TOP, T], I32)
        tile_row = sb(ctx, "tile_row", [1, TABLE], I32)
        tile_exp = sb(ctx, "tile_exp", [1, TABLE], I32)
        with ExitStack() as wctx:
            w = {"w1": sb(wctx, "e_w1", [P, NE, KC, EH]), "w2": sb(wctx, "e_w2", [P, NE, EHC, D]),
                 "b1": sb(wctx, "e_b1", [P, NE, EH]), "b2": sb(wctx, "e_b2", [P, NE, D])}
            route(nc, k, d, dram, sb, ps, sem, w, hots, pos, y_at, tile_row, tile_exp)
            run_tiles(nc, k, dram, sb, ps, sem, w, tile_row, tile_exp)
        combine(nc, k, dram, sb, sem, y_at)


def route(nc, k, d, dram, sb, ps, sem, w, hots, pos, y_at, tile_row, tile_exp):
    ctx = ExitStack()
    with ctx:
        X, ident, ones = k["X"], k["ident"], k["ones"]
        wg = sb(ctx, "wg", [P, KC, NE])
        bg = sb(ctx, "bg", [P, NE])
        st = sb(ctx, "e_st", [P, T, 6])
        mv = sb(ctx, "e_mv", [P, T, 2])
        var = sb(ctx, "e_var", [P, T])
        sd = sb(ctx, "e_sd", [P, T])
        r = sb(ctx, "e_r", [P, T])
        nb = sb(ctx, "e_nb", [P, T])
        z = sb(ctx, "e_z", [P, 2, J, D])
        zT = sb(ctx, "e_zT", [P, J, D])
        gate = sb(ctx, "gate", [P, J, NE])
        rank_i = sb(ctx, "rank_i", [P, NE], I32)
        rank = sb(ctx, "rank", [P, NE])
        m1 = sb(ctx, "m1", [P, J])
        eq = sb(ctx, "eq", [P, J, NE])
        mask = sb(ctx, "mask", [P, J + 1, NE])
        before = sb(ctx, "e_before", [P, P])
        region_i = sb(ctx, "region_i", [P, NE], I32)
        region = sb(ctx, "region", [P, NE])
        base = sb(ctx, "base", [P, NE])
        base_i = sb(ctx, "base_i", [P, NE], I32)
        away_i = sb(ctx, "away_i", [P, TOP, T], I32)
        away = sb(ctx, "away", [P, TOP, T])
        valid = sb(ctx, "valid", [P, 1])
        place = sb(ctx, "place", [P, J, NE])
        chosen = sb(ctx, "chosen", [P, TOP, J, NE])
        picked = sb(ctx, "picked", [P, TOP, J])
        z_at = sb(ctx, "z_at", [P, 2, TOP, J], I32)
        none = sb(ctx, "none", [P, D])
        tiles_i = sb(ctx, "tiles_i", [P, NE], I32)
        tiles = sb(ctx, "tiles_e", [P, NE])
        tend = sb(ctx, "tend", [P, NE])
        delta = sb(ctx, "delta", [P, NE])
        step = sb(ctx, "step", [P, NE])
        moved = sb(ctx, "moved", [P, TOP, T])
        onesE = sb(ctx, "onesE", [P, NE])
        tnum_i = sb(ctx, "tnum_i", [1, TABLE], I32)
        tnum = sb(ctx, "tnum", [1, TABLE])
        full = sb(ctx, "full", [1, TABLE, NE])
        texp = sb(ctx, "texp", [1, TABLE])
        trow = sb(ctx, "trow", [1, TABLE])
        pt = [ps(ctx, f"e_pt{i}", [P, 512]) for i in range(2)]
        pg = [ps(ctx, f"e_pg{i}", [P, 512]) for i in range(2)]
        pr = ps(ctx, "e_pr", [P, 512])
        s = {n: sem("e_" + n) for n in ("w_in gate_in consts var_go sd_done stats z_made z_turned zT_kept gate_prod "
                                        "mask_made rank_prod sent_free at_made none_made base_made filled").split()}
        sent = [sem("e_sent0"), sem("e_sent1")]
        block = ctx.enter_context(nc.Block())

        @block.sync
        def _(sp):
            sp.dma_start(wg[:, :, :], d["Wg"].rearrange("(k p) n -> p k n", p=P)).then_inc(s["gate_in"], 16)
            sp.dma_start(bg[:, :], d["bg"].partition_broadcast(P)).then_inc(s["gate_in"], 16)
            for e in range(NE):
                sp.dma_start(w["w1"][:, e, :, :], d["eW1"][e].rearrange("(k p) n -> p k n", p=P)).then_inc(s["w_in"], 16)
                sp.dma_start(w["w2"][:, e, :, :], d["eW2"][e].rearrange("(k p) n -> p k n", p=P)).then_inc(s["w_in"], 16)
            sp.dma_start(w["b1"][:, :, :], d["eb1"].partition_broadcast(P)).then_inc(s["w_in"], 16)
            sp.dma_start(w["b2"][:, :, :], d["eb2"].partition_broadcast(P)).then_inc(s["w_in"], 16)
            sp.wait_ge(s["none_made"], 1)
            sp.dma_start(dram["z"][IDLE:IDLE + P, :], none[:, :]).then_inc(s["filled"], 16)
            sp.wait_ge(s["base_made"], 1)
            _, ends = nc.values_load_multi_w_load_instructions(
                base_i[0:1, :], engines=[sp.engine], min_val=0, max_val=IDLE - P,
                skip_runtime_bounds_check_because="an expert's region is longer than the number of nodes")
            sp.wait_ge(s["sent_free"], G + 2)
            for e in range(NE):
                sp.dma_start(dram["z"][ds(ends[e], P), :], none[:, :]).then_inc(s["filled"], 16)
            sp.wait_ge(s["filled"], 16 * (NE + 1))
            sp.wait_ge(s["w_in"], 16 * (2 * NE + 2))

        @block.gpsimd
        def _(pool):
            nc.gpsimd.iota(rank_i[:, :], pattern=[[-1, NE]], base=NE, channel_multiplier=0).then_inc(s["consts"], 1)
            nc.gpsimd.iota(region_i[:, :], pattern=[[CAP, NE]], base=0, channel_multiplier=0).then_inc(s["consts"], 1)
            nc.gpsimd.iota(away_i[:, :, :], pattern=[[T * P, TOP], [P, T]], base=NOWHERE, channel_multiplier=1).then_inc(s["consts"], 1)
            nc.gpsimd.iota(tnum_i[:, :], pattern=[[1, TABLE]], base=0, channel_multiplier=0).then_inc(s["consts"], 1)
            nc.gpsimd.memset(before[:, :], 1.0).then_inc(s["consts"], 1)
            nc.gpsimd.memset(valid[:, :], 1.0).then_inc(s["consts"], 1)
            pool.wait_ge(s["consts"], 6)
            nc.gpsimd.affine_select(out=before[:, :], in_=before[:, :], compare_op=ALU.is_gt, fill=0.0,
                                    base=0, pattern=[[1, P]], channel_multiplier=-1).then_inc(s["consts"], 1)
            nc.gpsimd.affine_select(out=valid[:, :], in_=valid[:, :], compare_op=ALU.is_gt, fill=0.0,
                                    base=LAST, pattern=[[0, 1]], channel_multiplier=-1).then_inc(s["consts"], 1)
            pool.sem_inc(s["sent_free"], 2)

            def send(g, u):
                wait(pool, s["at_made"], g + 1)
                for j in range(J):
                    for n in range(TOP):
                        nc.gpsimd.indirect_dma_start(dram["z"], bass.IndirectOffsetOnAxis(z_at[:, u, n, j:j + 1], 0),
                                                     z[:, u, j, :], None).then_inc(sent[u], 16)

            with pool.Fori(0, G // 2) as i:
                for u in range(2):
                    send(i * 2 + u, u)
                    wait(pool, sent[u], i * (16 * TOP * J) + 16 * TOP * J)
                    pool.sem_inc(s["sent_free"], 1)
            send(G - 1, 0)
            pool.wait_ge(sent[0], (G // 2 + 1) * 16 * TOP * J)
            pool.sem_inc(s["sent_free"], 1)

        @block.scalar
        def _(act):
            act.wait_ge(s["var_go"], 1)
            nc.scalar.activation(sd[:, :], var[:, :], ACT.Sqrt).then_inc(s["sd_done"], 1)
            act.wait_ge(s["stats"], 1)

            def norm(g, u):
                wait(act, s["sent_free"], g + 1)
                for j in range(J):
                    nc.scalar.activation(z[:, u, j, :], X[:, ds(g * J + j, 1), :].rearrange("p a c -> p (a c)"),
                                         ACT.Identity, bias=nb[:, ds(g * J + j, 1)], scale=r[:, ds(g * J + j, 1)])\
                        .then_inc(s["z_made"], 1)
                for j in range(J):
                    wait(act, s["z_turned"], g * J + j + 1)
                    nc.scalar.copy(zT[:, j, :], pt[j % 2][:, 0:D]).then_inc(s["zT_kept"], 1)

            with act.Fori(0, G // 2) as i:
                for u in range(2):
                    norm(i * 2 + u, u)
            norm(G - 1, 0)

        @block.tensor
        def _(pe):
            def gates(g, u):
                for j in range(J):
                    wait(pe, s["z_made"], g * J + j + 1)
                    wait(pe, s["zT_kept"], g * J + j + 1)
                    for c in range(KC):
                        last = nc.tensor.transpose(pt[j % 2][:, c * P:(c + 1) * P], z[:, u, j, c * P:(c + 1) * P],
                                                   ident[:, :])
                    last.then_inc(s["z_turned"], 1)
                wait(pe, s["zT_kept"], g * J + J + 2)
                for j in range(J):
                    for c in range(KC):
                        last = nc.tensor.matmul(pg[u][:, j * NE:(j + 1) * NE], zT[:, j, c * P:(c + 1) * P], wg[:, c, :],
                                                start=(c == 0), stop=(c == KC - 1))
                last.then_inc(s["gate_prod"], 1)

            def ranks(g):
                wait(pe, s["mask_made"], g + 1)
                nc.tensor.matmul(pr[:, 0:(J + 1) * NE], before[:, :], mask[:, :, :].rearrange("p j e -> p (j e)"),
                                 start=True, stop=False)
                for j in range(J):
                    last = nc.tensor.matmul(pr[:, (j + 1) * NE:(J + 1) * NE], ones[:, :],
                                            mask[:, j:j + 1, :].broadcast_to([P, J - j, NE]),
                                            start=False, stop=(j == J - 1))
                last.then_inc(s["rank_prod"], 1)

            pe.wait_ge(s["consts"], 8)
            pe.wait_ge(s["gate_in"], 32)
            pe.sem_inc(s["zT_kept"], 2)
            gates(0, 0)
            with pe.Fori(0, G // 2) as i:
                for u in range(2):
                    gates(i * 2 + u + 1, 1 - u)
                    ranks(i * 2 + u)
            ranks(G - 1)

        @block.vector
        def _(dve):
            nc.vector.memset(none[:, :], 0.0).then_inc(s["none_made"], 1)
            nc.vector.memset(mask[:, J, :], 0.0)
            nc.vector.memset(onesE[:, :], 1.0)
            with dve.Fori(0, G) as g:
                for j in range(J):
                    nc.vector.bn_stats(st[:, ds(g * J + j, 1), :].rearrange("p a c -> p (a c)"),
                                       X[:, ds(g * J + j, 1), :].rearrange("p a c -> p (a c)"))
            dve.drain()
            for t in range(T):
                nc.vector.bn_aggr(mv[:, t, :], st[:, t, :])
            dve.drain()
            nc.vector.tensor_scalar(var[:, :], mv[:, :, 1], EPS, None, ALU.add).then_inc(s["var_go"], 1)
            dve.wait_ge(s["sd_done"], 1)
            nc.vector.reciprocal(r[:, :], sd[:, :])
            dve.drain()
            nc.vector.scalar_tensor_tensor(nb[:, :], mv[:, :, 0], -1.0, r[:, :], ALU.mult, ALU.mult)\
                .then_inc(s["stats"], 1)
            dve.wait_ge(s["consts"], 8)
            dve.wait_ge(s["gate_in"], 32)
            nc.vector.tensor_copy(rank[:, :], rank_i[:, :])
            nc.vector.tensor_copy(region[:, :], region_i[:, :])
            nc.vector.tensor_copy(away[:, :, :], away_i[:, :, :])
            nc.vector.tensor_copy(tnum[:, :], tnum_i[:, :])
            dve.drain()
            nc.vector.tensor_copy(base[:, :], region[:, :])
            dve.drain()
            rank3 = rank[:, :].unsqueeze(1).broadcast_to([P, J, NE])

            def pick_top(hot):
                nc.vector.tensor_reduce(m1[:, :], gate[:, :, :], AX, ALU.max)
                dve.drain()
                nc.vector.tensor_tensor(eq[:, :, :], gate[:, :, :], m1[:, :].unsqueeze(2).broadcast_to([P, J, NE]),
                                        ALU.is_equal)
                dve.drain()
                nc.vector.tensor_tensor(eq[:, :, :], eq[:, :, :], rank3, ALU.mult)
                dve.drain()
                nc.vector.tensor_reduce(m1[:, :], eq[:, :, :], AX, ALU.max)
                dve.drain()
                nc.vector.tensor_tensor(hot, m1[:, :].unsqueeze(2).broadcast_to([P, J, NE]), rank3, ALU.is_equal)
                dve.drain()

            def pick(g, u, last):
                t0 = g * J
                hot = [hots[:, n, ds(t0, J), :] for n in range(TOP)]
                wait(dve, s["gate_prod"], g + 1)
                nc.vector.tensor_tensor(gate[:, :, :], pg[u][:, 0:J * NE].rearrange("p (j e) -> p j e", e=NE),
                                        bg[:, :].unsqueeze(1).broadcast_to([P, J, NE]), ALU.add)
                dve.drain()
                pick_top(hot[0])
                nc.vector.scalar_tensor_tensor(out=gate[:, :, :], in0=hot[0], scalar=-3e38, in1=gate[:, :, :],
                                               op0=ALU.mult, op1=ALU.add)
                dve.drain()
                pick_top(hot[1])
                if last:
                    nc.vector.tensor_scalar(hots[:, :, T - 1, :], hots[:, :, T - 1, :], valid[:, :], None, ALU.mult)
                    dve.drain()
                nc.vector.tensor_tensor(mask[:, 0:J, :], hot[0], hot[1], ALU.add).then_inc(s["mask_made"], 1)
                both = hots[:, :, ds(t0, J), :]
                nc.vector.tensor_reduce(picked[:, :, :], both, AX, ALU.add)
                dve.drain()
                nc.vector.tensor_scalar(picked[:, :, :], picked[:, :, :], -1.0, 1.0, ALU.mult, ALU.add)
                dve.drain()
                nc.vector.tensor_tensor(picked[:, :, :], picked[:, :, :], away[:, :, ds(t0, J)], ALU.mult)
                wait(dve, s["rank_prod"], g + 1)
                nc.vector.tensor_tensor(place[:, :, :], pr[:, 0:J * NE].rearrange("p (j e) -> p j e", e=NE),
                                        base[:, :].unsqueeze(1).broadcast_to([P, J, NE]), ALU.add)
                dve.drain()
                nc.vector.tensor_tensor(base[:, :], base[:, :], pr[:, J * NE:(J + 1) * NE], ALU.add)
                nc.vector.tensor_tensor(chosen[:, :, :, :], both,
                                        place[:, :, :].unsqueeze(1).broadcast_to([P, TOP, J, NE]), ALU.mult)
                dve.drain()
                nc.vector.tensor_reduce(pos[:, :, ds(t0, J)], chosen[:, :, :, :], AX, ALU.add)
                dve.drain()
                nc.vector.tensor_tensor(pos[:, :, ds(t0, J)], pos[:, :, ds(t0, J)], picked[:, :, :], ALU.add)
                dve.drain()
                wait(dve, s["sent_free"], g + 1)
                nc.vector.tensor_copy(z_at[:, u, :, :], pos[:, :, ds(t0, J)]).then_inc(s["at_made"], 1)

            with dve.Fori(0, G // 2) as i:
                for u in range(2):
                    pick(i * 2 + u, u, False)
            pick(G - 1, 0, True)
            dve.drain()
            nc.vector.tensor_copy(base_i[:, :], base[:, :]).then_inc(s["base_made"], 1)
            nc.vector.tensor_tensor(tiles[:, :], base[:, :], region[:, :], ALU.subtract)
            dve.drain()
            nc.vector.tensor_scalar(tiles_i[:, :], tiles[:, :], float(P - 1), None, ALU.add)
            dve.drain()
            nc.vector.tensor_scalar(tiles_i[:, :], tiles_i[:, :], P.bit_length() - 1, None, ALU.logical_shift_right)
            dve.drain()
            nc.vector.tensor_copy(tiles[:, :], tiles_i[:, :])
            dve.drain()
            nc.vector.tensor_tensor_scan(tend[:, :], onesE[:, :], tiles[:, :], 0.0, ALU.mult, ALU.add)
            nc.vector.tensor_scalar(step[:, :], tiles[:, :], -float(P), float(CAP), ALU.mult, ALU.add)
            dve.drain()
            nc.vector.tensor_tensor(delta[:, :], tend[:, :], tiles[:, :], ALU.subtract)
            nc.vector.tensor_tensor(full[:, :, :], tend[0:1, :].unsqueeze(1).broadcast_to([1, TABLE, NE]),
                                    tnum[:, :].unsqueeze(2).broadcast_to([1, TABLE, NE]), ALU.is_le)
            dve.drain()
            nc.vector.scalar_tensor_tensor(out=delta[:, :], in0=delta[:, :], scalar=float(P), in1=region[:, :],
                                           op0=ALU.mult, op1=ALU.subtract)
            nc.vector.tensor_reduce(texp[:, :], full[:, :, :], AX, ALU.add)
            dve.drain()
            nc.vector.tensor_scalar(tile_exp[:, :], texp[:, :], float(NE - 1), None, ALU.min)
            nc.vector.tensor_tensor(full[:, :, :], full[:, :, :], step[0:1, :].unsqueeze(1).broadcast_to([1, TABLE, NE]),
                                    ALU.mult)
            dve.drain()
            nc.vector.tensor_reduce(trow[:, :], full[:, :, :], AX, ALU.add)
            dve.drain()
            nc.vector.scalar_tensor_tensor(out=trow[:, :], in0=tnum[:, :], scalar=float(P), in1=trow[:, :],
                                           op0=ALU.mult, op1=ALU.add)
            dve.drain()
            nc.vector.tensor_scalar(tile_row[:, :], trow[:, :], float(IDLE), None, ALU.min)
            for n in range(TOP):
                nc.vector.tensor_tensor(hots[:, n, :, :], hots[:, n, :, :],
                                        delta[:, :].unsqueeze(1).broadcast_to([P, T, NE]), ALU.mult)
            dve.drain()
            nc.vector.tensor_reduce(moved[:, :, :], hots[:, :, :, :], AX, ALU.add)
            dve.drain()
            nc.vector.tensor_tensor(pos[:, :, :], pos[:, :, :], moved[:, :, :], ALU.add)
            dve.drain()
            nc.vector.tensor_scalar(y_at[:, :, :], pos[:, :, :], float(CT * P - 1), None, ALU.min)


def run_tiles(nc, k, dram, sb, ps, sem, w, tile_row, tile_exp):
    ctx = ExitStack()
    with ctx:
        ident = k["ident"]
        zt = sb(ctx, "t_z", [P, ZS, D])
        zT = sb(ctx, "t_zT", [P, 2, D])
        h = sb(ctx, "t_h", [P, 2, EH])
        gl = sb(ctx, "t_g", [P, 2, EH])
        gT = sb(ctx, "t_gT", [P, 2, EH])
        y = sb(ctx, "t_y", [P, ZS, D])
        pz = [ps(ctx, f"t_pz{i}", [P, 512]) for i in range(2)]
        pg = ps(ctx, "t_pg", [P, 512])
        p1 = [ps(ctx, f"t_p1{i}", [P, 512]) for i in range(2)]
        p2 = [ps(ctx, f"t_p2{i}", [P, 512]) for i in range(2)]
        s = {n: sem("t_" + n) for n in ("z_turned zT_kept h_prod h_made g_made g_turned gT_kept y_prod y_made "
                                        "y_out y_free").split()}
        z_in = [sem(f"t_z_in{i}") for i in range(ZS)]
        block = ctx.enter_context(nc.Block())

        def load(eng, table, at, n, top):
            _, regs = nc.values_load_multi_w_load_instructions(
                table[0:1, ds(at, n)], engines=[eng.engine], min_val=0, max_val=top,
                skip_runtime_bounds_check_because="the entries are clipped where the table is made")
            return regs

        @block.sync
        def _(sp):
            rows = load(sp, tile_row, 0, ZS, IDLE)
            for t in range(ZS):
                sp.dma_start(zt[:, t, :], dram["z"][ds(rows[t], P), :]).then_inc(z_in[t], 16)
            with sp.Fori(0, TURNS) as i:
                rows = load(sp, tile_row, i * TU + ZS, TU, IDLE)
                for v in range(TU):
                    t = i * TU + v + 1
                    wait(sp, s["z_turned"], t)
                    sp.dma_start(zt[:, v % ZS, :], dram["z"][ds(rows[v], P), :]).then_inc(z_in[v % ZS], 16)
            for n in range(ZS):
                sp.wait_ge(z_in[n], 16 * (TURNS * TU // ZS + 1))

        @block.gpsimd
        def _(pool):
            pool.sem_inc(s["y_free"], ZS)

            def store(t, slot):
                wait(pool, s["y_made"], t + 3)
                pool.dma_start(dram["y"][ds(t * P, P), :], y[:, slot, :]).then_inc(s["y_out"], 16)
                wait(pool, s["y_out"], t * 16 + 16)
                pool.sem_inc(s["y_free"], 1)

            with pool.Fori(0, CT // ZS) as i:
                for v in range(ZS):
                    store(i * ZS + v, v)
            for v in range(CT % ZS):
                store(CT // ZS * ZS + v, v)

        @block.scalar
        def _(act):
            def keep_rows(t, slot):
                wait(act, s["z_turned"], t + 1)
                nc.scalar.copy(zT[:, slot, :], pz[slot][:, 0:D]).then_inc(s["zT_kept"], 1)

            def keep_hidden(t, slot):
                wait(act, s["g_turned"], t + 1)
                nc.scalar.copy(gT[:, slot, :], pg[:, :]).then_inc(s["gT_kept"], 1)

            def gelu(t, slot):
                wait(act, s["h_made"], t + 1)
                nc.scalar.activation(gl[:, slot, :], h[:, slot, :], ACT.Gelu).then_inc(s["g_made"], 1)

            keep_rows(0, 0)
            keep_rows(1, 1)
            gelu(0, 0)
            with act.Fori(0, TURNS) as i:
                for v in range(TU):
                    t, u = i * TU + v + 1, (v + 1) % 2
                    keep_rows(t + 1, 1 - u)
                    keep_hidden(t - 1, 1 - u)
                    gelu(t, u)
            keep_hidden(CT - 1, (CT - 1) % 2)

        @block.tensor
        def _(pe):
            def turn_rows(t, slot, used, u):
                wait(pe, z_in[slot], used * 16 + 16)
                for c in range(KC):
                    last = nc.tensor.transpose(pz[u][:, c * P:(c + 1) * P], zt[:, slot, c * P:(c + 1) * P], ident[:, :])
                last.then_inc(s["z_turned"], 1)

            def turn_hidden(t, u):
                wait(pe, s["g_made"], t + 1)
                for c in range(EHC):
                    last = nc.tensor.transpose(pg[:, c * P:(c + 1) * P], gl[:, u, c * P:(c + 1) * P], ident[:, :])
                last.then_inc(s["g_turned"], 1)

            def first(t, e, u):
                wait(pe, s["zT_kept"], t + 1)
                for c in range(KC):
                    last = nc.tensor.matmul(p1[u][:, :], zT[:, u, c * P:(c + 1) * P],
                                            w["w1"][:, ds(e, 1), c, :].rearrange("p a n -> p (a n)"),
                                            start=(c == 0), stop=(c == KC - 1))
                last.then_inc(s["h_prod"], 1)

            def second(t, e, u):
                wait(pe, s["gT_kept"], t + 1)
                wait(pe, s["y_made"], t + 1)
                for c in range(EHC):
                    last = nc.tensor.matmul(p2[u][:, 0:D], gT[:, u, c * P:(c + 1) * P],
                                            w["w2"][:, ds(e, 1), c, :].rearrange("p a n -> p (a n)"),
                                            start=(c == 0), stop=(c == EHC - 1))
                last.then_inc(s["y_prod"], 1)

            pe.sem_inc(s["y_made"], 2)
            turn_rows(0, 0, 0, 0)
            turn_rows(1, 1, 0, 1)
            first(0, load(pe, tile_exp, 0, 1, NE - 1)[0], 0)
            with pe.Fori(0, TURNS) as i:
                exp = load(pe, tile_exp, i * TU, TU + 1, NE - 1)
                for v in range(TU):
                    t, u = i * TU + v + 1, (v + 1) % 2
                    turn_rows(t + 1, (v + 2) % ZS, i * (TU // ZS) + (v + 2) // ZS, 1 - u)
                    turn_hidden(t - 1, 1 - u)
                    first(t, exp[v + 1], u)
                    second(t - 1, exp[v], 1 - u)
            turn_hidden(CT - 1, (CT - 1) % 2)
            second(CT - 1, load(pe, tile_exp, CT - 1, 1, NE - 1)[0], (CT - 1) % 2)

        @block.vector
        def _(dve):
            def hidden(t, e, u):
                wait(dve, s["h_prod"], t + 1)
                nc.vector.tensor_tensor(h[:, u, :], p1[u][:, :], w["b1"][:, ds(e, 1), :].rearrange("p a n -> p (a n)"),
                                        ALU.add).then_inc(s["h_made"], 1)

            def result(t, e, u, slot):
                wait(dve, s["y_prod"], t + 1)
                wait(dve, s["y_free"], t + 1)
                nc.vector.tensor_tensor(y[:, slot, :], p2[u][:, 0:D], w["b2"][:, ds(e, 1), :].rearrange("p a n -> p (a n)"),
                                        ALU.add).then_inc(s["y_made"], 1)

            hidden(0, load(dve, tile_exp, 0, 1, NE - 1)[0], 0)
            with dve.Fori(0, TURNS) as i:
                exp = load(dve, tile_exp, i * TU, TU + 1, NE - 1)
                for v in range(TU):
                    t, u = i * TU + v + 1, (v + 1) % 2
                    hidden(t, exp[v + 1], u)
                    result(t - 1, exp[v], 1 - u, v % ZS)
            result(CT - 1, load(dve, tile_exp, CT - 1, 1, NE - 1)[0], (CT - 1) % 2, (CT - 1) % ZS)


def combine(nc, k, dram, sb, sem, y_at):
    ctx = ExitStack()
    with ctx:
        X = k["X"]
        at = sb(ctx, "c_at", [P, 2, TOP, J], I32)
        got = sb(ctx, "c_got", [P, 2, TOP, J, D])
        at_made, summed, added, out_done = sem("c_at_made"), sem("c_summed"), sem("c_added"), sem("c_out_done")
        fetched = [sem("c_fetched0"), sem("c_fetched1")]
        block = ctx.enter_context(nc.Block())

        @block.sync
        def _(sp):
            with sp.Fori(0, G - 1) as g:
                wait(sp, added, g + 1)
                sp.dma_start(dram["out"][ds(g * GN, GN), :].rearrange("(j p) c -> p j c", p=P), X[:, ds(g * J, J), :])\
                    .then_inc(out_done, 16)
            sp.wait_ge(added, G)
            sp.dma_start(dram["out"][(G - 1) * GN:(T - 1) * P, :].rearrange("(j p) c -> p j c", p=P),
                         X[:, T - J:T - 1, :]).then_inc(out_done, 16)
            sp.dma_start(dram["out"][(T - 1) * P:N, :], X[0:LAST, T - 1, :]).then_inc(out_done, 16)
            sp.wait_ge(out_done, 16 * (G + 1))

        @block.gpsimd
        def _(pool):
            def fetch(g, u):
                wait(pool, summed, g + 1)
                nc.gpsimd.tensor_copy(at[:, u, :, :], y_at[:, :, ds(g * J, J)]).then_inc(at_made, 1)
                wait(pool, at_made, g + 1)
                for j in range(J):
                    for n in range(TOP):
                        nc.gpsimd.indirect_dma_start(got[:, u, n, j, :], None, dram["y"],
                                                     bass.IndirectOffsetOnAxis(at[:, u, n, j:j + 1], 0))\
                            .then_inc(fetched[u], 16)

            pool.sem_inc(summed, 2)
            with pool.Fori(0, G // 2) as i:
                for u in range(2):
                    fetch(i * 2 + u, u)
            fetch(G - 1, 0)

        @block.vector
        def _(dve):
            def add(g, u, turn):
                wait(dve, fetched[u], turn * (16 * TOP * J) + 16 * TOP * J)
                nc.vector.tensor_tensor(got[:, u, 0, :, :], got[:, u, 0, :, :], got[:, u, 1, :, :], ALU.add)
                dve.drain()
                nc.vector.tensor_tensor(X[:, ds(g * J, J), :], X[:, ds(g * J, J), :], got[:, u, 0, :, :], ALU.add)\
                    .then_inc(added, 1)
                dve.drain()
                dve.sem_inc(summed, 1)

            with dve.Fori(0, G // 2) as i:
                for u in range(2):
                    add(i * 2 + u, u, i)
            add(G - 1, 0, G // 2)


def build(nc, d, out):
    dram = {
        "feat": nc.dram_tensor("feat", (T * P, FW), F32, kind="Internal").ap(),
        "qk": nc.dram_tensor("qk_rows", (T * P, 2 * D), F32, kind="Internal").ap(),
        "rec": nc.dram_tensor("edge_records", (P * CH, 4), F32, kind="Internal").ap(),
        "ctile": nc.dram_tensor("unit_tiles", (CH // CU,), I32, kind="Internal").ap(),
        "z": nc.dram_tensor("expert_rows", (NOWHERE + TOP * T * P, D), F32, kind="Internal").ap(),
        "y": nc.dram_tensor("expert_results", (CT * P, D), F32, kind="Internal").ap(),
        "out": out,
    }
    with ExitStack() as ctx:
        def sb(stack, name, shape, dt=F32):
            return stack.enter_context(nc.sbuf_tensor(name, shape, dt))

        def ps(stack, name, shape):
            return stack.enter_context(nc.psum_tensor(name, shape, F32))

        def sem(name):
            return ctx.enter_context(nc.semaphore(name))

        k = constants(nc, ctx, sb, sem)
        with ExitStack() as keep:
            front(nc, k, d, dram, sb, ps, sem, keep)
            mixer(nc, k, d, dram, sb, ps, sem)
        graph(nc, k, d, dram, sb, ps, sem)
        experts(nc, k, d, dram, sb, ps, sem)


def kernel(x, src, dst, edge_weight, L0_gnn_Ws, L0_gnn_bs, L0_gnn_aw, L0_gnn_ab, L0_mix_ln1_w, L0_mix_ln1_b,
           L0_mix_Wx, L0_mix_bx, L0_mix_Wq, L0_mix_Wk, L0_mix_Wv, L0_mix_Wo, L0_mix_bo, L0_mix_ln2_w, L0_mix_ln2_b,
           L0_mix_W1, L0_mix_b1, L0_mix_W2, L0_mix_b2, L0_ffn_Wg, L0_ffn_bg, L0_ffn_W1, L0_ffn_b1, L0_ffn_W2,
           L0_ffn_b2):
    import numpy as np
    import concourse.bacc as bacc
    from concourse.bass_utils import run_bass_kernel_spmd as run

    def a(v):
        return np.ascontiguousarray(np.asarray(v))

    def flip(v):
        return np.ascontiguousarray(np.asarray(v).T)

    def column(v):
        v = np.asarray(v)
        return a(np.moveaxis(v.reshape(v.shape[:-1] + (-1, P)), -1, 0))

    gws, gaw = np.asarray(L0_gnn_Ws), np.asarray(L0_gnn_aw)
    arrays = {
        "x": a(x), "src": a(src), "dst": a(dst), "edge_weight": a(edge_weight),
        "Ws": a(gws.transpose(1, 0, 2).reshape(D, GH * GO)), "WsT": a(gws.transpose(0, 2, 1).reshape(GH * GO, D)),
        "bs": a(np.asarray(L0_gnn_bs).reshape(GH * GO)),
        "bs_c": column(np.asarray(L0_gnn_bs).reshape(GH * GO)), "bx_c": column(L0_mix_bx),
        "ln1_wc": column(L0_mix_ln1_w), "ln1_bc": column(L0_mix_ln1_b), "ln2_wc": column(L0_mix_ln2_w),
        "ln2_bc": column(L0_mix_ln2_b), "b1_c": column(L0_mix_b1), 
        "aw": a(gaw), "awe": a(gaw[:, 2 * GO]), "ab": a(L0_gnn_ab),
        "ln1_w": a(L0_mix_ln1_w), "ln1_b": a(L0_mix_ln1_b), "Wx": a(L0_mix_Wx), "WxT": flip(L0_mix_Wx),
        "WqT": flip(L0_mix_Wq), "WkT": flip(L0_mix_Wk), "WvT": flip(L0_mix_Wv),
        "WoT": flip(L0_mix_Wo), "bo": a(L0_mix_bo), 
        "W1T": flip(L0_mix_W1), "W2T": flip(L0_mix_W2), "b2": a(L0_mix_b2),
        "Wg": a(L0_ffn_Wg), "bg": a(L0_ffn_bg), "eW1": a(L0_ffn_W1), "eW2": a(L0_ffn_W2),
        "eb1": a(L0_ffn_b1), "eb2": a(L0_ffn_b2),
    }
    nc = bacc.Bacc("TRN2", target_bir_lowering=False, num_devices=1)
    d = {n: nc.dram_tensor(f"in_{n}", v.shape, mybir.dt.from_np(v.dtype), kind="ExternalInput").ap()
         for n, v in arrays.items()}
    out = nc.dram_tensor("out_rows", (N, D), F32, kind="ExternalOutput").ap()
    build(nc, d, out)
    r = run(nc, [{f"in_{n}": v for n, v in arrays.items()}], core_ids=[0])
    return r.results[0]["out_rows"]
```

```python
from contextlib import ExitStack

import concourse.bass as bass
from concourse import mybir

F32 = mybir.dt.float32
I32 = mybir.dt.int32
BF16 = mybir.dt.bfloat16
ALU = mybir.AluOpType
ACT = mybir.ActivationFunctionType
AX = mybir.AxisListType.X
ds = bass.ds

P = 128
N = 6250
D = 256
T = -(-N // P)
LAST = N - (T - 1) * P
J = 7
G = T // J
GN = J * P
HALF = GN // 2
KC = D // P

GH, GO = 4, 64
FW = D + GH
FX = FW + GH

MH, MD = 8, 32
HID = 1024
HC = HID // P

NE, EH, TOP = 8, 512, 2
EHC = EH // P
CAP = (T + 1) * P
IDLE = NE * CAP
NOWHERE = IDLE + P
CT = (TOP * N + NE * (P - 1)) // P
TU = 8
ZW = D + 1
ZS = 4
ZB = 4
TURNS = (CT - 1) // TU
TABLE = CT + ZS - 1
assert TURNS * TU == CT - 1 and TU % ZS == 0

ECOUNT = 100000
EP = 125
EC = ECOUNT // EP
CB = 40
SC = CB // 2
NB = EC // CB
B = 8
CU = 2
UNIT = CU * P
UG = B // CU
CH = -(-(ECOUNT // UNIT + T) // (2 * UG)) * 2 * B
NG = CH // B
GS = 4
GPOOL = 2
FRONT = G
PLACED = G + 2 + G // 2
TWICE = NB - PLACED - (G - 1)
CPP = CH // B
EPS = 1e-5
NEG = -1e30
assert NG % 2 == 0 and GS % 2 == 0
assert T == G * J and NB * CB == EC and 0 < TWICE < G - 1


def wait(eng, sem, count):
    eng.wait_ge(sem, count)
    if not isinstance(count, int):
        eng.nop(nofuse=True)


def norm_begin(nc, dve, act_go, src, st, mv, var):
    for j in range(J):
        nc.vector.bn_stats(st[:, j, :], src(j))
    dve.drain()
    for j in range(J):
        nc.vector.bn_aggr(mv[:, j, :], st[:, j, :])
    dve.drain()
    nc.vector.tensor_scalar(var[:, :], mv[:, :, 1], EPS, None, ALU.add).then_inc(act_go, 1)


def norm_end(nc, dve, act_done, count, mv, sd, r, nb):
    wait(dve, act_done, count)
    nc.vector.reciprocal(r[:, :], sd[:, :])
    dve.drain()
    return nc.vector.scalar_tensor_tensor(nb[:, :], mv[:, :, 0], -1.0, r[:, :], ALU.mult, ALU.mult)


def norm_stats(nc, dve, act_go, act_done, count, src, st, mv, var, sd, r, nb):
    norm_begin(nc, dve, act_go, src, st, mv, var)
    return norm_end(nc, dve, act_done, count, mv, sd, r, nb)


def constants(nc, ctx, sb, sem):
    k = {}
    k["X"] = sb(ctx, "X", [P, T, D])
    k["scl"] = sb(ctx, "scl", [P, T, 4])
    k["a_src"] = sb(ctx, "a_src", [P, T, 3, GH], BF16)
    k["ident"] = sb(ctx, "ident", [P, P])
    k["ones"] = sb(ctx, "ones", [P, P])
    k["iota"] = sb(ctx, "iota", [P, P])
    k["awe"] = sb(ctx, "awe", [P, GH])
    k["tiles"] = sb(ctx, "tiles", [1, CH // CU + 4 * UG], I32)
    return k


def front(nc, k, d, dram, sb, ps, sem, keep):
    ctx = ExitStack()
    with ctx:
        X, scl, a_src, ident, ones, iota = (k[n] for n in ("X", "scl", "a_src", "ident", "ones", "iota"))
        order = sb(keep, "order", [EP, EC], I32)
        rec = sb(keep, "rec", [EP, EC, 4])
        tile_f = sb(keep, "tile_f", [EP, EC])
        carry = sb(keep, "carry", [EP, T])
        kmax = sb(keep, "kmax", [P, D])
        stage_i = sb(keep, "stage_i", [EP, 2, SC], I32)
        stage_r = sb(keep, "stage_r", [EP, 2, SC, 4])
        k.update(order=order, rec=rec, tile_f=tile_f, carry=carry, kmax=kmax, stage_i=stage_i, stage_r=stage_r)
        k["E"] = sb(keep, "E", [EP, T, CB])
        k["S"] = sb(keep, "S", [EP, T, CB])
        k["seg"] = seg = sb(keep, "seg", [EP, T, CB], mybir.dt.bfloat16)
        k["pos"] = sb(keep, "pos", [EP, CB])
        k["pos_i"] = sb(keep, "pos_i", [EP, 3, CB], I32)
        k["eq0"] = sb(keep, "eq0", [EP, T])
        src_i = sb(ctx, "src_i", [EP, EC], I32)
        dst_i = sb(ctx, "dst_i", [EP, EC], I32)
        tmp_i = sb(ctx, "tmp_i", [EP, EC], I32)
        elem = sb(ctx, "elem", [EP, EC])
        tile_h = sb(ctx, "tile_h", [EP, EC], BF16)
        junk = sb(ctx, "junk", [EP, J, EC], BF16)
        hist = sb(ctx, "hist", [EP, T])
        before = sb(ctx, "before", [P, P])
        nch_i = sb(ctx, "nch_i", [P, T], I32)
        nch = sb(ctx, "nch", [P, T])
        cend = sb(ctx, "cend", [P, T])
        onesT = sb(ctx, "onesT", [P, T])
        unit_i = sb(ctx, "unit_i", [CPP, UG], I32)
        unit = sb(ctx, "unit", [CPP, UG])
        before_unit = sb(ctx, "before_unit", [CPP, UG, T])
        unit_tile = sb(ctx, "unit_tile", [CPP, UG])
        unit_tile_i = sb(ctx, "unit_tile_i", [CPP, UG], I32)
        iota_i = sb(ctx, "iota_i", [P, P], I32)
        blank = k["erec"][:, 0:CH, :]
        padneg = sb(ctx, "padneg", [P, T])
        wx = sb(ctx, "wx", [P, KC, D])
        wst = sb(ctx, "wst", [P, KC, D])
        wfe = sb(ctx, "wfe", [P, KC, FX])
        wqk = sb(ctx, "wqk", [P, KC, 2 * D])
        bdqk = sb(ctx, "bdqk", [P, 2, P])
        bdaw = sb(ctx, "bdaw", [P, KC, 2 * GH])
        bcol = sb(ctx, "bcol", [P, 2, KC])
        bbc = sb(ctx, "bbc", [P, 2, KC, P])
        fbias = sb(ctx, "fbias", [P, FX])
        abias = sb(ctx, "abias", [P, GH])
        qkbias = sb(ctx, "qkbias", [P, 2 * D])
        ln1 = sb(ctx, "ln1", [P, 2, KC])
        st = sb(ctx, "st", [P, J, 6])
        mv = sb(ctx, "mv", [P, J, 2])
        var = sb(ctx, "var", [P, J])
        sd = sb(ctx, "sd", [P, J])
        r = sb(ctx, "r", [P, 2, J])
        nb = sb(ctx, "nb", [P, 2, J])
        tmpj = sb(ctx, "tmpj", [P, J])
        xn = sb(ctx, "xn", [P, J, D])
        z = sb(ctx, "z", [P, J, D])
        xnT = sb(ctx, "xnT", [P, J, D])
        lT = sb(ctx, "lT", [P, J, D])
        fe = sb(ctx, "fe", [P, J, FX])
        qk = sb(ctx, "qk", [P, J, 2 * D])
        gmax = sb(ctx, "gmax", [P, D])
        part = sb(ctx, "part", [P, J, GH], BF16)
        rest = sb(ctx, "rest", [P, J, GH])
        qs = sb(ctx, "qs", [P, 2, J * MH])
        pt = [ps(ctx, f"f_pt{i}", [P, 512]) for i in range(2)]
        pf = [ps(ctx, f"f_pf{i}", [P, 512]) for i in range(2)]
        pq = [ps(ctx, f"f_pq{i}", [P, 512]) for i in range(2)]
        pc = ps(ctx, "f_pc", [P, 512])
        pb = ps(ctx, "f_pb", [P, 512])

        x_in, src_in, edges_in, weights_in = sem("x_in"), sem("src_in"), sem("edges_in"), sem("weights_in")
        consts_made, blocks_made, x_cleared = sem("consts_made"), sem("blocks_made"), sem("x_cleared")
        hist_done, counts_done = sem("hist_done"), sem("counts_done")
        k["sorted"] = sem("sorted_")
        k["scattered"] = [sem("scattered0"), sem("scattered1")]
        k["staged"] = sem("staged")
        blank_made, blank_out = sem("blank_made"), sem("blank_out")
        unit_tile_made, unit_tile_out, tiles_in = sem("unit_tile_made"), sem("unit_tile_out"), sem("tiles_in")
        bias_made, folded, fold_kept = sem("bias_made"), sem("folded"), sem("fold_kept")
        var_go, sd_done, stats_go, xn_done, z_done = (sem(s) for s in ("var_go", "sd_done", "stats_go", "xn_done", "z_done"))
        turned, turned_kept, fe_prod, fe_kept = (sem(s) for s in ("turned", "turned_kept", "fe_prod", "fe_kept"))
        qk_prod, qk_kept, qsub, qexp, rows_ready = (sem(s) for s in ("qk_prod", "qk_kept", "qsub", "qexp", "rows_ready"))
        rows_made, rows_out, rows_free = sem("rows_made"), sem("rows_out"), sem("rows_free")

        block = ctx.enter_context(nc.Block())

        @block.sync
        def _(sp):
            for tile, name in ((src_i, "src"), (dst_i, "dst"), (elem, "edge_weight")):
                sp.dma_start(tile[:, :], d[name].rearrange("(p c) -> p c", p=EP))\
                    .then_inc(src_in if name == "src" else edges_in, 16)
            sp.wait_ge(x_cleared, 1)
            sp.dma_start(X[:, 0:T - 1, :], d["x"][0:(T - 1) * P, :].rearrange("(t p) c -> p t c", p=P)).then_inc(x_in, 16)
            sp.dma_start(X[0:LAST, T - 1, :], d["x"][(T - 1) * P:N, :]).then_inc(x_in, 16)
            sp.wait_ge(unit_tile_made, 1)
            sp.dma_start(dram["unit_tile"].rearrange("(p b) -> p b", b=UG), unit_tile_i[:, :]).then_inc(unit_tile_out, 16)
            sp.wait_ge(unit_tile_out, 16)
            sp.dma_start(k["tiles"][0:1, UG:UG + CH // CU], dram["unit_tile"].unsqueeze(0)).then_inc(tiles_in, 16)
            sp.sem_inc(rows_free, 1)
            with sp.Fori(0, G) as g:
                wait(sp, rows_made, g + 1)
                sp.dma_start(dram["feat"][ds(g * GN, GN), :].rearrange("(j p) f -> p j f", p=P),
                             fe[:, :, 0:FW]).then_inc(rows_out, 16)
                sp.dma_start(dram["qk"][ds(g * GN, GN), D:2 * D].rearrange("(j p) f -> p j f", p=P),
                             qk[:, :, D:2 * D]).then_inc(rows_out, 16)
                wait(sp, rows_ready, g + 1)
                sp.dma_start(dram["qk"][ds(g * GN, GN), 0:D].rearrange("(j p) f -> p j f", p=P),
                             qk[:, :, 0:D]).then_inc(rows_out, 16)
                wait(sp, rows_out, g * 48 + 48)
                sp.sem_inc(rows_free, 1)
            sp.wait_ge(tiles_in, 16)
            sp.wait_ge(blank_out, 16)

        @block.gpsimd
        def _(pool):
            nc.gpsimd.iota(iota_i[:, :], pattern=[[1, P]], base=0, channel_multiplier=0).then_inc(consts_made, 1)
            nc.gpsimd.iota(unit_i[:, :], pattern=[[1, UG]], base=0, channel_multiplier=UG).then_inc(consts_made, 1)
            nc.gpsimd.memset(before[:, :], 1.0).then_inc(consts_made, 1)
            nc.gpsimd.memset(ones[:, :], 1.0).then_inc(consts_made, 1)
            nc.gpsimd.memset(ident[:, :], 0.0).then_inc(consts_made, 1)
            nc.gpsimd.memset(padneg[:, :], 0.0).then_inc(consts_made, 1)
            nc.gpsimd.memset(onesT[:, :], 1.0).then_inc(consts_made, 1)
            pool.wait_ge(consts_made, 7)
            nc.gpsimd.affine_select(out=before[:, :], in_=before[:, :], compare_op=ALU.is_gt, fill=0.0,
                                    base=0, pattern=[[1, P]], channel_multiplier=-1).then_inc(consts_made, 1)
            nc.gpsimd.affine_select(out=ident[:, :], in_=ident[:, :], compare_op=ALU.not_equal, fill=1.0,
                                    base=0, pattern=[[-1, P]], channel_multiplier=1).then_inc(consts_made, 1)
            nc.gpsimd.affine_select(out=padneg[:, T - 1:T], in_=padneg[:, T - 1:T], compare_op=ALU.is_gt, fill=NEG,
                                    base=LAST, pattern=[[0, 1]], channel_multiplier=-1).then_inc(consts_made, 1)
            nc.gpsimd.memset(blank[:, :, :], 0.0).then_inc(blank_made, 1)
            pool.wait_ge(blank_made, 1)
            nc.gpsimd.memset(blank[:, :, 1], -1.0).then_inc(blank_made, 1)
            nc.gpsimd.memset(rec[:, :, 3], 0.0).then_inc(consts_made, 1)
            pool.wait_ge(blank_made, 2)
            pool.dma_start(dram["rec"].rearrange("(p c) f -> p c f", p=P), blank[:, :, :]).then_inc(blank_out, 16)
            pool.wait_ge(consts_made, 11)
            pool.wait_ge(blank_out, 16)
            scatter(nc, pool, k, dram, 0, True)
            with pool.Fori(1, FRONT) as b:
                scatter(nc, pool, k, dram, b, False)

        @block.scalar
        def _(act):
            act.wait_ge(blocks_made, 2)
            loads = [(wx, "Wx"), (wst, "WsT")]
            for tile, name in loads:
                act.dma_start(tile[:, :, :], d[name].rearrange("(k p) n -> p k n", p=P)).then_inc(weights_in, 16)
            act.dma_start(wfe[:, :, 0:D], d["Ws"].rearrange("(k p) n -> p k n", p=P)).then_inc(weights_in, 16)
            for i, name in enumerate(("WqT", "WkT")):
                for h in range(P // MD):
                    act.dma_start(bdqk[h * MD:(h + 1) * MD, i, h * MD:(h + 1) * MD], d[name]).then_inc(weights_in, 16)
            for h in range(GH):
                p0 = h % 2 * GO
                for i, c0 in ((0, GO), (1, 0)):
                    act.dma_start(bdaw[p0:p0 + GO, h // 2, i * GH + h:i * GH + h + 1],
                                  d["aw"][h, c0:c0 + GO].unsqueeze(1)).then_inc(weights_in, 16)
            act.dma_start(bcol[:, 0, :], d["bx_c"]).then_inc(weights_in, 16)
            act.dma_start(bcol[:, 1, :], d["bs_c"]).then_inc(weights_in, 16)
            act.dma_start(fbias[:, 0:D], d["bs"].partition_broadcast(P)).then_inc(weights_in, 16)
            act.dma_start(abias[:, :], d["ab"].partition_broadcast(P)).then_inc(weights_in, 16)
            act.dma_start(k["awe"][:, :], d["awe"].partition_broadcast(P)).then_inc(weights_in, 16)
            act.dma_start(ln1[:, 0, :], d["ln1_wc"]).then_inc(weights_in, 16)
            act.dma_start(ln1[:, 1, :], d["ln1_bc"]).then_inc(weights_in, 16)
            assert NW == 3 + 2 * (P // MD) + 2 * GH + 7
            act.wait_ge(fold_kept, 1)
            act.wait_ge(x_in, 32)

            def normed(g):
                for i in range(2):
                    wait(act, var_go, 2 * g + i + 1)
                    nc.scalar.activation(sd[:, :], var[:, :], ACT.Sqrt).then_inc(sd_done, 1)
                    wait(act, stats_go, 2 * g + i + 1)
                    for j in range(J):
                        if i == 0:
                            nc.scalar.activation(xn[:, j, :], X[:, ds(g * J + j, 1), :].rearrange("p a c -> p (a c)"),
                                                 ACT.Identity, bias=nb[:, 0, j:j + 1],
                                                 scale=r[:, 0, j:j + 1]).then_inc(xn_done, 1)
                        else:
                            nc.scalar.activation(z[:, j, :], xn[:, j, :], ACT.Identity, bias=nb[:, 1, j:j + 1],
                                                 scale=r[:, 1, j:j + 1]).then_inc(z_done, 1)
                for j in range(J):
                    wait(act, turned, g * J + j + 1)
                    nc.scalar.copy(xnT[:, j, :], pt[j % 2][:, 0:D])
                    for c in range(KC):
                        last = nc.scalar.activation(lT[:, j, c * P:(c + 1) * P], pt[j % 2][:, D + c * P:D + (c + 1) * P],
                                                    ACT.Identity, bias=ln1[:, 1, c:c + 1], scale=ln1[:, 0, c:c + 1])
                    last.then_inc(turned_kept, 1)

            def exp_q(g):
                wait(act, qsub, g + 1)
                nc.scalar.activation(qk[:, :, 0:D], qk[:, :, 0:D], ACT.Exp).then_inc(qexp, 1)

            normed(0)
            with act.Fori(0, G - 1) as g:
                normed(g + 1)
                exp_q(g)
            exp_q(G - 1)

        @block.tensor
        def _(pe):
            pe.wait_ge(consts_made, 10)
            pe.wait_ge(hist_done, 1)
            nc.tensor.matmul(pc[:, 0:T], before[0:EP, :], hist[:, :], start=True, stop=True)
            nc.tensor.matmul(pc[:, 64:64 + T], ones[0:EP, :], hist[:, :], start=True, stop=True).then_inc(counts_done, 1)
            pe.wait_ge(weights_in, NW * 16)
            for c2 in range(KC):
                for i in range(2):
                    for c in range(KC):
                        last = nc.tensor.matmul(pq[c2][:, i * D + c * P:i * D + (c + 1) * P],
                                                wx[:, c, c2 * P:(c2 + 1) * P], bdqk[:, i, :], start=True, stop=True)
            last.then_inc(folded, 1)
            for c2 in range(KC):
                for c in range(KC):
                    last = nc.tensor.matmul(pb[:, c2 * 16:c2 * 16 + 2 * GH], wst[:, c, c2 * P:(c2 + 1) * P],
                                            bdaw[:, c, :], start=(c == 0), stop=(c == KC - 1))
            pe.wait_ge(bias_made, 1)
            for c in range(KC):
                nc.tensor.matmul(pb[:, 64:64 + 2 * GH], bbc[:, 1, c, :], bdaw[:, c, :], start=(c == 0), stop=(c == KC - 1))
            for i in range(2):
                for c in range(KC):
                    last = nc.tensor.matmul(pf[0][:, i * D + c * P:i * D + (c + 1) * P], bbc[:, 0, c, :],
                                            bdqk[:, i, :], start=True, stop=True)
            last.then_inc(folded, 1)
            pe.wait_ge(fold_kept, 1)
            pe.sem_inc(turned_kept, 1)
            pe.sem_inc(fe_kept, 1)
            pe.sem_inc(qk_kept, 1)

            def turn(g):
                for j in range(J):
                    if j == 0:
                        wait(pe, z_done, g * J + J)
                    wait(pe, turned_kept, g * J + max(j - 1, 0) + 1)
                    for c in range(KC):
                        nc.tensor.transpose(pt[j % 2][:, c * P:(c + 1) * P], xn[:, j, c * P:(c + 1) * P], ident[:, :])
                    for c in range(KC):
                        last = nc.tensor.transpose(pt[j % 2][:, D + c * P:D + (c + 1) * P], z[:, j, c * P:(c + 1) * P],
                                                   ident[:, :])
                    last.then_inc(turned, 1)

            def products(g):
                for j in range(J):
                    wait(pe, turned_kept, g * J + j + 2)
                    wait(pe, fe_kept, g * J + max(j - 1, 0) + 1)
                    for c in range(KC):
                        last = nc.tensor.matmul(pf[j % 2][:, 0:FX], xnT[:, j, c * P:(c + 1) * P], wfe[:, c, :],
                                                start=(c == 0), stop=(c == KC - 1))
                    last.then_inc(fe_prod, 1)
                    wait(pe, qk_kept, g * J + max(j - 1, 0) + 1)
                    for c in range(KC):
                        last = nc.tensor.matmul(pq[j % 2][:, :], lT[:, j, c * P:(c + 1) * P], wqk[:, c, :],
                                                start=(c == 0), stop=(c == KC - 1))
                    last.then_inc(qk_prod, 1)

            turn(0)
            with pe.Fori(0, G - 1) as g:
                products(g)
                turn(g + 1)
            products(G - 1)

        @block.vector
        def _(dve):
            nc.vector.memset(bdqk[:, :, :], 0.0).then_inc(blocks_made, 1)
            nc.vector.memset(bdaw[:, :, :], 0.0).then_inc(blocks_made, 1)
            nc.vector.memset(X[:, T - 1, :], 0.0).then_inc(x_cleared, 1)
            nc.vector.memset(kmax[:, :], NEG)
            nc.vector.memset(seg[:, :, :], 1.0)
            nc.vector.memset(k["tiles"][0:1, 0:UG], 0)
            nc.vector.memset(k["tiles"][0:1, UG + CH // CU:], 0)
            dve.drain()
            nc.vector.memset(seg[:, :, 0], 0.0)
            dve.wait_ge(src_in, 16)
            nc.vector.tensor_scalar(tmp_i[:, :], src_i[:, :], 7, None, ALU.logical_shift_right)
            dve.wait_ge(consts_made, 10)
            nc.vector.tensor_copy(iota[:, :], iota_i[:, :])
            nc.vector.tensor_copy(unit[:, :], unit_i[:, :])
            dve.drain()
            nc.vector.tensor_copy(tile_f[:, :], tmp_i[:, :])
            nc.vector.tensor_copy(tile_h[:, :], tmp_i[:, :])
            dve.drain()
            for t in range(T):
                nc.vector.tensor_scalar(junk[:, t % J, :], tile_h[:, :], float(t), 0.0, ALU.is_equal, ALU.add,
                                        accum_out=hist[:, t:t + 1])
                if t % J == J - 1:
                    dve.drain()
            nc.vector.tensor_scalar(tmp_i[:, :], src_i[:, :], P - 1, None, ALU.bitwise_and).then_inc(hist_done, 1)
            dve.wait_ge(counts_done, 1)
            nc.vector.tensor_scalar(nch_i[:, :], pc[:, 64:64 + T], float(UNIT - 1), None, ALU.add)
            dve.drain()
            nc.vector.tensor_scalar(nch_i[:, :], nch_i[:, :], UNIT.bit_length() - 1, None, ALU.logical_shift_right)
            dve.drain()
            dve.wait_ge(edges_in, 32)
            nc.vector.tensor_copy(nch[:, :], nch_i[:, :])
            nc.vector.tensor_copy(rec[:, :, 1], tmp_i[:, :])
            nc.vector.tensor_copy(rec[:, :, 0], dst_i[:, :])
            nc.vector.tensor_copy(rec[:, :, 2], elem[:, :])
            dve.drain()
            nc.vector.tensor_tensor_scan(cend[:, :], onesT[:, :], nch[:, :], 0.0, ALU.mult, ALU.add)
            dve.drain()
            nc.vector.tensor_tensor(nch[:, :], cend[:, :], nch[:, :], ALU.subtract)
            nc.vector.tensor_tensor(before_unit[:, :, :], cend[0:CPP, :].unsqueeze(1).broadcast_to([CPP, UG, T]),
                                    unit[:, :].unsqueeze(2).broadcast_to([CPP, UG, T]), ALU.is_le)
            dve.drain()
            nc.vector.tensor_scalar(nch[:, :], nch[:, :], float(UNIT), -1.0, ALU.mult, ALU.add)
            nc.vector.tensor_reduce(unit_tile[:, :], before_unit[:, :, :], AX, ALU.add)
            dve.drain()
            nc.vector.tensor_tensor(carry[:, :], pc[0:EP, 0:T], nch[0:EP, :], ALU.add)
            nc.vector.tensor_scalar(unit_tile_i[:, :], unit_tile[:, :], float(T - 1), None, ALU.min).then_inc(unit_tile_made, 1)
            place_edges(nc, dve, k, iota, 0)
            dve.wait_ge(weights_in, NW * 16)
            for i in range(2):
                for c in range(KC):
                    last = nc.vector.tensor_scalar(bbc[:, i, c, :], ones[:, :], bcol[:, i, c:c + 1], None, ALU.mult)
            last.then_inc(bias_made, 1)
            dve.wait_ge(folded, 2)
            for c2 in range(KC):
                nc.vector.tensor_copy(wqk[:, c2, :], pq[c2][:, :])
                nc.vector.tensor_copy(wfe[:, c2, D:FX], pb[:, c2 * 16:c2 * 16 + 2 * GH])
            nc.vector.tensor_copy(fbias[:, D:FW], pb[:, 64:64 + GH])
            nc.vector.tensor_tensor(fbias[:, FW:FX], pb[:, 64 + GH:64 + 2 * GH], abias[:, :], ALU.add)
            nc.vector.tensor_copy(qkbias[:, :], pf[0][:, :]).then_inc(fold_kept, 1)
            dve.wait_ge(x_in, 32)

            def begin(g, i):
                norm_begin(nc, dve, var_go, (lambda j: xn[:, j, :]) if i else
                           (lambda j: X[:, ds(g * J + j, 1), :].rearrange("p a c -> p (a c)")), st, mv, var)

            def end(g, i):
                norm_end(nc, dve, sd_done, 2 * g + i + 1, mv, sd, r[:, i, :], nb[:, i, :]).then_inc(stats_go, 1)

            def compose(g):
                nc.vector.tensor_tensor(tmpj[:, :], nb[:, 0, :], r[:, 1, :], ALU.mult)
                nc.vector.tensor_copy(scl[:, ds(g * J, J), 0], r[:, 0, :])
                nc.vector.tensor_copy(scl[:, ds(g * J, J), 1], nb[:, 0, :])
                nc.vector.tensor_tensor(scl[:, ds(g * J, J), 2], r[:, 0, :], r[:, 1, :], ALU.mult)
                dve.drain()
                nc.vector.tensor_tensor(scl[:, ds(g * J, J), 3], tmpj[:, :], nb[:, 1, :], ALU.add)

            def keep_rows(g, tiles):
                for j in tiles:
                    wait(dve, fe_prod, g * J + j + 1)
                    nc.vector.tensor_tensor(fe[:, j, :], pf[j % 2][:, 0:FX], fbias[:, :], ALU.add).then_inc(fe_kept, 1)
                    wait(dve, qk_prod, g * J + j + 1)
                    nc.vector.scalar_tensor_tensor(out=qk[:, j, :], in0=pq[j % 2][:, :],
                                                   scalar=padneg[:, ds(g * J + j, 1)], in1=qkbias[:, :],
                                                   op0=ALU.add, op1=ALU.add).then_inc(qk_kept, 1)

            def finish_rows(g, sort):
                dve.drain()
                dve.sem_inc(rows_made, 1)
                nc.vector.tensor_copy(part[:, :, :], fe[:, :, FW:FX])
                nc.vector.tensor_copy(rest[:, :, :], fe[:, :, FW:FX])
                dve.drain()
                for n in range(3):
                    nc.vector.tensor_copy(a_src[:, ds(g * J, J), n, :], part[:, :, :])
                    if n < 2:
                        nc.vector.tensor_tensor(rest[:, :, :], rest[:, :, :], part[:, :, :], ALU.subtract)
                        dve.drain()
                        nc.vector.tensor_copy(part[:, :, :], rest[:, :, :])
                        dve.drain()
                q4 = qk[:, :, 0:D].rearrange("p j (h s) -> p j h s", s=MD)
                nc.vector.tensor_reduce(qs[:, 0, :].rearrange("p (j h) -> p j h", h=MH), q4, AX, ALU.max)
                nc.vector.tensor_reduce(gmax[:, :], qk[:, :, D:2 * D].rearrange("p j c -> p c j"), AX, ALU.max)
                dve.drain()
                top = qs[:, 0, :].rearrange("p (j h) -> p j h", h=MH).unsqueeze(3).broadcast_to([P, J, MH, MD])
                nc.vector.tensor_tensor(q4, q4, top, ALU.subtract).then_inc(qsub, 1)
                nc.vector.tensor_tensor(kmax[:, :], kmax[:, :], gmax[:, :], ALU.max)
                if sort:
                    count_edges(nc, dve, k, iota, g + 2)
                wait(dve, qexp, g + 1)
                nc.vector.tensor_reduce(qs[:, 0, :].rearrange("p (j h) -> p j h", h=MH), q4, AX, ALU.add)
                dve.drain()
                nc.vector.reciprocal(qs[:, 1, :], qs[:, 0, :])
                dve.drain()
                inv = qs[:, 1, :].rearrange("p (j h) -> p j h", h=MH).unsqueeze(3).broadcast_to([P, J, MH, MD])
                nc.vector.tensor_tensor(q4, q4, inv, ALU.mult).then_inc(rows_ready, 1)

            begin(0, 0)
            end(0, 0)
            dve.wait_ge(xn_done, J)
            begin(0, 1)
            end(0, 1)
            compose(0)
            count_edges(nc, dve, k, iota, 1)
            with dve.Fori(0, G - 1) as g:
                give_places(nc, dve, k, g + 1)
                wait(dve, rows_free, g + 1)
                begin(g + 1, 0)
                keep_rows(g, (0,))
                end(g + 1, 0)
                keep_rows(g, (1, 2))
                wait(dve, xn_done, g * J + 2 * J)
                begin(g + 1, 1)
                keep_rows(g, (3,))
                end(g + 1, 1)
                dve.drain()
                compose(g + 1)
                keep_rows(g, range(4, J))
                finish_rows(g, True)
            give_places(nc, dve, k, G)
            dve.wait_ge(rows_free, G)
            keep_rows(G - 1, range(J))
            finish_rows(G - 1, False)
            place_edges(nc, dve, k, iota, G + 1)


NW = 3 + 2 * (P // MD) + 2 * GH + 7


def place_edges(nc, dve, k, iota, b):
    count_edges(nc, dve, k, iota, b)
    give_places(nc, dve, k, b)


def count_edges(nc, dve, k, iota, b):
    E, S, seg, carry, tile_f, eq0 = (k[n] for n in ("E", "S", "seg", "carry", "tile_f", "eq0"))
    cols = tile_f[:, ds(b * CB, CB)]
    dve.drain()
    nc.vector.tensor_tensor(E[:, :, :], cols.unsqueeze(1).broadcast_to([EP, T, CB]),
                            iota[0:EP, 0:T].unsqueeze(2).broadcast_to([EP, T, CB]), ALU.is_equal)
    dve.drain()
    nc.vector.tensor_copy(eq0[:, :], E[:, :, 0])
    dve.drain()
    nc.vector.tensor_tensor(E[:, :, 0], eq0[:, :], carry[:, :], ALU.add)
    dve.drain()
    nc.vector.tensor_tensor_scan(S[:, :, :].rearrange("p t c -> p (t c)"), seg[:, :, :].rearrange("p t c -> p (t c)"),
                                 E[:, :, :].rearrange("p t c -> p (t c)"), 0.0, ALU.mult, ALU.add)
    dve.drain()
    nc.vector.tensor_copy(carry[:, :], S[:, :, CB - 1])
    nc.vector.tensor_copy(E[:, :, 0], eq0[:, :])


def give_places(nc, dve, k, b):
    E, S, pos, pos_i = (k[n] for n in ("E", "S", "pos", "pos_i"))
    dve.drain()
    nc.vector.tensor_tensor(S[:, :, :], S[:, :, :], E[:, :, :], ALU.mult)
    dve.drain()
    nc.vector.tensor_reduce(pos[:, :], S[:, :, :].rearrange("p t c -> p c t"), AX, ALU.add)
    dve.drain()
    nc.vector.tensor_copy(pos_i[:, 0, :], pos[:, :])
    dve.drain()
    nc.vector.tensor_scalar(pos_i[:, 1, :], pos_i[:, 0, :], P - 1, None, ALU.bitwise_and)
    nc.vector.tensor_scalar(pos_i[:, 2, :], pos_i[:, 0, :], 7, None, ALU.logical_shift_right)
    dve.drain()
    nc.vector.scalar_tensor_tensor(out=k["order"][:, ds(b * CB, CB)], in0=pos_i[:, 1, :], scalar=float(CH),
                                   in1=pos_i[:, 2, :], op0=ALU.mult, op1=ALU.add).then_inc(k["sorted"], 1)


def scatter(nc, pool, k, dram, b, first):
    wait(pool, k["sorted"], b + 1)
    for slot in range(2):
        c0 = b * CB + slot * SC
        if not first:
            wait(pool, k["scattered"][slot], b * (16 * SC))
        nc.gpsimd.tensor_copy(k["stage_i"][:, slot, :], k["order"][:, ds(c0, SC)]).then_inc(k["staged"], 1)
        nc.gpsimd.tensor_copy(k["stage_r"][:, slot, :, :], k["rec"][:, ds(c0, SC), :]).then_inc(k["staged"], 1)
        wait(pool, k["staged"], b * 4 + slot * 2 + 2)
        for c in range(SC):
            nc.gpsimd.indirect_dma_start(dram["rec"], bass.IndirectOffsetOnAxis(k["stage_i"][:, slot, c:c + 1], 0),
                                         k["stage_r"][:, slot, c, :], None).then_inc(k["scattered"][slot], 16)


def mixer(nc, k, d, dram, sb, ps, sem):
    ctx = ExitStack()
    with ctx:
        X, scl, ident, ones, iota, kmax = (k[n] for n in ("X", "scl", "ident", "ones", "iota", "kmax"))
        w1 = sb(ctx, "w1", [P, KC, HID])
        w2 = sb(ctx, "w2", [P, HC, D])
        wxt = sb(ctx, "wxt", [P, KC, D])
        wot = sb(ctx, "wot", [P, KC, D])
        bdv = sb(ctx, "bdv", [P, P])
        headmask = sb(ctx, "headmask", [P, P])
        cols = sb(ctx, "cols", [P, 3, KC])
        b1c = sb(ctx, "b1c", [P, HC])
        rows = sb(ctx, "m_rows", [P, 4, D])
        M = sb(ctx, "M", [P, KC, D])
        chain = sb(ctx, "chain", [P, 3, KC, D])
        small = sb(ctx, "small", [P, 8])
        st = sb(ctx, "m_st", [P, J, 6])
        mv = sb(ctx, "m_mv", [P, J, 2])
        var = sb(ctx, "m_var", [P, J])
        sd = sb(ctx, "m_sd", [P, J])
        r = sb(ctx, "m_r", [P, J])
        nb = sb(ctx, "m_nb", [P, J])
        scs = sb(ctx, "scs", [P, J, 4])
        qin = sb(ctx, "qin", [P, J, D])
        qT = sb(ctx, "qT", [P, 2, D])
        xnb = sb(ctx, "xnb", [P, J, D])
        h = sb(ctx, "h", [P, J, D])
        z2 = sb(ctx, "z2", [P, J, D])
        yT = sb(ctx, "yT", [P, KC, GN])
        gT = sb(ctx, "gT", [P, HC, GN])
        zx = gT[:, :, :].rearrange("p a n -> p (a n)")[:, 0:2 * J * (D + 2)]\
            .rearrange("p (u j f) -> p u j f", j=J, f=D + 2)
        kin, kx = z2, [h, xnb]
        pk = [ps(ctx, f"m_pk{i}", [P, 512]) for i in range(2)]
        pt = [ps(ctx, f"m_pt{i}", [P, 512]) for i in range(2)]
        p1 = [ps(ctx, f"m_p1{i}", [P, 512]) for i in range(2)]
        p2 = [ps(ctx, f"m_p2{i}", [P, 512]) for i in range(2)]

        names = ("bd_made w_in kmax_turned kdiag kmax_row k_in ksub kexp scs_made zx_made ktz_prod kl "
                 "kl_turned klt kxt kxt_kept kvt kvt_kept m_prod m_kept q_in q_turned qT_kept att att_kept "
                 "xn_made m_var_go m_sd_done m_stats z2_made z_turned yT_kept h1_prod g_made h2_prod "
                 "h2_kept rec_in k_used")
        s = {n: sem(n) for n in names.split()}
        block = ctx.enter_context(nc.Block())

        zeros = yT[:, 0, :]

        def attend(pe, g, j):
            wait(pe, s["qT_kept"], g * J + j + 2)
            wait(pe, s["att_kept"], g * J + max(j - 1, 0) + 1)
            for c in range(KC):
                last = nc.tensor.matmul(pk[j % 2][:, 0:D], qT[:, j % 2, c * P:(c + 1) * P], M[:, c, :],
                                        start=(c == 0), stop=(c == KC - 1))
            last.then_inc(s["att"], 1)

        @block.sync
        def _(sp):
            sp.wait_ge(s["bd_made"], 1)
            def load_keys(g):
                sp.dma_start(kin[:, :, :], dram["qk"][ds(g * GN, GN), D:2 * D].rearrange("(j p) f -> p j f", p=P))\
                    .then_inc(s["k_in"], 16)

            load_keys(0)
            for tile, name in ((w1, "W1T"), (w2, "W2T"), (wxt, "WxT"), (wot, "WoT")):
                sp.dma_start(tile[:, :, :], d[name].rearrange("(k p) n -> p k n", p=P)).then_inc(s["w_in"], 16)
            for i in range(P // MD):
                sp.dma_start(bdv[i * MD:(i + 1) * MD, i * MD:(i + 1) * MD], d["WvT"]).then_inc(s["w_in"], 16)
            for i, name in enumerate(("ln2_wc", "ln2_bc", "bx_c")):
                sp.dma_start(cols[:, i, :], d[name]).then_inc(s["w_in"], 16)
            sp.dma_start(b1c[:, :], d["b1_c"]).then_inc(s["w_in"], 16)
            for i, name in enumerate(("ln1_w", "ln1_b", "bo", "b2")):
                sp.dma_start(rows[:, i, :], d[name].partition_broadcast(P)).then_inc(s["w_in"], 16)
            sp.sem_inc(s["q_turned"], 1)
            with sp.Fori(1, G) as g:
                wait(sp, s["k_used"], g)
                load_keys(g)
            with sp.Fori(0, G) as g:
                wait(sp, s["q_turned"], g * J + 1)
                sp.dma_start(qin[:, :, :], dram["qk"][ds(g * GN, GN), 0:D].rearrange("(j p) f -> p j f", p=P))\
                    .then_inc(s["q_in"], 16)

        @block.gpsimd
        def _(pool):
            with pool.Fori(FRONT, NB) as b:
                scatter(nc, pool, k, dram, b, False)
            for slot in range(2):
                pool.wait_ge(k["scattered"][slot], NB * 16 * SC)
            pool.dma_start(k["erec"][:, 0:CH, :], dram["rec"].rearrange("(p c) f -> p c f", p=P)).then_inc(s["rec_in"], 16)
            pool.wait_ge(s["rec_in"], 16)

        @block.scalar
        def _(act):
            def keys(g, u):
                wait(act, s["scs_made"], g + 1)
                for j in range(J):
                    last = nc.scalar.activation(zx[:, u, j, 0:D], X[:, ds(g * J + j, 1), :].rearrange("p a c -> p (a c)"),
                                                ACT.Identity, bias=scs[:, j, 3:4], scale=scs[:, j, 2:3])
                last.then_inc(s["zx_made"], 1)
                wait(act, s["ksub"], g + 1)
                nc.scalar.activation(kx[u][:, :, :], kx[u][:, :, :], ACT.Exp).then_inc(s["kexp"], 1)

            with act.Fori(0, G // 2) as i:
                for u in range(2):
                    keys(i * 2 + u, u)
            keys(G - 1, 0)

            def attention_in(g):
                wait(act, s["scs_made"], G + g + 1)
                for j in range(J):
                    nc.scalar.activation(xnb[:, j, :], X[:, ds(g * J + j, 1), :].rearrange("p a c -> p (a c)"),
                                         ACT.Identity, bias=scs[:, j, 1:2], scale=scs[:, j, 0:1]).then_inc(s["xn_made"], 1)
                    wait(act, s["q_turned"], g * J + j + 2)
                    wait(act, s["att"], g * J + max(j - 1, 0) + 1)
                    nc.scalar.copy(qT[:, j % 2, :], pt[j % 2][:, 0:D]).then_inc(s["qT_kept"], 1)

            def second_norm(g):
                wait(act, s["m_var_go"], g + 1)
                nc.scalar.activation(sd[:, :], var[:, :], ACT.Sqrt).then_inc(s["m_sd_done"], 1)
                wait(act, s["m_stats"], g + 1)
                for j in range(J):
                    nc.scalar.activation(z2[:, j, :], h[:, j, :], ACT.Identity, bias=nb[:, j:j + 1],
                                         scale=r[:, j:j + 1]).then_inc(s["z2_made"], 1)

            def turned_rows(g):
                for j in range(J):
                    wait(act, s["z_turned"], g * J + j + 1)
                    for c in range(KC):
                        last = nc.scalar.activation(yT[:, c, j * P:(j + 1) * P], pt[j % 2][:, c * P:(c + 1) * P],
                                                    ACT.Identity, bias=cols[:, 1, c:c + 1], scale=cols[:, 0, c:c + 1])
                    last.then_inc(s["yT_kept"], 1)

            def gelus(g):
                for n in range(2 * HC):
                    hc, half = n // 2, n % 2
                    wait(act, s["h1_prod"], g * 2 * HC + n + 1)
                    nc.scalar.activation(gT[:, hc, half * HALF:(half + 1) * HALF], p1[half][:, 0:HALF], ACT.Gelu,
                                         bias=b1c[:, hc:hc + 1]).then_inc(s["g_made"], 1)

            attention_in(0)
            second_norm(0)
            turned_rows(0)
            with act.Fori(0, G - 1) as g:
                gelus(g)
                attention_in(g + 1)
                second_norm(g + 1)
                turned_rows(g + 1)
            gelus(G - 1)

        @block.tensor
        def _(pe):
            for c in range(KC):
                last = nc.tensor.transpose(pt[0][:, c * P:(c + 1) * P], kmax[:, c * P:(c + 1) * P], ident[:, :])
            last.then_inc(s["kmax_turned"], 1)
            pe.wait_ge(s["kdiag"], 1)
            nc.tensor.matmul(pt[1][:, 0:D], ones[:, :], chain[:, 0, 0, :], start=True, stop=True).then_inc(s["kmax_row"], 1)
            pe.wait_ge(s["bd_made"], 1)
            for c in range(KC):
                nc.tensor.matmul(pk[c][:, 0:D + 2], zeros[:, 0:P], zeros[:, 0:D + 2], start=True, stop=False, skip_group_check=True)
            def keys(g, u):
                wait(pe, s["kexp"], g + 1)
                wait(pe, s["zx_made"], g + 2)
                for j in range(J):
                    for c in range(KC):
                        last = nc.tensor.matmul(pk[c][:, 0:D + 2], kx[u][:, j, c * P:(c + 1) * P], zx[:, u, j, :],
                                                start=False, stop=False, skip_group_check=True)
                last.then_inc(s["ktz_prod"], 1)

            with pe.Fori(0, G // 2) as i:
                for u in range(2):
                    keys(i * 2 + u, u)
            keys(G - 1, 0)
            for c in range(KC):
                last = nc.tensor.matmul(pk[c][:, 0:D + 2], zeros[:, 0:P], zeros[:, 0:D + 2], start=False, stop=True,
                                        skip_group_check=True)
            last.then_inc(s["ktz_prod"], 1)
            pe.wait_ge(s["kl"], 1)
            for kk in range(KC):
                for c in range(KC):
                    last = nc.tensor.transpose(pt[0][:, kk * D + c * P:kk * D + (c + 1) * P],
                                               chain[:, 0, c, kk * P:(kk + 1) * P], ident[:, :])
            last.then_inc(s["kl_turned"], 1)
            pe.wait_ge(s["w_in"], 16 * 16)
            pe.wait_ge(s["klt"], 1)
            for c in range(KC):
                for kk in range(KC):
                    last = nc.tensor.matmul(pt[1][:, c * P:(c + 1) * P], wxt[:, kk, c * P:(c + 1) * P],
                                            chain[:, 1, kk, c * P:(c + 1) * P], start=(kk == 0), stop=(kk == KC - 1))
            last.then_inc(s["kxt"], 1)
            pe.wait_ge(s["kxt_kept"], 1)
            last = nc.tensor.matmul(pt[0][:, 0:D], bdv[:, :], chain[:, 2, 0, :], start=True, stop=True)
            last.then_inc(s["kvt"], 1)
            pe.wait_ge(s["kvt_kept"], 1)
            for c in range(KC):
                last = nc.tensor.matmul(pt[1][:, c * D:(c + 1) * D], chain[:, 0, 0, c * P:(c + 1) * P], wot[:, c, :],
                                        start=True, stop=True)
            last.then_inc(s["m_prod"], 1)
            pe.wait_ge(s["m_kept"], 1)
            pe.sem_inc(s["att"], 1)
            pe.sem_inc(s["att_kept"], 1)
            pe.sem_inc(s["g_made"], 2)
            pe.sem_inc(s["h2_kept"], 1)

            def attention(g):
                wait(pe, s["q_in"], g * 16 + 16)
                for j in range(J):
                    wait(pe, s["qT_kept"], g * J + max(j - 1, 0) + 1)
                    for c in range(KC):
                        last = nc.tensor.transpose(pt[j % 2][:, c * P:(c + 1) * P], qin[:, j, c * P:(c + 1) * P], ident[:, :])
                    last.then_inc(s["q_turned"], 1)
                    if j:
                        attend(pe, g, j - 1)
                attend(pe, g, J - 1)

            def turn(g):
                wait(pe, s["z2_made"], g * J + J)
                for j in range(J):
                    wait(pe, s["yT_kept"], g * J + max(j - 1, 0) + 1)
                    for c in range(KC):
                        last = nc.tensor.transpose(pt[j % 2][:, c * P:(c + 1) * P], z2[:, j, c * P:(c + 1) * P], ident[:, :])
                    last.then_inc(s["z_turned"], 1)

            def first(g):
                wait(pe, s["yT_kept"], g * J + J + 1)
                for n in range(2 * HC):
                    hc, half = n // 2, n % 2
                    wait(pe, s["g_made"], g * 2 * HC + n + 1)
                    for c in range(KC):
                        last = nc.tensor.matmul(p1[half][:, 0:HALF], w1[:, c, hc * P:(hc + 1) * P],
                                                yT[:, c, half * HALF:(half + 1) * HALF],
                                                start=(c == 0), stop=(c == KC - 1))
                    last.then_inc(s["h1_prod"], 1)

            def second(g):
                wait(pe, s["g_made"], g * 2 * HC + 2 * HC + 2)
                for j in range(J):
                    wait(pe, s["h2_kept"], g * J + max(j - 1, 0) + 1)
                    for hc in range(HC):
                        last = nc.tensor.matmul(p2[j % 2][:, 0:D], gT[:, hc, j * P:(j + 1) * P], w2[:, hc, :],
                                                start=(hc == 0), stop=(hc == HC - 1))
                    last.then_inc(s["h2_prod"], 1)

            attention(0)
            turn(0)
            with pe.Fori(0, G - 1) as g:
                first(g)
                attention(g + 1)
                second(g)
                turn(g + 1)
            first(G - 1)
            second(G - 1)

        @block.vector
        def _(dve):
            nc.vector.memset(bdv[:, :], 0.0)
            nc.vector.memset(headmask[:, :], 0.0)
            nc.vector.memset(zx[:, :, :, D:D + 2], 1.0)
            nc.vector.memset(zeros[:, 0:D + 2], 0.0)
            dve.drain()
            for i in range(P // MD):
                last = nc.vector.memset(headmask[i * MD:(i + 1) * MD, i * MD:(i + 1) * MD], 1.0)
            last.then_inc(s["bd_made"], 1)
            dve.sem_inc(s["qT_kept"], 1)
            dve.sem_inc(s["yT_kept"], 1)
            dve.wait_ge(s["kmax_turned"], 1)
            nc.vector.tensor_reduce(small[:, 0:KC], pt[0][:, 0:D].rearrange("p (k q) -> p k q", k=KC), AX, ALU.max)
            dve.drain()
            for c in range(KC):
                last = nc.vector.tensor_scalar(chain[:, 0, 0, c * P:(c + 1) * P], ident[:, :], small[:, c:c + 1], None, ALU.mult)
            last.then_inc(s["kdiag"], 1)
            dve.wait_ge(s["kmax_row"], 1)
            nc.vector.tensor_copy(chain[:, 1, 0, :], pt[1][:, 0:D])
            dve.drain()
            krow = chain[:, 1, 0, :].unsqueeze(1).broadcast_to([P, J, D])
            dve.sem_inc(s["ktz_prod"], 2)
            dve.sem_inc(s["zx_made"], 1)

            def keys(g, u):
                wait(dve, s["ktz_prod"], g + 1)
                wait(dve, s["zx_made"], g + 1)
                nc.vector.tensor_copy(scs[:, :, :], scl[:, ds(g * J, J), :]).then_inc(s["scs_made"], 1)
                wait(dve, s["k_in"], g * 16 + 16)
                nc.vector.tensor_tensor(kx[u][:, :, :], kin[:, :, :], krow, ALU.subtract).then_inc(s["ksub"], 1)
                wait(dve, s["ksub"], g + 1)
                dve.sem_inc(s["k_used"], 1)

            with dve.Fori(0, G // 2) as i:
                keys(i * 2, 0)
                place_edges(nc, dve, k, iota, i + G + 2)
                keys(i * 2 + 1, 1)
            keys(G - 1, 0)
            dve.wait_ge(s["ktz_prod"], G + 3)
            dve.wait_ge(s["w_in"], 16 * 16)
            for c in range(KC):
                nc.vector.reciprocal(small[:, 2 + c:3 + c], pk[c][:, D:D + 1])
            dve.drain()
            for c in range(KC):
                nc.vector.scalar_tensor_tensor(out=chain[:, 0, c, :], in0=pk[c][:, 0:D], scalar=small[:, 2 + c:3 + c],
                                               in1=rows[:, 0, :], op0=ALU.mult, op1=ALU.mult)
            dve.drain()
            nc.vector.tensor_tensor(chain[:, 0, :, :], chain[:, 0, :, :],
                                    rows[:, 1, :].unsqueeze(1).broadcast_to([P, KC, D]), ALU.add).then_inc(s["kl"], 1)
            dve.wait_ge(s["kl_turned"], 1)
            nc.vector.tensor_copy(chain[:, 1, :, :], pt[0][:, :].rearrange("p (k c) -> p k c", k=KC)).then_inc(s["klt"], 1)
            dve.wait_ge(s["kxt"], 1)
            for c in range(KC):
                last = nc.vector.scalar_tensor_tensor(out=chain[:, 2, 0, c * P:(c + 1) * P], in0=pt[1][:, c * P:(c + 1) * P],
                                                      scalar=cols[:, 2, c:c + 1], in1=headmask[:, :],
                                                      op0=ALU.add, op1=ALU.mult)
            last.then_inc(s["kxt_kept"], 1)
            dve.wait_ge(s["kvt"], 1)
            nc.vector.tensor_copy(chain[:, 0, 0, :], pt[0][:, 0:D]).then_inc(s["kvt_kept"], 1)
            dve.wait_ge(s["m_prod"], 1)
            nc.vector.tensor_copy(M[:, :, :], pt[1][:, :].rearrange("p (k c) -> p k c", k=KC)).then_inc(s["m_kept"], 1)

            def scales(g):
                nc.vector.tensor_copy(scs[:, :, :], scl[:, ds(g * J, J), :]).then_inc(s["scs_made"], 1)

            def attended(g):
                for j in range(J):
                    wait(dve, s["xn_made"], g * J + j + 1)
                    nc.vector.tensor_tensor(xnb[:, j, :], xnb[:, j, :], rows[:, 2, :], ALU.add)
                    dve.drain()
                    wait(dve, s["att"], g * J + j + 2)
                    nc.vector.tensor_tensor(h[:, j, :], pk[j % 2][:, 0:D], xnb[:, j, :], ALU.add).then_inc(s["att_kept"], 1)
                dve.drain()
                norm_begin(nc, dve, s["m_var_go"], lambda j: h[:, j, :], st, mv, var)

            def normed(g):
                norm_end(nc, dve, s["m_sd_done"], g + 1, mv, sd, r, nb).then_inc(s["m_stats"], 1)

            def take_h(g):
                xg = X[:, ds(g * J, J), :]
                nc.vector.tensor_tensor(xg, xg, h[:, :, :], ALU.add)
                dve.drain()
                nc.vector.tensor_tensor(xg, xg, rows[:, 3, :].unsqueeze(1).broadcast_to([P, J, D]), ALU.add)
                dve.drain()

            def take_second(g, tiles):
                for j in tiles:
                    xt = X[:, ds(g * J + j, 1), :].rearrange("p a c -> p (a c)")
                    wait(dve, s["h2_prod"], g * J + j + 1)
                    nc.vector.tensor_tensor(xt, xt, p2[j % 2][:, 0:D], ALU.add).then_inc(s["h2_kept"], 1)

            scales(0)
            attended(0)
            normed(0)
            take_h(0)
            def step(g, blocks):
                scales(g + 1)
                for b in blocks:
                    place_edges(nc, dve, k, iota, b)
                attended(g + 1)
                take_second(g, (0,))
                normed(g + 1)
                take_second(g, (1,))
                take_h(g + 1)
                take_second(g, range(2, J))

            with dve.Fori(0, TWICE) as g:
                step(g, (2 * g + PLACED, 2 * g + PLACED + 1))
            with dve.Fori(TWICE, G - 1) as g:
                step(g, (g + PLACED + TWICE,))
            take_second(G - 1, range(J))


def graph(nc, k, d, dram, sb, ps, sem):
    ctx = ExitStack()
    with ctx:
        X, a_src, ident, iota, awe = (k[n] for n in ("X", "a_src", "ident", "iota", "awe"))
        erec = k["erec"]
        acc = sb(ctx, "acc", [P, T, FW])
        hot = sb(ctx, "hot", [P, GS, B, P])
        hotT = sb(ctx, "hotT", [P, 2, B, P], BF16)
        rows = sb(ctx, "g_rows", [P, GS, B, FW])
        wrows = sb(ctx, "wrows", [P, 2, B, FW])
        ew = sb(ctx, "ew", [P, 2, B, GH])
        pre = sb(ctx, "pre", [P, 2, B, GH])
        sc = sb(ctx, "sc", [P, 2, B, GH])
        gi = sb(ctx, "gi", [P, GS, B], I32)
        pad_i = sb(ctx, "pad_i", [P, 1])
        warm = sb(ctx, "warm", [P, 2])
        inv = sb(ctx, "g_inv", [P, T, GH])
        pT = [ps(ctx, f"g_pT{i}", [P, 512]) for i in range(2)]
        pA = [ps(ctx, f"g_pA{i}", [P, 512]) for i in range(2)]
        pO = [ps(ctx, f"g_pO{i}", [P, 512]) for i in range(UG)]
        gathered = [sem(f"gathered{i}") for i in range(GS)]
        s = {n: sem(n) for n in ("idx_made hot_made hot_turned hotT_kept a_prod pre_made sc_made w_made "
                                 "scaled out_prod acc_done pad_made inv_made").split()}
        block = ctx.enter_context(nc.Block())

        def divide(ops, eng, groups):
            for g in groups:
                t0 = g * J
                a4 = acc[:, t0:t0 + J, 0:D].rearrange("p j (h o) -> p j h o", o=GO)
                ops.tensor_tensor(a4, a4, inv[:, t0:t0 + J, :].unsqueeze(3).broadcast_to([P, J, GH, GO]), ALU.mult)
            eng.drain()
            for g in groups:
                t0 = g * J
                ops.tensor_tensor(X[:, t0:t0 + J, :], X[:, t0:t0 + J, :], acc[:, t0:t0 + J, 0:D], ALU.add)

        @block.gpsimd
        def _(pool):
            nc.gpsimd.memset(pad_i[:, :], 0.0).then_inc(s["pad_made"], 1)
            pool.wait_ge(s["pad_made"], 1)
            nc.gpsimd.affine_select(out=pad_i[:, :], in_=pad_i[:, :], compare_op=ALU.is_gt, fill=1.0,
                                    base=LAST, pattern=[[0, 1]], channel_multiplier=-1).then_inc(s["pad_made"], 1)
            pool.sem_inc(s["scaled"], GS)

            def gather(q, u):
                wait(pool, s["scaled"], q + 1)
                nc.gpsimd.tensor_copy(gi[:, u, :], erec[:, ds(q * B, B), 0]).then_inc(s["idx_made"], 1)
                wait(pool, s["idx_made"], q + 1)
                for b in range(B):
                    nc.gpsimd.indirect_dma_start(rows[:, u, b, :], None, dram["feat"],
                                                 bass.IndirectOffsetOnAxis(gi[:, u, b:b + 1], 0))\
                        .then_inc(gathered[u], 16)

            with pool.Fori(0, NG // GS) as i:
                for u in range(GS):
                    gather(i * GS + u, u)
            for u in range(NG % GS):
                gather(NG // GS * GS + u, u)
            pool.wait_ge(s["inv_made"], 1)
            divide(nc.gpsimd, pool, range(G - GPOOL, G))

        @block.scalar
        def _(act):
            def keep_turned(q, u):
                wait(act, s["hot_turned"], q + 1)
                for n in range(2):
                    last = nc.scalar.copy(hotT[:, u, 4 * n:4 * n + 4, :].rearrange("p b e -> p (b e)"), pT[n][:, :])
                last.then_inc(s["hotT_kept"], 1)

            keep_turned(0, 0)
            def weights(q, u):
                wait(act, s["sc_made"], q + 1)
                nc.scalar.activation(wrows[:, u, :, D:FW], sc[:, u, :, :], ACT.Exp).then_inc(s["w_made"], 1)
                keep_turned(q + 1, 1 - u)

            with act.Fori(0, NG // GS) as i:
                nc.scalar.activation(warm[:, 1:2], warm[:, 0:1], ACT.Exp)
                for u in range(GS):
                    weights(i * GS + u, u % 2)
            for u in range(NG % GS):
                weights(NG // GS * GS + u, u % 2)

        @block.tensor
        def _(pe):
            def turn(q, slot):
                wait(pe, s["hot_made"], q + 1)
                wait(pe, s["hotT_kept"], q + 1)
                for b in range(B):
                    last = nc.tensor.transpose(pT[b // 4][:, b % 4 * P:(b % 4 + 1) * P], hot[:, slot, b, :], ident[:, :])
                last.then_inc(s["hot_turned"], 1)

            def source_scores(q, u, tiles):
                wait(pe, s["hotT_kept"], q + 2)
                wait(pe, s["pre_made"], q + 1)
                for b in range(B):
                    last = nc.tensor.matmul(pA[u][:, b * 3 * GH:(b + 1) * 3 * GH], hotT[:, u, b, :],
                                            a_src[:, ds(tiles[b // CU], 1), :, :].rearrange("p a n h -> p (a n h)"),
                                            start=True, stop=True)
                last.then_inc(s["a_prod"], 1)

            def load_tiles(c0, n):
                _, regs = nc.values_load_multi_w_load_instructions(
                    k["tiles"][0:1, ds(c0, n)], engines=[pe.engine], min_val=0, max_val=T - 1,
                    skip_runtime_bounds_check_because="the tile numbers are clipped where the table is made")
                return regs

            pe.sem_inc(s["hotT_kept"], 1)
            pe.sem_inc(s["pre_made"], 2)
            turn(0, 0)
            source_scores(0, 0, load_tiles(UG, UG))
            for n in range(UG):
                nc.tensor.matmul(pO[n][:, 0:FW], hot[:, GS - 1, n, :], wrows[:, 1, n, :], start=True, stop=True)\
                    .then_inc(s["out_prod"], 1)

            def step(q, slot, tiles):
                u = slot % 2
                turn(q + 1, (slot + 1) % GS)
                wait(pe, s["scaled"], q + GS + 1)
                for n in range(UG):
                    if n == 1:
                        source_scores(q + 1, 1 - u, tiles)
                    wait(pe, s["acc_done"], q * UG + n + 1)
                    for c in range(CU):
                        b = n * CU + c
                        last = nc.tensor.matmul(pO[n][:, 0:FW], hot[:, slot, b, :], wrows[:, u, b, :],
                                                start=(c == 0), stop=(c == CU - 1))
                    last.then_inc(s["out_prod"], 1)

            with pe.Fori(0, NG // GS) as i:
                tiles = load_tiles(i * GS * UG + 2 * UG, GS * UG)
                for u in range(GS):
                    step(i * GS + u, u, tiles[u * UG:(u + 1) * UG])
            q0 = NG // GS * GS
            for u in range(NG % GS):
                step(q0 + u, u, load_tiles((q0 + u + 2) * UG, UG))

        @block.vector
        def _(dve):
            def make_hot(q, slot):
                nc.vector.tensor_tensor(hot[:, slot, :, :], iota[:, :].unsqueeze(1).broadcast_to([P, B, P]),
                                        erec[:, ds(q * B, B), 1].unsqueeze(2).broadcast_to([P, B, P]),
                                        ALU.is_equal).then_inc(s["hot_made"], 1)

            def weight_part(q, u):
                nc.vector.tensor_tensor(ew[:, u, :, :], erec[:, ds(q * B, B), 2].unsqueeze(2).broadcast_to([P, B, GH]),
                                        awe[:, :].unsqueeze(1).broadcast_to([P, B, GH]), ALU.mult)

            def known_part(q, u):
                wait(dve, s["a_prod"], q + 1)
                nc.vector.tensor_reduce(pre[:, u, :, :],
                                        pA[u][:, 0:B * 3 * GH].rearrange("p (b n h) -> p b h n", n=3, h=GH), AX, ALU.add)
                dve.drain()
                nc.vector.tensor_tensor(pre[:, u, :, :], pre[:, u, :, :], ew[:, u, :, :], ALU.add)\
                    .then_inc(s["pre_made"], 1)

            def add_sums(q, tiles):
                for n in range(UG):
                    at = acc[:, ds(tiles[n], 1), :].rearrange("p a f -> p (a f)")
                    wait(dve, s["out_prod"], (q + 1) * UG + n + 1)
                    if n:
                        wait(dve, s["acc_done"], (q + 1) * UG + n)
                    nc.vector.tensor_tensor(at, at, pO[n][:, 0:FW], ALU.add).then_inc(s["acc_done"], 1)

            nc.vector.memset(hot[:, GS - 1, :, :], 0.0)
            nc.vector.memset(wrows[:, 1, :, :], 0.0)
            nc.vector.memset(acc[:, :, :], 0.0)
            nc.vector.memset(erec[:, CH:, :], 0.0)
            nc.vector.memset(warm[:, :], 0.0)
            dve.drain()
            dve.wait_ge(s["pad_made"], 2)
            nc.vector.tensor_copy(acc[:, T - 1, D:FW], pad_i[:, 0:1].broadcast_to([P, GH]))
            make_hot(0, 0)
            weight_part(0, 0)
            dve.drain()
            known_part(0, 0)

            def load_tiles(c0, n):
                _, regs = nc.values_load_multi_w_load_instructions(
                    k["tiles"][0:1, ds(c0, n)], engines=[dve.engine], min_val=0, max_val=T - 1,
                    skip_runtime_bounds_check_because="the tile numbers are clipped where the table is made")
                return regs

            def step(q, slot, turn, tiles):
                u = slot % 2
                dve.drain()
                wait(dve, gathered[slot], turn * (16 * B) + 16 * B)
                nc.vector.tensor_tensor(sc[:, u, :, :], pre[:, u, :, :], rows[:, slot, :, D:FW], ALU.add)
                dve.drain()
                nc.vector.tensor_scalar(sc[:, u, :, :], sc[:, u, :, :], 0.0, -1.0 / 20.0, ALU.max, ALU.mult)\
                    .then_inc(s["sc_made"], 1)
                make_hot(q + 1, (slot + 1) % GS)
                weight_part(q + 1, 1 - u)
                wait(dve, s["w_made"], q + 1)
                nc.vector.tensor_tensor(wrows[:, u, :, 0:D].rearrange("p b (h o) -> p b h o", o=GO),
                                        rows[:, slot, :, 0:D].rearrange("p b (h o) -> p b h o", o=GO),
                                        wrows[:, u, :, D:FW].unsqueeze(3).broadcast_to([P, B, GH, GO]),
                                        ALU.mult).then_inc(s["scaled"], 1)
                add_sums(q - 1, tiles)
                known_part(q + 1, 1 - u)

            with dve.Fori(0, NG // GS) as i:
                tiles = load_tiles(i * GS * UG, GS * UG)
                for u in range(GS):
                    step(i * GS + u, u, i, tiles[u * UG:(u + 1) * UG])
            q0 = NG // GS * GS
            for u in range(NG % GS):
                step(q0 + u, u, NG // GS, load_tiles((q0 + u) * UG, UG))
            dve.drain()
            add_sums(NG - 1, load_tiles(NG * UG, UG))
            dve.drain()
            nc.vector.reciprocal(inv[:, :, :], acc[:, :, D:FW]).then_inc(s["inv_made"], 1)
            dve.drain()
            divide(nc.vector, dve, range(G - GPOOL))


def experts(nc, k, d, dram, sb, ps, sem):
    ctx = ExitStack()
    with ctx:
        tile_row = sb(ctx, "tile_row", [1, TABLE], I32)
        tile_exp = sb(ctx, "tile_exp", [1, TABLE], I32)
        w = {"w1": sb(ctx, "e_w1", [P, NE, KC, EH]), "w2": sb(ctx, "e_w2", [P, NE, EHC, D]),
             "b1": sb(ctx, "e_b1", [P, NE, EH]), "b2": sb(ctx, "e_b2", [P, NE, D])}
        route(nc, k, d, dram, sb, ps, sem, w, tile_row, tile_exp)
        run_tiles(nc, k, dram, sb, ps, sem, w, tile_row, tile_exp)


def route(nc, k, d, dram, sb, ps, sem, w, tile_row, tile_exp):
    ctx = ExitStack()
    with ctx:
        X, ident, ones = k["X"], k["ident"], k["ones"]
        wg = sb(ctx, "wg", [P, KC, NE])
        bg = sb(ctx, "bg", [P, NE])
        st = sb(ctx, "e_st", [P, J, 6])
        mv = sb(ctx, "e_mv", [P, J, 2])
        var = sb(ctx, "e_var", [P, J])
        sd = sb(ctx, "e_sd", [P, J])
        r = sb(ctx, "e_r", [P, J])
        nb = sb(ctx, "e_nb", [P, J])
        z = sb(ctx, "e_z", [P, ZB, J, ZW])
        hot = sb(ctx, "hot_e", [P, TOP, J, NE])
        pos = sb(ctx, "pos_e", [P, TOP, J])
        node_i = sb(ctx, "node_i", [P, T], I32)
        node = sb(ctx, "node", [P, T])
        zT = sb(ctx, "e_zT", [P, J, D])
        gate = sb(ctx, "gate", [P, J, NE])
        rank_i = sb(ctx, "rank_i", [P, NE], I32)
        rank = sb(ctx, "rank", [P, NE])
        m1 = sb(ctx, "m1", [P, J])
        eq = sb(ctx, "eq", [P, J, NE])
        mask = sb(ctx, "mask", [P, J + 1, NE])
        before = sb(ctx, "e_before", [P, P])
        region_i = sb(ctx, "region_i", [P, NE], I32)
        region = sb(ctx, "region", [P, NE])
        base = sb(ctx, "base", [P, NE])
        base_i = sb(ctx, "base_i", [P, NE], I32)
        away_i = sb(ctx, "away_i", [P, TOP, T], I32)
        away = sb(ctx, "away", [P, TOP, T])
        valid = sb(ctx, "valid", [P, 1])
        place = sb(ctx, "place", [P, J, NE])
        chosen = sb(ctx, "chosen", [P, TOP, J, NE])
        picked = sb(ctx, "picked", [P, TOP, J])
        z_at = sb(ctx, "z_at", [P, ZB, TOP, J], I32)
        none = sb(ctx, "none", [P, ZW])
        past_i = sb(ctx, "past_i", [P, 1], I32)
        tiles_i = sb(ctx, "tiles_i", [P, NE], I32)
        tiles = sb(ctx, "tiles_e", [P, NE])
        tend = sb(ctx, "tend", [P, NE])
        step = sb(ctx, "step", [P, NE])
        onesE = sb(ctx, "onesE", [P, NE])
        tnum_i = sb(ctx, "tnum_i", [1, TABLE], I32)
        tnum = sb(ctx, "tnum", [1, TABLE])
        full = sb(ctx, "full", [1, TABLE, NE])
        texp = sb(ctx, "texp", [1, TABLE])
        trow = sb(ctx, "trow", [1, TABLE])
        pt = [ps(ctx, f"e_pt{i}", [P, 512]) for i in range(2)]
        pg = [ps(ctx, f"e_pg{i}", [P, 512]) for i in range(2)]
        pr = ps(ctx, "e_pr", [P, 512])
        s = {n: sem("e_" + n) for n in ("w_in gate_in consts var_go sd_done stats z_made z_turned zT_kept gate_prod "
                                        "mask_made rank_prod sent_free at_made none_made base_made filled").split()}
        sent = [sem(f"e_sent{i}") for i in range(ZB)]
        block = ctx.enter_context(nc.Block())

        @block.sync
        def _(sp):
            sp.dma_start(wg[:, :, :], d["Wg"].rearrange("(k p) n -> p k n", p=P)).then_inc(s["gate_in"], 16)
            sp.dma_start(bg[:, :], d["bg"].partition_broadcast(P)).then_inc(s["gate_in"], 16)
            sp.wait_ge(s["none_made"], 1)
            sp.dma_start(dram["z"][IDLE:IDLE + P, :], none[:, :]).then_inc(s["filled"], 16)
            sp.dma_start(dram["out"][N:N + P, :], none[:, 0:D]).then_inc(s["filled"], 16)
            for g in range(G):
                sp.wait_ge(s["at_made"], g + 1)
                for e in range(g * NE // G, (g + 1) * NE // G):
                    sp.dma_start(w["w1"][:, e, :, :], d["eW1"][e].rearrange("(k p) n -> p k n", p=P))\
                        .then_inc(s["w_in"], 16)
                    sp.dma_start(w["w2"][:, e, :, :], d["eW2"][e].rearrange("(k p) n -> p k n", p=P))\
                        .then_inc(s["w_in"], 16)
                    sp.dma_start(w["b1"][:, e, :], d["eb1"][e].partition_broadcast(P)).then_inc(s["w_in"], 16)
                    sp.dma_start(w["b2"][:, e, :], d["eb2"][e].partition_broadcast(P)).then_inc(s["w_in"], 16)
                tiles = J - (g == G - 1)
                sp.dma_start(dram["out"][g * GN:g * GN + tiles * P, :].rearrange("(t p) c -> p t c", p=P),
                             X[:, g * J:g * J + tiles, :]).then_inc(s["filled"], 16)
            sp.dma_start(dram["out"][(T - 1) * P:N, :], X[0:LAST, T - 1, :]).then_inc(s["filled"], 16)
            sp.wait_ge(s["base_made"], 1)
            _, ends = nc.values_load_multi_w_load_instructions(
                base_i[0:1, :], engines=[sp.engine], min_val=0, max_val=IDLE - P,
                skip_runtime_bounds_check_because="an expert's region is longer than the number of nodes")
            for e in range(NE):
                sp.dma_start(dram["z"][ds(ends[e], P), :], none[:, :]).then_inc(s["filled"], 16)
            sp.wait_ge(s["filled"], 16 * (NE + 3 + G))
            sp.wait_ge(s["w_in"], 16 * 4 * NE)

        @block.gpsimd
        def _(pool):
            nc.gpsimd.iota(rank_i[:, :], pattern=[[-1, NE]], base=NE, channel_multiplier=0).then_inc(s["consts"], 1)
            nc.gpsimd.iota(region_i[:, :], pattern=[[CAP, NE]], base=0, channel_multiplier=0).then_inc(s["consts"], 1)
            nc.gpsimd.iota(away_i[:, :, :], pattern=[[T * P, TOP], [P, T]], base=NOWHERE, channel_multiplier=1).then_inc(s["consts"], 1)
            nc.gpsimd.iota(tnum_i[:, :], pattern=[[1, TABLE]], base=0, channel_multiplier=0).then_inc(s["consts"], 1)
            nc.gpsimd.iota(node_i[:, :], pattern=[[P, T]], base=0, channel_multiplier=1).then_inc(s["consts"], 1)
            nc.gpsimd.iota(past_i[:, :], pattern=[[0, 1]], base=N, channel_multiplier=1).then_inc(s["consts"], 1)
            nc.gpsimd.memset(before[:, :], 1.0).then_inc(s["consts"], 1)
            nc.gpsimd.memset(valid[:, :], 1.0).then_inc(s["consts"], 1)
            pool.wait_ge(s["consts"], 8)
            nc.gpsimd.affine_select(out=before[:, :], in_=before[:, :], compare_op=ALU.is_gt, fill=0.0,
                                    base=0, pattern=[[1, P]], channel_multiplier=-1).then_inc(s["consts"], 1)
            nc.gpsimd.affine_select(out=valid[:, :], in_=valid[:, :], compare_op=ALU.is_gt, fill=0.0,
                                    base=LAST, pattern=[[0, 1]], channel_multiplier=-1).then_inc(s["consts"], 1)
            pool.sem_inc(s["sent_free"], ZB)

            def send(g, u):
                wait(pool, s["at_made"], g + 1)
                for j in range(J):
                    for n in range(TOP):
                        nc.gpsimd.indirect_dma_start(dram["z"], bass.IndirectOffsetOnAxis(z_at[:, u, n, j:j + 1], 0),
                                                     z[:, u, j, :], None).then_inc(sent[u], 16)

            def left(g):
                pool.wait_ge(sent[g % ZB], (g // ZB + 1) * 16 * TOP * J)
                pool.sem_inc(s["sent_free"], 1)

            for g in range(G):
                send(g, g % ZB)
                if g:
                    left(g - 1)
            left(G - 1)

        @block.scalar
        def _(act):
            def norm(g, u):
                wait(act, s["var_go"], g + 1)
                nc.scalar.activation(sd[:, :], var[:, :], ACT.Sqrt).then_inc(s["sd_done"], 1)
                wait(act, s["stats"], g + 1)
                wait(act, s["sent_free"], g + 1)
                for j in range(J):
                    nc.scalar.activation(z[:, u, j, 0:D], X[:, ds(g * J + j, 1), :].rearrange("p a c -> p (a c)"),
                                         ACT.Identity, bias=nb[:, j:j + 1], scale=r[:, j:j + 1])\
                        .then_inc(s["z_made"], 1)
                for j in range(J):
                    wait(act, s["z_turned"], g * J + j + 1)
                    nc.scalar.copy(zT[:, j, :], pt[j % 2][:, 0:D]).then_inc(s["zT_kept"], 1)

            for g in range(G):
                norm(g, g % ZB)

        @block.tensor
        def _(pe):
            def gates(g, u, bank):
                for j in range(J):
                    wait(pe, s["z_made"], g * J + j + 1)
                    wait(pe, s["zT_kept"], g * J + j + 1)
                    for c in range(KC):
                        last = nc.tensor.transpose(pt[j % 2][:, c * P:(c + 1) * P], z[:, u, j, c * P:(c + 1) * P],
                                                   ident[:, :])
                    last.then_inc(s["z_turned"], 1)
                wait(pe, s["zT_kept"], g * J + J + 2)
                for j in range(J):
                    for c in range(KC):
                        last = nc.tensor.matmul(pg[bank][:, j * NE:(j + 1) * NE], zT[:, j, c * P:(c + 1) * P], wg[:, c, :],
                                                start=(c == 0), stop=(c == KC - 1))
                last.then_inc(s["gate_prod"], 1)

            def ranks(g):
                wait(pe, s["mask_made"], g + 1)
                nc.tensor.matmul(pr[:, 0:(J + 1) * NE], before[:, :], mask[:, :, :].rearrange("p j e -> p (j e)"),
                                 start=True, stop=False)
                for j in range(J):
                    last = nc.tensor.matmul(pr[:, (j + 1) * NE:(J + 1) * NE], ones[:, :],
                                            mask[:, j:j + 1, :].broadcast_to([P, J - j, NE]),
                                            start=False, stop=(j == J - 1))
                last.then_inc(s["rank_prod"], 1)

            pe.wait_ge(s["consts"], 10)
            pe.wait_ge(s["gate_in"], 32)
            pe.sem_inc(s["zT_kept"], 2)
            gates(0, 0, 0)
            for g in range(G):
                ranks(g)
                if g == 0:
                    gates(1, 1, 1)
                if g + 2 < G:
                    gates(g + 2, (g + 2) % ZB, g % 2)

        @block.vector
        def _(dve):
            nc.vector.memset(none[:, 0:D], 0.0)
            nc.vector.memset(mask[:, J, :], 0.0)
            nc.vector.memset(onesE[:, :], 1.0)

            def stats(g, first):
                norm_begin(nc, dve, s["var_go"], lambda j: X[:, ds(g * J + j, 1), :].rearrange("p a c -> p (a c)"),
                           st, mv, var)
                if not first:
                    wait(dve, s["z_made"], g * J)
                norm_end(nc, dve, s["sd_done"], g + 1, mv, sd, r, nb).then_inc(s["stats"], 1)

            stats(0, True)
            stats(1, False)
            dve.wait_ge(s["consts"], 10)
            nc.vector.tensor_copy(none[:, D:ZW], past_i[:, :]).then_inc(s["none_made"], 1)
            nc.vector.tensor_copy(rank[:, :], rank_i[:, :])
            nc.vector.tensor_copy(region[:, :], region_i[:, :])
            nc.vector.tensor_copy(away[:, :, :], away_i[:, :, :])
            nc.vector.tensor_copy(node[:, :], node_i[:, :])
            nc.vector.tensor_copy(tnum[:, :], tnum_i[:, :])
            dve.drain()
            nc.vector.tensor_copy(base[:, :], region[:, :])
            dve.drain()
            dve.wait_ge(s["gate_in"], 32)
            rank3 = rank[:, :].unsqueeze(1).broadcast_to([P, J, NE])

            def pick_top(hot):
                nc.vector.tensor_reduce(m1[:, :], gate[:, :, :], AX, ALU.max)
                dve.drain()
                nc.vector.tensor_tensor(eq[:, :, :], gate[:, :, :], m1[:, :].unsqueeze(2).broadcast_to([P, J, NE]),
                                        ALU.is_equal)
                dve.drain()
                nc.vector.tensor_tensor(eq[:, :, :], eq[:, :, :], rank3, ALU.mult)
                dve.drain()
                nc.vector.tensor_reduce(m1[:, :], eq[:, :, :], AX, ALU.max)
                dve.drain()
                nc.vector.tensor_tensor(hot, m1[:, :].unsqueeze(2).broadcast_to([P, J, NE]), rank3, ALU.is_equal)
                dve.drain()

            def pick(g, u, bank, last):
                wait(dve, s["gate_prod"], g + 1)
                nc.vector.tensor_tensor(gate[:, :, :], pg[bank][:, 0:J * NE].rearrange("p (j e) -> p j e", e=NE),
                                        bg[:, :].unsqueeze(1).broadcast_to([P, J, NE]), ALU.add)
                dve.drain()
                pick_top(hot[:, 0, :, :])
                nc.vector.scalar_tensor_tensor(out=gate[:, :, :], in0=hot[:, 0, :, :], scalar=-3e38, in1=gate[:, :, :],
                                               op0=ALU.mult, op1=ALU.add)
                dve.drain()
                pick_top(hot[:, 1, :, :])
                if last:
                    nc.vector.tensor_scalar(hot[:, :, J - 1, :], hot[:, :, J - 1, :], valid[:, :], None, ALU.mult)
                    dve.drain()
                nc.vector.tensor_tensor(mask[:, 0:J, :], hot[:, 0, :, :], hot[:, 1, :, :], ALU.add)\
                    .then_inc(s["mask_made"], 1)
                nc.vector.tensor_reduce(picked[:, :, :], hot[:, :, :, :], AX, ALU.add)
                dve.drain()
                nc.vector.tensor_scalar(picked[:, :, :], picked[:, :, :], -1.0, 1.0, ALU.mult, ALU.add)
                dve.drain()
                nc.vector.tensor_tensor(picked[:, :, :], picked[:, :, :], away[:, :, ds(g * J, J)], ALU.mult)
                if g + 2 < G:
                    stats(g + 2, False)
                wait(dve, s["rank_prod"], g + 1)
                nc.vector.tensor_tensor(place[:, :, :], pr[:, 0:J * NE].rearrange("p (j e) -> p j e", e=NE),
                                        base[:, :].unsqueeze(1).broadcast_to([P, J, NE]), ALU.add)
                dve.drain()
                nc.vector.tensor_tensor(base[:, :], base[:, :], pr[:, J * NE:(J + 1) * NE], ALU.add)
                nc.vector.tensor_tensor(chosen[:, :, :, :], hot[:, :, :, :],
                                        place[:, :, :].unsqueeze(1).broadcast_to([P, TOP, J, NE]), ALU.mult)
                dve.drain()
                nc.vector.tensor_reduce(pos[:, :, :], chosen[:, :, :, :], AX, ALU.add)
                wait(dve, s["sent_free"], g + 1)
                nc.vector.tensor_copy(z[:, u, :, D], node[:, ds(g * J, J)])
                dve.drain()
                nc.vector.tensor_tensor(z_at[:, u, :, :], pos[:, :, :], picked[:, :, :], ALU.add)\
                    .then_inc(s["at_made"], 1)

            for g in range(G):
                pick(g, g % ZB, g % 2, g == G - 1)
            dve.drain()
            nc.vector.tensor_copy(base_i[:, :], base[:, :]).then_inc(s["base_made"], 1)
            nc.vector.tensor_tensor(tiles[:, :], base[:, :], region[:, :], ALU.subtract)
            dve.drain()
            nc.vector.tensor_scalar(tiles_i[:, :], tiles[:, :], float(P - 1), None, ALU.add)
            dve.drain()
            nc.vector.tensor_scalar(tiles_i[:, :], tiles_i[:, :], P.bit_length() - 1, None, ALU.logical_shift_right)
            dve.drain()
            nc.vector.tensor_copy(tiles[:, :], tiles_i[:, :])
            dve.drain()
            nc.vector.tensor_tensor_scan(tend[:, :], onesE[:, :], tiles[:, :], 0.0, ALU.mult, ALU.add)
            nc.vector.tensor_scalar(step[:, :], tiles[:, :], -float(P), float(CAP), ALU.mult, ALU.add)
            dve.drain()
            nc.vector.tensor_tensor(full[:, :, :], tend[0:1, :].unsqueeze(1).broadcast_to([1, TABLE, NE]),
                                    tnum[:, :].unsqueeze(2).broadcast_to([1, TABLE, NE]), ALU.is_le)
            dve.drain()
            nc.vector.tensor_reduce(texp[:, :], full[:, :, :], AX, ALU.add)
            dve.drain()
            nc.vector.tensor_scalar(tile_exp[:, :], texp[:, :], float(NE - 1), None, ALU.min)
            nc.vector.tensor_tensor(full[:, :, :], full[:, :, :], step[0:1, :].unsqueeze(1).broadcast_to([1, TABLE, NE]),
                                    ALU.mult)
            dve.drain()
            nc.vector.tensor_reduce(trow[:, :], full[:, :, :], AX, ALU.add)
            dve.drain()
            nc.vector.scalar_tensor_tensor(out=trow[:, :], in0=tnum[:, :], scalar=float(P), in1=trow[:, :],
                                           op0=ALU.mult, op1=ALU.add)
            dve.drain()
            nc.vector.tensor_scalar(tile_row[:, :], trow[:, :], float(IDLE), None, ALU.min)


def run_tiles(nc, k, dram, sb, ps, sem, w, tile_row, tile_exp):
    ctx = ExitStack()
    with ctx:
        ident = k["ident"]
        zt = sb(ctx, "t_z", [P, ZS, ZW])
        to = sb(ctx, "t_to", [P, ZS], I32)
        zT = sb(ctx, "t_zT", [P, 2, D])
        h = sb(ctx, "t_h", [P, 2, EH])
        gl = sb(ctx, "t_g", [P, 2, EH])
        gT = sb(ctx, "t_gT", [P, 2, EH])
        y = sb(ctx, "t_y", [P, ZS, D])
        pz = [ps(ctx, f"t_pz{i}", [P, 512]) for i in range(2)]
        pg = ps(ctx, "t_pg", [P, 512])
        p1 = [ps(ctx, f"t_p1{i}", [P, 512]) for i in range(2)]
        p2 = [ps(ctx, f"t_p2{i}", [P, 512]) for i in range(2)]
        s = {n: sem("t_" + n) for n in ("z_turned zT_kept h_prod h_made g_made g_turned gT_kept y_prod y_made "
                                        "y_out y_free to_made").split()}
        z_in = [sem(f"t_z_in{i}") for i in range(ZS)]
        block = ctx.enter_context(nc.Block())

        def load(eng, table, at, n, top):
            _, regs = nc.values_load_multi_w_load_instructions(
                table[0:1, ds(at, n)], engines=[eng.engine], min_val=0, max_val=top,
                skip_runtime_bounds_check_because="the entries are clipped where the table is made")
            return regs

        @block.sync
        def _(sp):
            rows = load(sp, tile_row, 0, ZS, IDLE)
            for t in range(ZS):
                sp.dma_start(zt[:, t, :], dram["z"][ds(rows[t], P), :]).then_inc(z_in[t], 16)
            with sp.Fori(0, TURNS) as i:
                rows = load(sp, tile_row, i * TU + ZS, TU, IDLE)
                for v in range(TU):
                    t = i * TU + v + 1
                    wait(sp, s["z_turned"], t)
                    wait(sp, s["to_made"], t)
                    sp.dma_start(zt[:, v % ZS, :], dram["z"][ds(rows[v], P), :]).then_inc(z_in[v % ZS], 16)
            for n in range(ZS):
                sp.wait_ge(z_in[n], 16 * (TURNS * TU // ZS + 1))

        @block.gpsimd
        def _(pool):
            pool.sem_inc(s["y_free"], ZS)

            def add_rows(turn, slot):
                t = turn * ZS + slot
                wait(pool, z_in[slot], turn * 16 + 16)
                nc.gpsimd.tensor_copy(to[:, slot:slot + 1], zt[:, slot, D:ZW]).then_inc(s["to_made"], 1)
                wait(pool, s["to_made"], t + 1)
                wait(pool, s["y_made"], t + 3)
                nc.gpsimd.indirect_dma_start(dram["out"], bass.IndirectOffsetOnAxis(to[:, slot:slot + 1], 0),
                                             y[:, slot, :], None, compute_op=ALU.add).then_inc(s["y_out"], 16)
                wait(pool, s["y_out"], t * 16 + 16)
                pool.sem_inc(s["y_free"], 1)

            with pool.Fori(0, CT // ZS) as i:
                for v in range(ZS):
                    add_rows(i, v)
            for v in range(CT % ZS):
                add_rows(CT // ZS, v)

        @block.scalar
        def _(act):
            def keep_rows(t, slot):
                wait(act, s["z_turned"], t + 1)
                nc.scalar.copy(zT[:, slot, :], pz[slot][:, 0:D]).then_inc(s["zT_kept"], 1)

            def keep_hidden(t, slot):
                wait(act, s["g_turned"], t + 1)
                nc.scalar.copy(gT[:, slot, :], pg[:, :]).then_inc(s["gT_kept"], 1)

            def gelu(t, slot):
                wait(act, s["h_made"], t + 1)
                nc.scalar.activation(gl[:, slot, :], h[:, slot, :], ACT.Gelu).then_inc(s["g_made"], 1)

            keep_rows(0, 0)
            keep_rows(1, 1)
            gelu(0, 0)
            with act.Fori(0, TURNS) as i:
                for v in range(TU):
                    t, u = i * TU + v + 1, (v + 1) % 2
                    keep_rows(t + 1, 1 - u)
                    keep_hidden(t - 1, 1 - u)
                    gelu(t, u)
            keep_hidden(CT - 1, (CT - 1) % 2)

        @block.tensor
        def _(pe):
            def turn_rows(t, slot, used, u):
                wait(pe, z_in[slot], used * 16 + 16)
                for c in range(KC):
                    last = nc.tensor.transpose(pz[u][:, c * P:(c + 1) * P], zt[:, slot, c * P:(c + 1) * P], ident[:, :])
                last.then_inc(s["z_turned"], 1)

            def turn_hidden(t, u):
                wait(pe, s["g_made"], t + 1)
                for c in range(EHC):
                    last = nc.tensor.transpose(pg[:, c * P:(c + 1) * P], gl[:, u, c * P:(c + 1) * P], ident[:, :])
                last.then_inc(s["g_turned"], 1)

            def first(t, e, u):
                wait(pe, s["zT_kept"], t + 1)
                for c in range(KC):
                    last = nc.tensor.matmul(p1[u][:, :], zT[:, u, c * P:(c + 1) * P],
                                            w["w1"][:, ds(e, 1), c, :].rearrange("p a n -> p (a n)"),
                                            start=(c == 0), stop=(c == KC - 1))
                last.then_inc(s["h_prod"], 1)

            def second(t, e, u):
                wait(pe, s["gT_kept"], t + 1)
                wait(pe, s["y_made"], t + 1)
                for c in range(EHC):
                    last = nc.tensor.matmul(p2[u][:, 0:D], gT[:, u, c * P:(c + 1) * P],
                                            w["w2"][:, ds(e, 1), c, :].rearrange("p a n -> p (a n)"),
                                            start=(c == 0), stop=(c == EHC - 1))
                last.then_inc(s["y_prod"], 1)

            pe.sem_inc(s["y_made"], 2)
            turn_rows(0, 0, 0, 0)
            turn_rows(1, 1, 0, 1)
            first(0, load(pe, tile_exp, 0, 1, NE - 1)[0], 0)
            with pe.Fori(0, TURNS) as i:
                exp = load(pe, tile_exp, i * TU, TU + 1, NE - 1)
                for v in range(TU):
                    t, u = i * TU + v + 1, (v + 1) % 2
                    turn_rows(t + 1, (v + 2) % ZS, i * (TU // ZS) + (v + 2) // ZS, 1 - u)
                    turn_hidden(t - 1, 1 - u)
                    first(t, exp[v + 1], u)
                    second(t - 1, exp[v], 1 - u)
            turn_hidden(CT - 1, (CT - 1) % 2)
            second(CT - 1, load(pe, tile_exp, CT - 1, 1, NE - 1)[0], (CT - 1) % 2)

        @block.vector
        def _(dve):
            def hidden(t, e, u):
                wait(dve, s["h_prod"], t + 1)
                nc.vector.tensor_tensor(h[:, u, :], p1[u][:, :], w["b1"][:, ds(e, 1), :].rearrange("p a n -> p (a n)"),
                                        ALU.add).then_inc(s["h_made"], 1)

            def result(t, e, u, slot):
                wait(dve, s["y_prod"], t + 1)
                wait(dve, s["y_free"], t + 1)
                nc.vector.tensor_tensor(y[:, slot, :], p2[u][:, 0:D], w["b2"][:, ds(e, 1), :].rearrange("p a n -> p (a n)"),
                                        ALU.add).then_inc(s["y_made"], 1)

            hidden(0, load(dve, tile_exp, 0, 1, NE - 1)[0], 0)
            with dve.Fori(0, TURNS) as i:
                exp = load(dve, tile_exp, i * TU, TU + 1, NE - 1)
                for v in range(TU):
                    t, u = i * TU + v + 1, (v + 1) % 2
                    hidden(t, exp[v + 1], u)
                    result(t - 1, exp[v], 1 - u, v % ZS)
            result(CT - 1, load(dve, tile_exp, CT - 1, 1, NE - 1)[0], (CT - 1) % 2, (CT - 1) % ZS)


def build(nc, d, out):
    dram = {
        "feat": nc.dram_tensor("feat", (T * P, FW), F32, kind="Internal").ap(),
        "qk": nc.dram_tensor("qk_rows", (T * P, 2 * D), F32, kind="Internal").ap(),
        "rec": nc.dram_tensor("edge_records", (P * CH, 4), F32, kind="Internal").ap(),
        "unit_tile": nc.dram_tensor("unit_tiles", (CH // CU,), I32, kind="Internal").ap(),
        "z": nc.dram_tensor("expert_rows", (NOWHERE + TOP * T * P, ZW), F32, kind="Internal").ap(),
        "out": out,
    }
    with ExitStack() as ctx:
        def sb(stack, name, shape, dt=F32):
            return stack.enter_context(nc.sbuf_tensor(name, shape, dt))

        def ps(stack, name, shape):
            return stack.enter_context(nc.psum_tensor(name, shape, F32))

        def sem(name):
            return ctx.enter_context(nc.semaphore(name))

        k = constants(nc, ctx, sb, sem)
        with ExitStack() as edges:
            k["erec"] = sb(edges, "erec", [P, CH + 2 * B, 4])
            with ExitStack() as keep:
                front(nc, k, d, dram, sb, ps, sem, keep)
                mixer(nc, k, d, dram, sb, ps, sem)
            graph(nc, k, d, dram, sb, ps, sem)
        experts(nc, k, d, dram, sb, ps, sem)


def kernel(x, src, dst, edge_weight, L0_gnn_Ws, L0_gnn_bs, L0_gnn_aw, L0_gnn_ab, L0_mix_ln1_w, L0_mix_ln1_b,
           L0_mix_Wx, L0_mix_bx, L0_mix_Wq, L0_mix_Wk, L0_mix_Wv, L0_mix_Wo, L0_mix_bo, L0_mix_ln2_w, L0_mix_ln2_b,
           L0_mix_W1, L0_mix_b1, L0_mix_W2, L0_mix_b2, L0_ffn_Wg, L0_ffn_bg, L0_ffn_W1, L0_ffn_b1, L0_ffn_W2,
           L0_ffn_b2):
    import numpy as np
    import concourse.bacc as bacc
    from concourse.bass_utils import run_bass_kernel_spmd as run

    def a(v):
        return np.ascontiguousarray(np.asarray(v))

    def flip(v):
        return np.ascontiguousarray(np.asarray(v).T)

    def column(v):
        v = np.asarray(v)
        return a(np.moveaxis(v.reshape(v.shape[:-1] + (-1, P)), -1, 0))

    gws, gaw = np.asarray(L0_gnn_Ws), np.asarray(L0_gnn_aw)
    arrays = {
        "x": a(x), "src": a(src), "dst": a(dst), "edge_weight": a(edge_weight),
        "Ws": a(gws.transpose(1, 0, 2).reshape(D, GH * GO)), "WsT": a(gws.transpose(0, 2, 1).reshape(GH * GO, D)),
        "bs": a(np.asarray(L0_gnn_bs).reshape(GH * GO)),
        "bs_c": column(np.asarray(L0_gnn_bs).reshape(GH * GO)), "bx_c": column(L0_mix_bx),
        "ln1_wc": column(L0_mix_ln1_w), "ln1_bc": column(L0_mix_ln1_b), "ln2_wc": column(L0_mix_ln2_w),
        "ln2_bc": column(L0_mix_ln2_b), "b1_c": column(L0_mix_b1), 
        "aw": a(gaw), "awe": a(gaw[:, 2 * GO]), "ab": a(L0_gnn_ab),
        "ln1_w": a(L0_mix_ln1_w), "ln1_b": a(L0_mix_ln1_b), "Wx": a(L0_mix_Wx), "WxT": flip(L0_mix_Wx),
        "WqT": flip(L0_mix_Wq), "WkT": flip(L0_mix_Wk), "WvT": flip(L0_mix_Wv),
        "WoT": flip(L0_mix_Wo), "bo": a(L0_mix_bo),
        "W1T": flip(L0_mix_W1), "W2T": flip(L0_mix_W2), "b2": a(L0_mix_b2),
        "Wg": a(L0_ffn_Wg), "bg": a(L0_ffn_bg), "eW1": a(L0_ffn_W1), "eW2": a(L0_ffn_W2),
        "eb1": a(L0_ffn_b1), "eb2": a(L0_ffn_b2),
    }
    nc = bacc.Bacc("TRN2", target_bir_lowering=False, num_devices=1)
    d = {n: nc.dram_tensor(f"in_{n}", v.shape, mybir.dt.from_np(v.dtype), kind="ExternalInput").ap()
         for n, v in arrays.items()}
    out = nc.dram_tensor("out_rows", (N + P, D), F32, kind="ExternalOutput").ap()
    build(nc, d, out)
    r = run(nc, [{f"in_{n}": v for n, v in arrays.items()}], core_ids=[0])
    return r.results[0]["out_rows"][0:N]
```
